# Optimizing a Trainium2 kernel written in Bass

```python
import numpy as np
import jax
import jax.numpy as jnp

def _softmax(x, axis=-1):
    return jax.nn.softmax(x, axis=axis)

def _gelu(x):
    return jax.nn.gelu(x, approximate=True)

def _silu(x):
    return jax.nn.silu(x)

def _sigmoid(x):
    return jax.nn.sigmoid(x)

def _layernorm(x, axis=-1, eps=1e-05):
    m = jnp.mean(x, axis=axis, keepdims=True)
    v = jnp.var(x, axis=axis, keepdims=True)
    return (x - m) / jnp.sqrt(v + eps)

def _scatter_add(tgt, idx, src, axis=0):
    return tgt.at[idx].add(src)

def _segment_sum(src, seg, n):
    return jax.ops.segment_sum(src, seg, n)
kernel_name = 'mk_perceiver_d1_seqx_r8_24951e'

def setup_inputs(seed: int=0):
    np.random.seed(seed)
    _w = jnp.asarray

    def _rec_inputs():
        import jax
        import jax.numpy as jnp
        _rk = jax.random.key(seed)
        x = -0.0003929 + 0.9999 * jax.random.normal(jax.random.fold_in(_rk, 1), (2, 128, 256), jnp.float32)
        _lenS = 128 - jax.random.randint(jax.random.fold_in(_rk, 7), (2,), 0, max(1, 128 // 4) + 1, jnp.int32)
        _lenS2 = 2048 - jax.random.randint(jax.random.fold_in(_rk, 8), (2,), 0, max(1, 2048 // 4) + 1, jnp.int32)
        _ctx_1024P = jax.random.normal(jax.random.fold_in(_rk, 11), (2, 16, 128), jnp.float32)
        _ctx_1024c = jax.random.dirichlet(jax.random.fold_in(_rk, 511), 0.3 * jnp.ones((16,), jnp.float32), (2, 2048))
        _ctx_1024t = jnp.einsum('bsk,bkd->bsd', _ctx_1024c, _ctx_1024P)
        _ctx_1024t = _ctx_1024t * jax.lax.rsqrt(jnp.mean(jnp.square(_ctx_1024t)) + 1e-12) * 0.953939
        ctx_1024 = -0.000494167 + 1.00018 * (_ctx_1024t + 0.3 * jax.random.normal(jax.random.fold_in(_rk, 611), (2, 2048, 128), jnp.float32))
        _validS = jnp.arange(128)[None, :] < _lenS[:, None]
        _validS2 = jnp.arange(2048)[None, :] < _lenS2[:, None]
        _causal = jnp.tril(jnp.ones((128, 128), dtype=bool))
        mask_BxS2_bf1 = jnp.ones((2, 2048), dtype=bool)
        return (x, ctx_1024, mask_BxS2_bf1)
    x, ctx_1024, mask_BxS2_bf1 = _rec_inputs()

    def _L0_xattn_setup():
        import jax, jax.numpy as jnp
        import numpy as np
        N_HEADS = 16
        N_KV_HEADS = 8
        HEAD_DIM = 128
        D_TEXT = 256
        D_VISION = 128
        GROUPS = N_HEADS // N_KV_HEADS
        key = jax.random.key(seed)
        ks = jax.random.split(key, 6)
        B, T_text, T_vis = (4, 256, 72)
        text_hidden = jax.random.normal(ks[0], (B, T_text, D_TEXT), dtype=jnp.float32)
        vision_tokens = jax.random.normal(ks[1], (B, T_vis, D_VISION), dtype=jnp.float32)
        vision_mask = jnp.ones((B, T_vis), dtype=bool)
        s = 0.02
        Wq = jax.random.normal(ks[2], (D_TEXT, N_HEADS * HEAD_DIM), dtype=jnp.float32) * s
        Wk = jax.random.normal(ks[3], (D_VISION, N_KV_HEADS * HEAD_DIM), dtype=jnp.float32) * s
        Wv = jax.random.normal(ks[4], (D_VISION, N_KV_HEADS * HEAD_DIM), dtype=jnp.float32) * s
        Wo = jax.random.normal(ks[5], (N_HEADS * HEAD_DIM, D_TEXT), dtype=jnp.float32) * s
        return {'text_hidden': text_hidden, 'vision_tokens': vision_tokens, 'vision_mask': vision_mask, 'Wq': Wq, 'Wk': Wk, 'Wv': Wv, 'Wo': Wo}
    _L0_xattn_all = _L0_xattn_setup()
    _L0_xattn_in = {k: v for k, v in _L0_xattn_all.items() if k in ('Wq', 'Wk', 'Wv', 'Wo')}
    del _L0_xattn_all

    def _L0_attn_setup():
        import jax, jax.numpy as jnp
        import numpy as np
        NUM_HEADS = 16
        ROPE_BASE = 10000.0
        QK_GAIN_INIT = 12.0
        EPS = 1e-06
        ROPE_MASK = jnp.asarray(np.tile([1.0, 0.0], NUM_HEADS // 2), dtype=jnp.float32)

        def _rope_cos_sin(seqlen, head_dim, dtype):
            half = head_dim // 2
            inv_freq = ROPE_BASE ** (-jnp.arange(0, half, dtype=jnp.float32) / half)
            theta = jnp.arange(seqlen, dtype=jnp.float32)[:, None] * inv_freq[None, :]
            return (jnp.cos(theta).astype(dtype), jnp.sin(theta).astype(dtype))

        def _apply_rope(t, cos, sin):
            d2 = t.shape[-1] // 2
            t1, t2 = (t[..., :d2], t[..., d2:])
            c = cos[None, :, None, :]
            s = sin[None, :, None, :]
            return jnp.concatenate([t1 * c - t2 * s, t1 * s + t2 * c], axis=-1)

        def _unit_norm(t):
            return t * jax.lax.rsqrt(jnp.sum(t * t, axis=-1, keepdims=True) + EPS)
        key = jax.random.key(seed)
        k0, k1, k2 = jax.random.split(key, 3)
        B, S, Dm = (2, 256, 256)
        x = jax.random.normal(k0, (B, S, Dm), dtype=jnp.float32)
        w_qkv = jax.random.normal(k1, (Dm, 3 * Dm), dtype=jnp.float32) * Dm ** (-0.5)
        w_out = jax.random.normal(k2, (Dm, Dm), dtype=jnp.float32) * Dm ** (-0.5)
        q_gain = jnp.full((NUM_HEADS,), QK_GAIN_INIT, dtype=jnp.float32)
        return {'x': x, 'w_qkv': w_qkv, 'w_out': w_out, 'q_gain': q_gain}
    _L0_attn_all = _L0_attn_setup()
    _L0_attn_in = {k: v for k, v in _L0_attn_all.items() if k in ('w_qkv', 'w_out', 'q_gain')}
    del _L0_attn_all

    def _L0_ffn_setup():
        import jax, jax.numpy as jnp
        import numpy as np
        ALPHA = 1.702
        LIMIT = 7.0
        TOP_K = 2
        E, H, I = (8, 256, 256)
        B, S = (2, 256)
        key = jax.random.key(seed)
        ks = jax.random.split(key, 7)
        return {'hidden_states': jax.random.normal(ks[0], (B, S, H), dtype=jnp.float32), 'router_weight': jax.random.normal(ks[1], (E, H), dtype=jnp.float32) * 0.02, 'router_bias': jax.random.normal(ks[2], (E,), dtype=jnp.float32) * 0.02, 'gate_up_proj': jax.random.normal(ks[3], (E, H, 2 * I), dtype=jnp.float32) * 0.02, 'gate_up_proj_bias': jax.random.normal(ks[4], (E, 2 * I), dtype=jnp.float32) * 0.02, 'down_proj': jax.random.normal(ks[5], (E, I, H), dtype=jnp.float32) * 0.02, 'down_proj_bias': jax.random.normal(ks[6], (E, H), dtype=jnp.float32) * 0.02}
    _L0_ffn_all = _L0_ffn_setup()
    _L0_ffn_in = {k: v for k, v in _L0_ffn_all.items() if k in ('router_weight', 'router_bias', 'gate_up_proj', 'gate_up_proj_bias', 'down_proj', 'down_proj_bias')}
    del _L0_ffn_all
    return {'x': x, 'ctx_1024': ctx_1024, 'mask_BxS2_bf1': mask_BxS2_bf1, 'L0_xattn_Wq': _L0_xattn_in['Wq'], 'L0_xattn_Wk': _L0_xattn_in['Wk'], 'L0_xattn_Wv': _L0_xattn_in['Wv'], 'L0_xattn_Wo': _L0_xattn_in['Wo'], 'L0_attn_w_qkv': _L0_attn_in['w_qkv'], 'L0_attn_w_out': _L0_attn_in['w_out'], 'L0_attn_q_gain': _L0_attn_in['q_gain'], 'L0_ffn_router_weight': _L0_ffn_in['router_weight'], 'L0_ffn_router_bias': _L0_ffn_in['router_bias'], 'L0_ffn_gate_up_proj': _L0_ffn_in['gate_up_proj'], 'L0_ffn_gate_up_proj_bias': _L0_ffn_in['gate_up_proj_bias'], 'L0_ffn_down_proj': _L0_ffn_in['down_proj'], 'L0_ffn_down_proj_bias': _L0_ffn_in['down_proj_bias']}

def reference(x, ctx_1024, mask_BxS2_bf1, L0_xattn_Wq, L0_xattn_Wk, L0_xattn_Wv, L0_xattn_Wo, L0_attn_w_qkv, L0_attn_w_out, L0_attn_q_gain, L0_ffn_router_weight, L0_ffn_router_bias, L0_ffn_gate_up_proj, L0_ffn_gate_up_proj_bias, L0_ffn_down_proj, L0_ffn_down_proj_bias):
    import jax
    import jax.numpy as jnp

    def _L0_xattn_ref(text_hidden, vision_tokens, vision_mask, Wq, Wk, Wv, Wo):
        import jax, jax.numpy as jnp
        import numpy as np
        N_HEADS = 16
        N_KV_HEADS = 8
        HEAD_DIM = 128
        D_TEXT = 256
        D_VISION = 128
        GROUPS = N_HEADS // N_KV_HEADS
        B, T_text, _ = text_hidden.shape
        T_vis = vision_tokens.shape[1]
        scale = jnp.float32(np.sqrt(HEAD_DIM))
        q = (text_hidden @ Wq).reshape(B, T_text, N_HEADS, HEAD_DIM).transpose(0, 2, 1, 3)
        k = (vision_tokens @ Wk).reshape(B, T_vis, N_KV_HEADS, HEAD_DIM).transpose(0, 2, 1, 3)
        v = (vision_tokens @ Wv).reshape(B, T_vis, N_KV_HEADS, HEAD_DIM).transpose(0, 2, 1, 3)
        k = jnp.repeat(k, GROUPS, axis=1)
        v = jnp.repeat(v, GROUPS, axis=1)
        scores = jnp.einsum('bhtd,bhsd->bhts', q, k) / scale
        mask = vision_mask[:, None, None, :]
        scores = jnp.where(mask, scores, -jnp.inf)
        attn = jax.nn.softmax(scores, axis=-1)
        attn = jnp.nan_to_num(attn, nan=0.0)
        out = jnp.einsum('bhts,bhsd->bhtd', attn, v)
        out = out.transpose(0, 2, 1, 3).reshape(B, T_text, N_HEADS * HEAD_DIM)
        return out @ Wo

    def _L0_attn_ref(x, w_qkv, w_out, q_gain):
        import jax, jax.numpy as jnp
        import numpy as np
        NUM_HEADS = 16
        ROPE_BASE = 10000.0
        QK_GAIN_INIT = 12.0
        EPS = 1e-06
        ROPE_MASK = jnp.asarray(np.tile([1.0, 0.0], NUM_HEADS // 2), dtype=jnp.float32)

        def _rope_cos_sin(seqlen, head_dim, dtype):
            half = head_dim // 2
            inv_freq = ROPE_BASE ** (-jnp.arange(0, half, dtype=jnp.float32) / half)
            theta = jnp.arange(seqlen, dtype=jnp.float32)[:, None] * inv_freq[None, :]
            return (jnp.cos(theta).astype(dtype), jnp.sin(theta).astype(dtype))

        def _apply_rope(t, cos, sin):
            d2 = t.shape[-1] // 2
            t1, t2 = (t[..., :d2], t[..., d2:])
            c = cos[None, :, None, :]
            s = sin[None, :, None, :]
            return jnp.concatenate([t1 * c - t2 * s, t1 * s + t2 * c], axis=-1)

        def _unit_norm(t):
            return t * jax.lax.rsqrt(jnp.sum(t * t, axis=-1, keepdims=True) + EPS)
        B, S, Dm = x.shape
        H = NUM_HEADS
        D = Dm // H
        qkv = (x @ w_qkv).reshape(B, S, 3, H, D)
        q, k, v = (qkv[:, :, 0], qkv[:, :, 1], qkv[:, :, 2])
        q = _unit_norm(q)
        k = _unit_norm(k)
        cos, sin = _rope_cos_sin(S, D, x.dtype)
        m = ROPE_MASK[None, None, :, None]
        q = m * _apply_rope(q, cos, sin) + (1.0 - m) * q
        k = m * _apply_rope(k, cos, sin) + (1.0 - m) * k
        logits = jnp.einsum('bshd,bthd->bhst', q, k) * q_gain[None, :, None, None]
        causal = jnp.tril(jnp.ones((S, S), dtype=bool))
        logits = jnp.where(causal[None, None], logits, jnp.finfo(logits.dtype).min)
        attn = jax.nn.softmax(logits, axis=-1)
        y = jnp.einsum('bhst,bthd->bshd', attn, v).reshape(B, S, Dm)
        return y @ w_out

    def _L0_ffn_ref(hidden_states, router_weight, router_bias, gate_up_proj, gate_up_proj_bias, down_proj, down_proj_bias):
        import jax, jax.numpy as jnp
        import numpy as np
        ALPHA = 1.702
        LIMIT = 7.0
        TOP_K = 2
        E, H, I = (8, 256, 256)
        B, S = (2, 256)
        bsz, seq_len, hidden = hidden_states.shape
        h = hidden_states.reshape(-1, hidden)
        T = h.shape[0]
        logits = h @ router_weight.T + router_bias
        top_vals, top_idx = jax.lax.top_k(logits, TOP_K)
        top_w = jax.nn.softmax(top_vals, axis=-1)
        scores = jnp.zeros_like(logits).at[jnp.arange(T)[:, None], top_idx].set(top_w)
        gate_up = jnp.einsum('th,ehj->etj', h, gate_up_proj) + gate_up_proj_bias[:, None, :]
        gate = gate_up[..., ::2]
        up = gate_up[..., 1::2]
        gate = jnp.minimum(gate, LIMIT)
        up = jnp.clip(up, -LIMIT, LIMIT)
        glu = gate * jax.nn.sigmoid(gate * ALPHA)
        act = (up + 1.0) * glu
        expert_out = jnp.einsum('eti,eih->eth', act, down_proj) + down_proj_bias[:, None, :]
        out = jnp.einsum('te,eth->th', scores, expert_out)
        return out.reshape(bsz, seq_len, hidden)
    x = x + _L0_xattn_ref(_layernorm(x, axis=-1), ctx_1024, mask_BxS2_bf1, L0_xattn_Wq, L0_xattn_Wk, L0_xattn_Wv, L0_xattn_Wo)
    x = x + _L0_attn_ref(_layernorm(x, axis=-1), L0_attn_w_qkv, L0_attn_w_out, L0_attn_q_gain)
    x = x + _L0_ffn_ref(_layernorm(x, axis=-1), L0_ffn_router_weight, L0_ffn_router_bias, L0_ffn_gate_up_proj, L0_ffn_gate_up_proj_bias, L0_ffn_down_proj, L0_ffn_down_proj_bias)
    return x

_drawn_inputs = setup_inputs


def setup_inputs(seed=0):
    import zlib

    import numpy as np

    out = dict(_drawn_inputs(seed))
    spreads = {'L0_attn_q_gain': (12.0, 0.2)}
    factors = {'L0_xattn_Wq': 8.0,
     'L0_xattn_Wk': 8.0,
     'L0_ffn_router_bias': 8.0,
     'L0_ffn_gate_up_proj_bias': 23.441,
     'L0_ffn_down_proj_bias': 4.508}
    for name, (base, spread) in spreads.items():
        noise = np.random.default_rng([zlib.crc32(name.encode()), seed]).standard_normal(out[name].shape)
        drawn = base * np.exp(spread * noise) if base else spread * noise
        out[name] = jnp.asarray(drawn.astype(out[name].dtype))
    for name, factor in factors.items():
        out[name] = (out[name] * factor).astype(out[name].dtype)
    return out
```

```python
import concourse.bass as bass
from concourse import mybir
from contextlib import ExitStack
import math



def perceiver_block(nc, x, ctx, mask, Wq, Wk, Wv, Wo, w_qkv, w_out, q_gain, router_w, router_b,
                    gate_up, gate_up_bias, down, down_bias, rope, out):
    f32, f32r, bf16, u8 = mybir.dt.float32, mybir.dt.float32r, mybir.dt.bfloat16, mybir.dt.uint8
    ALU, ACT, AX = mybir.AluOpType, mybir.ActivationFunctionType, mybir.AxisListType
    P = 128

    B, T, D = x.shape
    KEYS, DV = ctx.shape[1], ctx.shape[2]
    DC = D // P
    H = Wq.shape[1] // P
    G = Wk.shape[1] // P
    KB = KEYS // P
    PAIRS = B * G
    SH = 16
    SD = D // SH
    E, TWO_I = gate_up.shape[0], gate_up.shape[2]
    IC = TWO_I // 2 // P
    SCALE = 1.0 / math.sqrt(P)
    MASKED = 3.0e38
    CAUSAL = -3.0e38
    LN_EPS, UNIT_EPS = 1e-5, 1e-6
    ALPHA, LIMIT = 1.702, 7.0

    es = ExitStack()
    with es:
        at = {"next": (nc.sbuf_base + 63) // 64 * 64}

        def size(dt):
            return {f32: 4, f32r: 4, bf16: 2, u8: 1}[dt]

        def sb(name, shape, dt, over=None):
            n = size(dt)
            for s in shape[1:]:
                n *= s
            n = (n + 31) // 32 * 32
            if over is None:
                offset = at["next"]
                at["next"] += n
            else:
                offset = over["next"]
                over["next"] += n
                assert over["next"] <= over["end"], name
            return nc.alloc_sbuf_tensor_at(name, shape, dt, offset=offset)

        def region(nbytes):
            start = at["next"]
            at["next"] += nbytes
            return lambda skip=0: {"next": start + skip, "end": start + nbytes}

        def sem(name):
            return es.enter_context(nc.semaphore(name))

        ident = sb("ident", [P, P], f32)
        xt = sb("xt", [P, B, D], f32)
        wprime = sb("wprime", [P, H, D], f32)
        mask_bias = sb("mask_bias", [P, B, KEYS], bf16)
        attend = sb("attend", [P, B], f32)
        att_acc = sb("att_acc", [P, B, 2, D], f32)
        w_qkv_s = sb("w_qkv_s", [P, DC, 3 * D], f32)
        w_out_s = sb("w_out_s", [P, DC, D], f32)
        gain_b = sb("gain_b", [P, SH], f32)
        rope_s = sb("rope_s", [P, 2, SD], f32)
        router_wT = sb("router_wT", [P, DC, E], f32)
        router_bb = sb("router_bb", [P, E], f32)
        gu_biasT = sb("gu_biasT", [P, IC, 2, E], f32)
        down_b = sb("down_b", [E, D], f32)
        causal = sb("causal", [P, P], f32)
        lower = sb("lower", [P, E, E], f32)
        minus_half = sb("minus_half", [P, 2 * SH], f32)
        ln_st = sb("ln_st", [P, 3, B, 6], f32)
        ln_mv = sb("ln_mv", [P, 3, B, 2], f32)
        ln_ve = sb("ln_ve", [P, 3, B], f32)
        ln_rs = sb("ln_rs", [P, 3, B], f32)
        row_max = sb("row_max", [P, 2, 4], f32)
        neg_max = sb("neg_max", [P, 2, 2], f32)
        row_sum = sb("row_sum", [P, 2, 4], f32)
        head_sum = sb("head_sum", [P, 2, 2], f32)
        head_inv = sb("head_inv", [P, 2, 2], f32)
        q_pair = sb("q_pair", [P, 2 * P], f32)
        u_s = sb("u_s", [P, 2 * P], f32)
        r_ctx = region(4 * B * KEYS * 4)
        r_p = region(2 * 2 * KEYS * 4)
        r_sm = region(2 * KEYS * 4)
        r_pt = region(2 * 4 * 4 * P * 4)
        r_qp = region(PAIRS * 2 * P * 4)
        r_qs = region(2 * 2 * 2 * P * 4)
        r_late = region(4 * DC * TWO_I * 4)

        o = r_ctx()
        ctx_hi = sb("ctx_hi", [P, B * KB, P], f32r, o)
        ctx_lo = sb("ctx_lo", [P, B * KB, P], f32r, o)
        ctxT_hi = sb("ctxT_hi", [P, B, KEYS], f32r, o)
        ctxT_lo = sb("ctxT_lo", [P, B, KEYS], f32r, o)
        o = r_p()
        probs = sb("probs", [P, 2, 2, KEYS], f32, o)
        o = r_sm()
        scores = sb("scores", [P, 2, KEYS], f32, o)
        o = r_pt()
        pT_hi = sb("pT_hi", [P, 4, 4 * P], f32r, o)
        pT_lo = sb("pT_lo", [P, 4, 4 * P], f32r, o)
        o = r_qp()
        qp = sb("qp", [P, PAIRS * 2 * P], f32, o)
        o = r_qs()
        qs_hi = sb("qs_hi", [P, 2, 2 * P], f32r, o)
        qs_lo = sb("qs_lo", [P, 2, 2 * P], f32r, o)

        o = r_p()
        wq_s = sb("wq_s", [P, DC, H * P], f32, o)
        wo_s = sb("wo_s", [P, H, D], f32, o)
        o = r_sm()
        wk_s = sb("wk_s", [P, G * P], f32, o)
        wv_s = sb("wv_s", [P, G * P], f32, o)
        wkT = sb("wkT", [P, G, P], f32, o)
        wvT = sb("wvT", [P, G, P], f32, o)
        o = r_pt()
        ctx_s = sb("ctx_s", [P, B * KB, P], f32, o)
        o = r_late()
        qT = sb("qT", [P, 2, 2 * B * T], f32, o)
        mask_u8 = sb("mask_u8", [P, B, KEYS], u8, o)
        h0 = sb("h0", [P, B, D], f32, o)
        hT0 = sb("hT0", [P, DC, B * T], f32, o)
        gu_bias = sb("gu_bias", [E, TWO_I], f32, o)
        router_s = sb("router_s", [E, D], f32, o)

        o = r_late()
        gu_a = sb("gu_a", [P, E // 2, DC, TWO_I], f32, o)
        o = r_p()
        gu_b = sb("gu_b", [P, E // 2, DC, TWO_I], f32, o)
        down_s = sb("down_s", [P, E, IC, D], f32, o)
        o = r_ctx()
        x1s = sb("x1s", [P, B, D], f32, o)
        x1 = sb("x1", [P, B, D], f32, o)
        h1 = sb("h1", [P, B, D], f32, o)
        hT1 = sb("hT1", [P, B, DC * P], f32, o)
        sq = sb("sq", [P, B, 2 * D], f32, o)
        v1 = sb("v1", [P, B, D], f32, o)
        ss = sb("ss", [P, B, 2 * SH], f32, o)
        sse = sb("sse", [P, B, 2 * SH], f32, o)
        rs = sb("rs", [P, B, 2 * SH], f32, o)
        rg = sb("rg", [P, B, 2 * SH], f32, o)
        even = sb("even", [P, B, 2, SH // 2, SD], f32, o)
        rot_a = sb("rot_a", [P, B, 2, SH // 2, SD], f32, o)
        rot_b = sb("rot_b", [P, B, 2, SH // 2, SD], f32, o)
        qkz = sb("qkz", [P, B, 3, D], f32, o)
        qkT = sb("qkT", [P, B, 6, P], f32, o)
        sm1 = sb("sm1", [P, SH, P], f32, o)
        o2 = r_sm()
        sm1b = sb("sm1b", [P, SH, P], f32, o2)
        mx1 = sb("mx1", [P, B, SH], f32, o)
        nb1 = sb("nb1", [P, B, SH], f32, o)
        l1 = sb("l1", [P, B, SH], f32, o)
        li1 = sb("li1", [P, B, SH], f32, o)
        y1 = sb("y1", [P, B, D], f32, o)
        yT = sb("yT", [P, B, DC * P], f32, o)
        o2 = r_pt()
        p1 = sb("p1", [P, B, SH, P], f32, o2)
        o2 = r_qp()
        p1T = sb("p1T", [P, B, SH, P], f32, o2)
        x2 = sb("x2", [P, B, D], f32, o)
        h2 = sb("h2", [P, B, D], f32, o)
        hT2 = sb("hT2", [P, DC, B * T], f32, o)
        lg = sb("lg", [P, B, E], f32, o)
        top = sb("top", [P, B, 8], f32, o)
        gap = sb("gap", [P, B, 4], f32, o)
        cmp_a = sb("cmp_a", [P, B, E, E], f32, o)
        cmp_b = sb("cmp_b", [P, B, E, E], f32, o)
        rank = sb("rank", [P, B, E], f32, o)
        pick = sb("pick", [P, B, E], f32, o)
        gates = sb("gates", [P, B, E], f32, o)
        gatesT = sb("gatesT", [E, B, P], f32, o)
        o2 = r_pt()
        g_s = sb("g_s", [P, 2, IC * B * T], f32, o2)
        u_c = sb("u_c", [P, 2, IC * B * T], f32, o2)
        u_1 = sb("u_1", [P, 2, IC * B * T], f32, o2)
        sg = sb("sg", [P, 2, IC * B * T], f32, o2)
        o2 = r_qp()
        gl = sb("gl", [P, 2, IC * B * T], f32, o2)
        act_s = sb("act_s", [P, 2, IC * B * T], f32, o2)
        res = sb("res", [P, B, D], f32, o)
        assert at["next"] <= nc.sbuf_usable_end, at

        ps = es.enter_context(nc.psum_tensor("ps", [P, 8 * 512], f32))

        def bank(k, n=512):
            return ps[:, 512 * k:512 * k + n]

        x_in, wk_in, ctx_in, mask_in = sem("x_in"), sem("wk_in"), [sem(f"ctx_in{b}") for b in range(B)], sem("mask_in")
        wq_in = [sem(f"wq_in{i}") for i in range(4)]
        wv_in, wo_in, small_in = sem("wv_in"), sem("wo_in"), sem("small_in")
        attn_w_in, gu_a_in, gu_b_in, down_in, out_stored = sem("attn_w_in"), sem("gu_a_in"), sem("gu_b_in"), sem("down_in"), sem("out_stored")
        ident_ready, consts_ready, pool_set = sem("ident_ready"), sem("consts_ready"), sem("pool_set")
        ln_stat, ln_aggr, ln_var, ln_rstd, ln_out = sem("ln_stat"), sem("ln_aggr"), sem("ln_var"), sem("ln_rstd"), sem("ln_out")
        prep_pe, prep_act, prep_dve = sem("prep_pe"), sem("prep_act"), sem("prep_dve")
        ctx_split = sem("ctx_split")
        mask_ready, acc_clear = sem("mask_ready"), sem("acc_clear")
        q_hi_ready, q_split_ready = sem("q_hi_ready"), sem("q_split_ready")
        scores_ready, scores_drained, nb_ready, exps = sem("scores_ready"), sem("scores_drained"), sem("nb_ready"), sem("exps")
        pT_ready, hi_ready, lo_ready = sem("pT_ready"), sem("hi_ready"), sem("lo_ready")
        u_ready, u_copied, proj_ready, proj_added = sem("u_ready"), sem("u_copied"), sem("proj_ready"), sem("proj_added")
        sums_ready, inv_ready = sem("sums_ready"), sem("inv_ready")

        prep = [("wkT", 0), ("wkT", 1), ("hT", 0), ("ctx", 0), ("ctx", 1), ("ctx", 2), ("ctx", 3),
                ("q", 0), ("q", 1), ("qp", 0), ("q", 2), ("qp", 1), ("q", 3), ("qp", 2), ("q", 4), ("qp", 3),
                ("q", 5), ("qp", 4), ("q", 6), ("qp", 5), ("q", 7), ("qp", 6), ("ctx", 4), ("qp", 7),
                ("ctx", 5), ("ctx", 6), ("ctx", 7), ("wvT", 0), ("wvT", 1), ("small", 0)] + [("wp", g) for g in range(G)]
        on_act = {"q", "wvT"}

        def engines_of(task):
            kind, n = task
            if kind == "ctx":
                return ("act", "dve")
            if kind == "wp":
                return ("act",) if n % 2 else ("dve",)
            return ("act",) if kind in on_act else ("dve",)

        def evacuated(task):
            e = engines_of(task)[-1]
            upto = prep[:prep.index(task) + 1]
            return (prep_act if e == "act" else prep_dve), sum(e in engines_of(t) for t in upto)

        n_act = sum("act" in engines_of(t) for t in prep)
        n_dve = sum("dve" in engines_of(t) for t in prep)

        def pair_loop(eng, body):
            for b in range(B):
                body(G * b, G * b)
                body(G * b + 1, G * b + 1)
                with eng.Fori(G * b // 2 + 1, G * (b + 1) // 2) as two:
                    body(two * 2, G * b + 2)
                    body(two * 2 + 1, G * b + 3)
            body(PAIRS, PAIRS)
            body(PAIRS + 1, PAIRS + 1)

        def wait_above(eng, s, value, at_value):
            if at_value > 0:
                eng.wait_ge(s, value)

        def live(p):
            return 0 <= p < PAIRS

        def layer_norm(dve, n, src, dst):
            for b in range(B):
                k = n * B + b + 1
                dve.bn_stats(ln_st[:, n, b, :], src[:, b, :]).then_inc(ln_stat, 1)
                dve.wait_ge(ln_stat, k)
                dve.bn_aggr(ln_mv[:, n, b, :], ln_st[:, n, b, :]).then_inc(ln_aggr, 1)
                dve.wait_ge(ln_aggr, k)
                dve.tensor_scalar(ln_ve[:, n, b:b + 1], ln_mv[:, n, b, 1:2], LN_EPS, None, ALU.add).then_inc(ln_var, 1)
            for b in range(B):
                k = n * B + b + 1
                dve.wait_ge(ln_rstd, k)
                dve.tensor_scalar(dst[:, b, :], src[:, b, :], ln_mv[:, n, b, 0:1], ln_rs[:, n, b:b + 1],
                                  ALU.subtract, ALU.mult).then_inc(ln_out, 1)

        s_ = {name: sem(name) for name in (
            "qkz_clear", "norm_sums", "norm_inv", "up_min", "up_ready", "att_sum", "x1_ready", "squares",
            "norm_a", "norm_gain", "normed", "rotated", "qk_final", "self_scores", "self_max", "self_nb",
            "self_pT", "pT_dve", "self_exp", "self_inv", "self_y", "y_ready", "self_proj", "x2_ready",
            "router_ready", "lg", "top", "cmp", "cmp2", "gap", "gap_exp", "gap2", "gsum", "gates_ready",
            "gatesT", "gatesT_copied", "bias_ready", "res_added", "down_ready", "gate_ready", "gate_min",
            "up_pe", "sig_ready", "glu", "act_ready", "hT1_pe", "hT1_ready", "qk_pe", "v_pe", "v_ready",
            "qkT_pe", "qkT_ready", "pT_act", "yT_pe", "yT_ready", "hT2_pe", "hT2_ready",)}.__getitem__

        def post_pool(pool):
            pool.wait_ge(u_ready, PAIRS)
            pool.memset(qkz[:, :, :, :], 0.0).then_inc(s_("qkz_clear"), 1)
            for b in range(B):
                pool.wait_ge(ln_var, B + b + 1)
                pool.tensor_tensor(ln_rs[:, 1, b:b + 1], ln_ve[:, 1, b:b + 1], minus_half[:, 0:1], ALU.pow).then_inc(ln_rstd, 1)
            for b in range(B):
                pool.wait_ge(s_("norm_sums"), b + 1)
                pool.tensor_tensor(rs[:, b, :], sse[:, b, :], minus_half[:, :], ALU.pow).then_inc(s_("norm_inv"), 1)
            for b in range(B):
                pool.wait_ge(ln_var, 2 * B + b + 1)
                pool.tensor_tensor(ln_rs[:, 2, b:b + 1], ln_ve[:, 2, b:b + 1], minus_half[:, 0:1], ALU.pow).then_inc(ln_rstd, 1)
            for e in range(E):
                pool.wait_ge(s_("up_min"), e + 1)
                pool.tensor_scalar(u_1[:, e % 2, :], u_c[:, e % 2, :], -LIMIT, 1.0, ALU.max, ALU.add).then_inc(s_("up_ready"), 1)

        sm_b = [sm1, sm1b]

        def post_dve(dve):
            for b in range(B):
                if b == 0:
                    dve.wait_ge(proj_added, PAIRS)
                    dve.wait_ge(u_ready, PAIRS)
                dve.tensor_tensor(x1s[:, b, :], att_acc[:, b, 0, :], att_acc[:, b, 1, :], ALU.add).then_inc(s_("att_sum"), 1)
                dve.wait_ge(s_("att_sum"), b + 1)
                dve.scalar_tensor_tensor(out=x1[:, b, :], in0=x1s[:, b, :], scalar=attend[:, b:b + 1], in1=xt[:, b, :],
                                         op0=ALU.mult, op1=ALU.add).then_inc(s_("x1_ready"), 1)
            dve.wait_ge(s_("x1_ready"), B)
            layer_norm(dve, 1, x1, h1)
            dve.wait_ge(small_in, 16 * 6)
            for b in range(B):
                qk = bank(4 * b + 1)
                dve.wait_ge(s_("squares"), b + 1)
                dve.tensor_reduce(ss[:, b, :], sq[:, b, :].rearrange("p (h d) -> p h d", d=SD), AX.X, ALU.add).then_inc(s_("norm_a"), 1)
                dve.wait_ge(s_("norm_a"), b + 1)
                dve.tensor_scalar(sse[:, b, :], ss[:, b, :], UNIT_EPS, None, ALU.add).then_inc(s_("norm_sums"), 1)
            for b in range(B):
                qk = bank(4 * b + 1)
                dve.wait_ge(s_("norm_inv"), b + 1)
                dve.tensor_tensor(rg[:, b, 0:SH], rs[:, b, 0:SH], gain_b[:, :], ALU.mult)
                dve.tensor_copy(rg[:, b, SH:2 * SH], rs[:, b, SH:2 * SH]).then_inc(s_("norm_gain"), 1)
                dve.wait_ge(s_("norm_gain"), b + 1)
                if b == 0:
                    dve.wait_ge(s_("qkz_clear"), 1)
                qk_v = qk.rearrange("p (w n two d) -> p w n two d", w=2, two=2, d=SD)
                rg_v = rg[:, b, :].rearrange("p (w n two) -> p w n two", w=2, two=2)
                for w in range(2):
                    dve.tensor_tensor(even[:, b, w], qk_v[:, w, :, 0, :], rg_v[:, w, :, 0:1].broadcast_to([P, SH // 2, SD]), ALU.mult)
                    dst = qkz[:, b, 1 + w, :].rearrange("p (n two d) -> p n two d", two=2, d=SD)
                    last = dve.tensor_tensor(dst[:, :, 1, :], qk_v[:, w, :, 1, :], rg_v[:, w, :, 1:2].broadcast_to([P, SH // 2, SD]), ALU.mult)
                last.then_inc(s_("normed"), 1)
                dve.wait_ge(s_("normed"), b + 1)
                ev = even[:, b].rearrange("p w n d -> p (w n) d")
                ra = rot_a[:, b].rearrange("p w n d -> p (w n) d")
                rb = rot_b[:, b].rearrange("p w n d -> p (w n) d")
                HD = SD // 2
                cos = rope_s[:, 0:1, :].broadcast_to([P, SH, SD])
                dve.tensor_tensor(ra, ev, cos, ALU.mult)
                dve.tensor_tensor(rb[:, :, 0:HD], ev[:, :, HD:SD], rope_s[:, 1:2, 0:HD].broadcast_to([P, SH, HD]), ALU.mult)
                dve.tensor_tensor(rb[:, :, HD:SD], ev[:, :, 0:HD], rope_s[:, 1:2, HD:SD].broadcast_to([P, SH, HD]), ALU.mult)\
                    .then_inc(s_("rotated"), 1)
                dve.wait_ge(s_("rotated"), b + 1)
                for w in range(2):
                    dst = qkz[:, b, 2 * w, :].rearrange("p (n two d) -> p n two d", two=2, d=SD)
                    last = dve.tensor_tensor(dst[:, :, 0, :], rot_a[:, b, w], rot_b[:, b, w], ALU.add)
                last.then_inc(s_("qk_final"), 1)
            dve.wait_ge(consts_ready, 2)
            for b in range(B):
                for g in range(4):
                    dve.wait_ge(s_("self_scores"), 4 * b + g + 1)
                    for r in range(4):
                        n = 4 * g + r
                        last = dve.tensor_tensor_reduce(sm_b[b][:, n, :], bank(4 * b + g)[:, r * P:(r + 1) * P], causal[:, :],
                                                        1.0, CAUSAL, ALU.add, ALU.max, mx1[:, b, n:n + 1])
                    last.then_inc(s_("self_max"), 1)
                    dve.wait_ge(s_("self_max"), 4 * b + g + 1)
                    dve.tensor_scalar(nb1[:, b, 4 * g:4 * g + 4], mx1[:, b, 4 * g:4 * g + 4], -1.0, None, ALU.mult).then_inc(s_("self_nb"), 1)
            for b in range(B):
                for g in range(4):
                    if g % 2 == 1:
                        dve.wait_ge(s_("self_pT"), 4 * b + g + 1)
                        dve.tensor_copy(p1T[:, b, 4 * g:4 * g + 4, :].rearrange("p h t -> p (h t)"), bank(4 * b + g)).then_inc(s_("pT_dve"), 1)
                dve.wait_ge(s_("self_exp"), 4 * b + 4)
                dve.reciprocal(li1[:, b, :], l1[:, b, :]).then_inc(s_("self_inv"), 1)
                dve.wait_ge(s_("self_inv"), b + 1)
                dve.wait_ge(s_("self_y"), b + 1)
                y_v = bank(4 * b, D).rearrange("p (c g r d) -> p c g r d", c=2, g=4, r=2)
                l_v = li1[:, b, :].rearrange("p (g c r) -> p c g r", c=2, r=2)
                o_v = y1[:, b, :].rearrange("p (c g r d) -> p c g r d", c=2, g=4, r=2)
                for c in range(2):
                    for r in range(2):
                        last = dve.tensor_tensor(o_v[:, c, :, r, :], y_v[:, c, :, r, :],
                                                 l_v[:, c, :, r:r + 1].broadcast_to([P, 4, SD]), ALU.mult)
                last.then_inc(s_("y_ready"), 1)
            for b in range(B):
                dve.wait_ge(s_("self_proj"), b + 1)
                dve.tensor_tensor(x2[:, b, :], x1[:, b, :], bank(4 * b + 2, D), ALU.add).then_inc(s_("x2_ready"), 1)
            dve.wait_ge(s_("x2_ready"), B)
            layer_norm(dve, 2, x2, h2)
            for b in range(B):
                dve.wait_ge(s_("router_ready"), 1)
                dve.tensor_tensor(lg[:, b, :], bank(7)[:, b * E:(b + 1) * E], router_bb[:, :], ALU.add).then_inc(s_("lg"), 1)
                dve.wait_ge(s_("lg"), b + 1)
                dve.max(top[:, b, :], lg[:, b, :]).then_inc(s_("top"), 1)
                l_e = lg[:, b, :].unsqueeze(2).broadcast_to([P, E, E])
                l_j = lg[:, b, :].unsqueeze(1).broadcast_to([P, E, E])
                dve.tensor_tensor(cmp_a[:, b], l_j, l_e, ALU.is_gt)
                dve.tensor_tensor(cmp_b[:, b], l_j, l_e, ALU.is_equal).then_inc(s_("cmp"), 1)
                dve.wait_ge(s_("cmp"), b + 1)
                dve.tensor_tensor(cmp_b[:, b], cmp_b[:, b], lower[:, :, :], ALU.mult).then_inc(s_("cmp2"), 1)
                dve.wait_ge(s_("cmp2"), 2 * b + 1)
                dve.tensor_tensor(cmp_a[:, b], cmp_a[:, b], cmp_b[:, b], ALU.add).then_inc(s_("cmp2"), 1)
                dve.wait_ge(s_("cmp2"), 2 * b + 2)
                dve.tensor_reduce(rank[:, b, :], cmp_a[:, b], AX.X, ALU.add)
                dve.wait_ge(s_("top"), b + 1)
                dve.tensor_tensor(gap[:, b, 0:1], top[:, b, 1:2], top[:, b, 0:1], ALU.subtract).then_inc(s_("gap"), 1)
                dve.wait_ge(s_("gap_exp"), b + 1)
                dve.tensor_scalar(gap[:, b, 2:3], gap[:, b, 1:2], 1.0, None, ALU.add).then_inc(s_("gap2"), 1)
                dve.wait_ge(s_("gap2"), 3 * b + 1)
                dve.reciprocal(gap[:, b, 3:4], gap[:, b, 2:3]).then_inc(s_("gap2"), 1)
                dve.wait_ge(s_("gap2"), 3 * b + 2)
                dve.tensor_scalar(pick[:, b, :], rank[:, b, :], 1.0, gap[:, b, 1:2], ALU.is_equal, ALU.mult).then_inc(s_("gap2"), 1)
                dve.wait_ge(s_("gap2"), 3 * b + 3)
                dve.scalar_tensor_tensor(out=cmp_a[:, b, 0, :], in0=rank[:, b, :], scalar=0.0, in1=pick[:, b, :],
                                         op0=ALU.is_equal, op1=ALU.add).then_inc(s_("gsum"), 1)
                dve.wait_ge(s_("gsum"), b + 1)
                dve.tensor_scalar(gates[:, b, :], cmp_a[:, b, 0, :], gap[:, b, 3:4], None, ALU.mult).then_inc(s_("gates_ready"), 1)
            dve.wait_ge(s_("gatesT"), 1)
            dve.tensor_copy(gatesT[:, :, :].rearrange("e b t -> e (b t)"), ps[0:E, 512 * 7:512 * 7 + B * P]).then_inc(s_("gatesT_copied"), 1)
            dve.wait_ge(s_("bias_ready"), 1)
            dve.tensor_tensor(res[:, :, :].rearrange("p b d -> p (b d)"), bank(6), x2[:, :, :].rearrange("p b d -> p (b d)"), ALU.add)\
                .then_inc(s_("res_added"), 1)

            def expert_sum(e):
                dve.wait_ge(s_("down_ready"), e + 1)
                dve.wait_ge(s_("res_added"), e + 1)
                for b in range(B):
                    last = dve.scalar_tensor_tensor(out=res[:, b, :], in0=bank(4 + e % 2)[:, b * D:(b + 1) * D],
                                                    scalar=gates[:, b, e:e + 1], in1=res[:, b, :], op0=ALU.mult, op1=ALU.add)
                last.then_inc(s_("res_added"), 1)

            for e in range(E):
                k = e % 2
                dve.wait_ge(s_("gate_ready"), e + 1)
                for ic in range(IC):
                    part = slice(ic * B * T, (ic + 1) * B * T)
                    last = dve.tensor_scalar(g_s[:, k, part], bank(2 * k)[:, part], gu_biasT[:, ic, 0, e:e + 1], LIMIT, ALU.add, ALU.min)
                last.then_inc(s_("gate_min"), 1)
                dve.wait_ge(s_("up_pe"), e + 1)
                for ic in range(IC):
                    part = slice(ic * B * T, (ic + 1) * B * T)
                    last = dve.tensor_scalar(u_c[:, k, part], bank(2 * k + 1)[:, part], gu_biasT[:, ic, 1, e:e + 1], LIMIT, ALU.add, ALU.min)
                last.then_inc(s_("up_min"), 1)
                dve.wait_ge(s_("sig_ready"), e + 1)
                dve.tensor_tensor(gl[:, k, :], g_s[:, k, :], sg[:, k, :], ALU.mult).then_inc(s_("glu"), 1)
                dve.wait_ge(s_("glu"), e + 1)
                dve.wait_ge(s_("up_ready"), e + 1)
                if e >= 2:
                    dve.wait_ge(s_("down_ready"), e - 1)
                dve.tensor_tensor(act_s[:, k, :], gl[:, k, :], u_1[:, k, :], ALU.mult).then_inc(s_("act_ready"), 1)
                if e >= 1:
                    expert_sum(e - 1)
            expert_sum(E - 1)

        def post_act(act):
            for b in range(B):
                act.wait_ge(s_("hT1_pe"), b + 1)
                act.activation(hT1[:, b, :], bank(4 * b, DC * P), ACT.Copy).then_inc(s_("hT1_ready"), 1)
            for b in range(B):
                act.wait_ge(s_("qk_pe"), b + 1)
                act.activation(sq[:, b, :], bank(4 * b + 1), ACT.Square).then_inc(s_("squares"), 1)
                act.wait_ge(s_("v_pe"), b + 1)
                act.activation(v1[:, b, :], bank(4 * b + 2, D), ACT.Copy).then_inc(s_("v_ready"), 1)
            for b in range(B):
                act.wait_ge(s_("qkT_pe"), b + 1)
                act.activation(qkT[:, b, 0:4, :].rearrange("p n t -> p (n t)"), bank(4 * b + 3), ACT.Copy)
                act.activation(qkT[:, b, 4:6, :].rearrange("p n t -> p (n t)"), bank(4 * b, 2 * P), ACT.Copy).then_inc(s_("qkT_ready"), 1)
            for b in range(B):
                for g in range(4):
                    act.wait_ge(s_("self_nb"), 4 * b + g + 1)
                    for r in range(4):
                        n = 4 * g + r
                        last = act.activation(p1[:, b, n, :], sm_b[b][:, n, :], ACT.Exp, bias=nb1[:, b, n:n + 1],
                                              accum_out=l1[:, b, n:n + 1])
                    last.then_inc(s_("self_exp"), 1)
                for g in range(0, 4, 2):
                    act.wait_ge(s_("self_pT"), 4 * b + g + 1)
                    act.activation(p1T[:, b, 4 * g:4 * g + 4, :].rearrange("p h t -> p (h t)"), bank(4 * b + g), ACT.Copy).then_inc(s_("pT_act"), 1)
            for b in range(B):
                act.wait_ge(s_("yT_pe"), b + 1)
                act.activation(yT[:, b, :], bank(4 * b + 1, DC * P), ACT.Copy).then_inc(s_("yT_ready"), 1)
            act.wait_ge(s_("hT2_pe"), 1)
            act.activation(hT2[:, :, :].rearrange("p c t -> p (c t)"), bank(3), ACT.Copy).then_inc(s_("hT2_ready"), 1)
            for b in range(B):
                act.wait_ge(s_("gap"), b + 1)
                act.activation(gap[:, b, 1:2], gap[:, b, 0:1], ACT.Exp).then_inc(s_("gap_exp"), 1)
            for e in range(E):
                k = e % 2
                act.wait_ge(s_("gate_min"), e + 1)
                act.activation(sg[:, k, :], g_s[:, k, :], ACT.Sigmoid, scale=ALPHA).then_inc(s_("sig_ready"), 1)
            act.wait_ge(s_("res_added"), E + 1)
            act.dma_start(out.rearrange("b t d -> t b d"), res[:, :, :]).then_inc(out_stored, 16)
            act.wait_ge(out_stored, 16)

        def post_pe(pe):
            for b in range(B):
                pe.wait_ge(ln_out, B + b + 1)
                if b == 0:
                    pe.wait_ge(proj_added, PAIRS)
                for c in range(DC):
                    mm = pe.transpose(bank(4 * b)[:, c * P:(c + 1) * P], h1[:, b, c * P:(c + 1) * P], ident[:, :])
                mm.then_inc(s_("hT1_pe"), 1)
            pe.wait_ge(attn_w_in, 32)
            for b in range(B):
                pe.wait_ge(s_("hT1_ready"), b + 1)
                for c in range(DC):
                    mm = pe.matmul(bank(4 * b + 1), hT1[:, b, c * P:(c + 1) * P], w_qkv_s[:, c, 0:2 * D], start=(c == 0), stop=(c == DC - 1))
                mm.then_inc(s_("qk_pe"), 1)
                for c in range(DC):
                    mm = pe.matmul(bank(4 * b + 2, D), hT1[:, b, c * P:(c + 1) * P], w_qkv_s[:, c, 2 * D:3 * D], start=(c == 0), stop=(c == DC - 1))
                mm.then_inc(s_("v_pe"), 1)
            for b in range(B):
                pe.wait_ge(s_("qk_final"), b + 1)
                for s in range(3):
                    for c in range(DC):
                        n = s * DC + c
                        dst = bank(4 * b + 3)[:, n * P:(n + 1) * P] if n < 4 else bank(4 * b)[:, (n - 4) * P:(n - 3) * P]
                        mm = pe.transpose(dst, qkz[:, b, s, c * P:(c + 1) * P], ident[:, :])
                mm.then_inc(s_("qkT_pe"), 1)
            for b in range(B):
                pe.wait_ge(s_("qkT_ready"), b + 1)
                pe.wait_ge(s_("v_ready"), b + 1)
                for g in range(4):
                    rows = slice(32 * g, 32 * g + 32)
                    for r in range(4):
                        c, odd = r // 2, r % 2
                        mm = pe.matmul(bank(4 * b + g)[:, r * P:(r + 1) * P], qkT[rows, b, odd * DC + c, :], qkT[rows, b, 2 * DC + c, :],
                                       start=True, stop=True)
                    mm.then_inc(s_("self_scores"), 1)
            for b in range(B):
                for g in range(4):
                    pe.wait_ge(s_("self_exp"), 4 * b + g + 1)
                    for r in range(4):
                        mm = pe.transpose(bank(4 * b + g)[:, r * P:(r + 1) * P], p1[:, b, 4 * g + r, :], ident[:, :])
                    mm.then_inc(s_("self_pT"), 1)
                for g in range(4):
                    pe.wait_ge(s_("pT_dve") if g % 2 else s_("pT_act"), 2 * b + g // 2 + 1)
                    for r in range(4):
                        h = (r // 2) * 8 + 2 * g + r % 2
                        mm = pe.matmul(bank(4 * b)[:, h * SD:(h + 1) * SD], p1T[:, b, 4 * g + r, :], v1[:, b, h * SD:(h + 1) * SD],
                                       start=True, stop=True)
                mm.then_inc(s_("self_y"), 1)
            for b in range(B):
                pe.wait_ge(s_("y_ready"), b + 1)
                for c in range(DC):
                    mm = pe.transpose(bank(4 * b + 1)[:, c * P:(c + 1) * P], y1[:, b, c * P:(c + 1) * P], ident[:, :])
                mm.then_inc(s_("yT_pe"), 1)
            for b in range(B):
                pe.wait_ge(s_("yT_ready"), b + 1)
                for c in range(DC):
                    mm = pe.matmul(bank(4 * b + 2, D), yT[:, b, c * P:(c + 1) * P], w_out_s[:, c, :], start=(c == 0), stop=(c == DC - 1))
                mm.then_inc(s_("self_proj"), 1)
            for b in range(B):
                pe.wait_ge(ln_out, 2 * B + b + 1)
                for c in range(DC):
                    mm = pe.transpose(bank(3)[:, (c * B + b) * P:(c * B + b + 1) * P], h2[:, b, c * P:(c + 1) * P], ident[:, :])
            mm.then_inc(s_("hT2_pe"), 1)
            pe.wait_ge(s_("hT2_ready"), 1)
            for b in range(B):
                for c in range(DC):
                    mm = pe.matmul(bank(7)[:, b * E:(b + 1) * E], hT2[:, c, b * T:(b + 1) * T], router_wT[:, c, :], start=(c == 0), stop=(c == DC - 1))
            mm.then_inc(s_("router_ready"), 1)

            def gates_and_ups(e):
                k = e % 2
                w = gu_a if e < E // 2 else gu_b
                if e == 0:
                    pe.wait_ge(gu_a_in, 16 * (E // 2))
                if e == E // 2:
                    pe.wait_ge(gu_b_in, 16 * (E // 2))
                for j in range(2):
                    if e >= 2:
                        pe.wait_ge(s_("up_min") if j else s_("gate_min"), e - 1)
                    for ic in range(IC):
                        for c in range(DC):
                            lhs = w[:, e % (E // 2), c, ic * 2 * P:(ic + 1) * 2 * P].rearrange("p (i two) -> p two i", two=2)[:, j, :]
                            mm = pe.matmul(bank(2 * k + j)[:, ic * B * T:(ic + 1) * B * T], lhs, hT2[:, c, :], start=(c == 0), stop=(c == DC - 1))
                    mm.then_inc(s_("up_pe") if j else s_("gate_ready"), 1)

            def downs(e):
                k = e % 2
                if e == 0:
                    pe.wait_ge(down_in, 16 * (E // 2))
                pe.wait_ge(s_("act_ready"), e + 1)
                if e >= 2:
                    pe.wait_ge(s_("res_added"), e)
                for b in range(B):
                    for ic in range(IC):
                        mm = pe.matmul(bank(4 + k)[:, b * D:(b + 1) * D], act_s[:, k, ic * B * T + b * T:ic * B * T + (b + 1) * T],
                                       down_s[:, e, ic, :], start=(ic == 0), stop=(ic == IC - 1))
                mm.then_inc(s_("down_ready"), 1)

            gates_and_ups(0)
            pe.wait_ge(s_("gates_ready"), B)
            for b in range(B):
                mm = pe.transpose(ps[0:E, 512 * 7 + b * P:512 * 7 + (b + 1) * P], gates[:, b, :], ident[:, :])
            mm.then_inc(s_("gatesT"), 1)
            pe.wait_ge(s_("gatesT_copied"), 1)
            pe.wait_ge(small_in, 16 * 6)
            for b in range(B):
                mm = pe.matmul(bank(6)[:, b * D:(b + 1) * D], gatesT[:, b, :], down_b[:, :], start=True, stop=True)
            mm.then_inc(s_("bias_ready"), 1)
            for e in range(1, E):
                gates_and_ups(e)
                downs(e - 1)
            downs(E - 1)

        block = es.enter_context(nc.Block())

        @block.sync
        def _(sp):
            sp.dma_start(xt[:, :, :], x.rearrange("b t d -> t b d")).then_inc(x_in, 16)
            sp.dma_start(wk_s[:, :], Wk).then_inc(wk_in, 16)
            ctx_v = ctx.rearrange("b (k p) d -> p b k d", p=P)
            for b in range(B):
                if b == 0:
                    sp.dma_start(ctx_s[:, 0:KB, :], ctx_v[:, 0]).then_inc(ctx_in[0], 16)
                    for i in range(4):
                        w = H * P // 4
                        sp.dma_start(wq_s[:, :, i * w:(i + 1) * w],
                                     Wq.rearrange("(c p) n -> p c n", p=P)[:, :, i * w:(i + 1) * w]).then_inc(wq_in[i], 16)
                else:
                    sp.dma_start(ctx_s[:, KB:2 * KB, :], ctx_v[:, 1]).then_inc(ctx_in[1], 16)
            sp.dma_start(wv_s[:, :], Wv).then_inc(wv_in, 16)
            sp.dma_start(wo_s[:, :, :], Wo.rearrange("(h p) n -> p h n", p=P)).then_inc(wo_in, 16)
            sp.dma_start(w_qkv_s[:, :, :], w_qkv.rearrange("(c p) n -> p c n", p=P)).then_inc(attn_w_in, 16)
            sp.dma_start(w_out_s[:, :, :], w_out.rearrange("(c p) n -> p c n", p=P)).then_inc(attn_w_in, 16)
            sp.wait_ge(prep_act, n_act)
            sp.wait_ge(prep_dve, n_dve)
            sp.wait_ge(mask_ready, 1)
            gu_v = gate_up.rearrange("e (c p) n -> p e c n", p=P)
            for e in range(E // 2):
                sp.dma_start(gu_a[:, e], gu_v[:, e]).then_inc(gu_a_in, 16)
            sp.wait_ge(pT_ready, G * PAIRS)
            for e in range(E // 2):
                sp.dma_start(gu_b[:, e], gu_v[:, e + E // 2]).then_inc(gu_b_in, 16)
            for e in range(0, E, 2):
                sp.dma_start(down_s[:, e:e + 2], down.rearrange("e (c p) n -> p e c n", p=P)[:, e:e + 2]).then_inc(down_in, 16)

        @block.gpsimd
        def _(pool):
            pool.memset(ident[:, :], 0.0).then_inc(pool_set, 1)
            pool.memset(minus_half[:, :], -0.5).then_inc(pool_set, 1)
            pool.memset(causal[:, :], 0.0).then_inc(pool_set, 1)
            pool.memset(lower[:, :, :], 1.0).then_inc(pool_set, 1)
            pool.wait_ge(pool_set, 4)
            pool.affine_select(out=ident[:, :], in_=ident[:, :], compare_op=ALU.not_equal, fill=1.0, base=0,
                               pattern=[[-1, P]], channel_multiplier=1).then_inc(ident_ready, 1)
            for b in range(B):
                pool.wait_ge(ln_var, b + 1)
                pool.tensor_tensor(ln_rs[:, 0, b:b + 1], ln_ve[:, 0, b:b + 1], minus_half[:, 0:1], ALU.pow).then_inc(ln_rstd, 1)
            pool.affine_select(out=causal[:, :], in_=causal[:, :], compare_op=ALU.is_ge, fill=CAUSAL, base=0,
                               pattern=[[-1, P]], channel_multiplier=1).then_inc(consts_ready, 1)
            pool.affine_select(out=lower[:, :, :], in_=lower[:, :, :], compare_op=ALU.is_gt, fill=0.0, base=0,
                               pattern=[[1, E], [-1, E]], channel_multiplier=0).then_inc(consts_ready, 1)

            def split_ctx(j):
                part = slice(4 * j, 4 * j + 4)
                pool.tensor_copy(ctx_hi[:, part, :], ctx_s[:, part, :]).then_inc(ctx_split, 1)
                pool.wait_ge(ctx_split, 2 * j + 1)
                pool.tensor_tensor(ctx_lo[:, part, :], ctx_s[:, part, :], ctx_hi[:, part, :].bitcast(f32), ALU.subtract)\
                    .then_inc(ctx_split, 1)

            def split_q(m, par, m_at):
                if m_at >= 2:
                    pool.wait_ge(scores_ready, 4 * (m - 1))
                wait_above(pool, q_split_ready, m, m_at)
                src = qp[:, bass.ds(m * (2 * P), 2 * P)]
                pool.tensor_copy(q_pair[:, :], src)
                pool.tensor_copy(qs_hi[:, par, :], src).then_inc(q_hi_ready, 1)
                pool.wait_ge(q_hi_ready, m + 1)
                pool.tensor_tensor(qs_lo[:, par, :], q_pair[:, :], qs_hi[:, par, :].bitcast(f32), ALU.subtract)\
                    .then_inc(q_split_ready, 1)

            pool.wait_ge(ctx_in[0], 16)
            for j in range(4):
                split_ctx(j)
            pool.wait_ge(ctx_in[1], 16)
            for j in range(4, 8):
                split_ctx(j)
            s, v = evacuated(("qp", G - 1))
            pool.wait_ge(s, v)
            split_q(0, 0, 0)
            split_q(1, 1, 1)
            with pool.Fori(1, PAIRS // 2) as two:
                split_q(two * 2, 0, 2)
                split_q(two * 2 + 1, 1, 3)
            post_pool(pool)

        @block.tensor
        def _(pe):
            pe.wait_ge(ident_ready, 1)
            for k, task in enumerate(prep):
                kind, n = task
                if k >= 8:
                    s, v = evacuated(prep[k - 8])
                    pe.wait_ge(s, v)
                bk = bank(k % 8)
                if kind in ("wkT", "wvT"):
                    pe.wait_ge(wk_in if kind == "wkT" else wv_in, 16)
                    src = wk_s if kind == "wkT" else wv_s
                    for i in range(4):
                        g = 4 * n + i
                        mm = pe.transpose(bk[:, i * P:(i + 1) * P], src[:, g * P:(g + 1) * P], ident[:, :])
                elif kind == "ctx":
                    if n % 4 == 0:
                        pe.wait_ge(ctx_in[n // 4], 16)
                    for i in range(4):
                        mm = pe.transpose(bk[:, i * P:(i + 1) * P], ctx_s[:, 4 * n + i, :], ident[:, :])
                elif kind == "hT":
                    pe.wait_ge(ln_out, B)
                    for c in range(DC):
                        for b in range(B):
                            mm = pe.transpose(bk[:, (c * B + b) * P:(c * B + b + 1) * P], h0[:, b, c * P:(c + 1) * P], ident[:, :])
                elif kind == "q":
                    if n == 0:
                        s, v = evacuated(("hT", 0))
                        pe.wait_ge(s, v)
                    if n % 2 == 0:
                        pe.wait_ge(wq_in[n // 2], 16)
                    for i in range(2):
                        for c in range(DC):
                            h = 2 * n + i
                            mm = pe.matmul(bk[:, i * B * T:(i + 1) * B * T], wq_s[:, c, h * P:(h + 1) * P], hT0[:, c, :],
                                           start=(c == 0), stop=(c == DC - 1))
                elif kind == "qp":
                    s, v = evacuated(("q", n))
                    pe.wait_ge(s, v)
                    if n == 0:
                        s, v = evacuated(("wkT", 1))
                        pe.wait_ge(s, v)
                    mm = pe.matmul(bk, wkT[:, n, :], qT[:, n % 2, :], start=True, stop=True)
                elif kind == "wp":
                    if n == 0:
                        pe.wait_ge(wo_in, 16)
                        s, v = evacuated(("wvT", 1))
                        pe.wait_ge(s, v)
                    for i in range(2):
                        mm = pe.matmul(bk[:, i * D:(i + 1) * D], wvT[:, n, :], wo_s[:, 2 * n + i, :], start=True, stop=True)
                elif kind == "small":
                    pe.wait_ge(small_in, 16 * 6)
                    for ic in range(IC):
                        for j in range(2):
                            src = gu_bias[:, ic * 2 * P:(ic + 1) * 2 * P].rearrange("e (i two) -> e two i", two=2)[:, j, :]
                            pe.transpose(bk[:, (2 * ic + j) * E:(2 * ic + j + 1) * E], src, ident[0:E, 0:E])
                    for c in range(DC):
                        mm = pe.transpose(bk[:, (4 + c) * E:(5 + c) * E], router_s[:, c * P:(c + 1) * P], ident[0:E, 0:E])
                mm.then_inc(prep_pe, 1)

            pe.wait_ge(prep_act, n_act)
            pe.wait_ge(prep_dve, n_dve)
            pe.wait_ge(ctx_split, 16)

            def body(m, a):
                par = a % 2
                for i in range(8):
                    if live(a):
                        b, h, half = a // G, i // 4, (i // 2) % 2
                        if i == 0:
                            pe.wait_ge(q_split_ready, m + 1)
                        if i % 2 == 0:
                            wait_above(pe, scores_drained, 4 * m + i // 2 - 1, 4 * a + i // 2 - 1)
                        dst = bank(2 * ((i // 2) % 2) + i % 2)
                        keys = slice((i % 4) * 512, (i % 4 + 1) * 512)
                        qh, ql = qs_hi[:, par, h * P:(h + 1) * P], qs_lo[:, par, h * P:(h + 1) * P]
                        pe.matmul(dst, qh, ctxT_hi[:, b, keys], start=True, stop=False)
                        pe.matmul(dst, qh, ctxT_lo[:, b, keys], start=False, stop=False)
                        mm = pe.matmul(dst, ql, ctxT_hi[:, b, keys], start=False, stop=True)
                        if i % 2 == 1:
                            mm.then_inc(scores_ready, 1)
                    d = 1 if i >= 2 else 2
                    t = (i - 2) % 8
                    if live(a - d) or live(a - (1 if i >= 4 else 2)):
                        wait_above(pe, lo_ready, 8 * m + i - 11, 8 * a + i - 11)
                    if live(a - d):
                        if t % 4 == 0:
                            pe.wait_ge(exps, 4 * (m - d) + 3 + t // 4)
                        for j in range(4):
                            kb, h = 2 * t + j // 2, j % 2
                            mm = pe.transpose(bank(4 + t % 2)[:, j * P:(j + 1) * P],
                                              probs[:, (a - d) % 2, h, kb * P:(kb + 1) * P], ident[:, :])
                        mm.then_inc(pT_ready, 1)
                    d = 1 if i >= 4 else 2
                    t = (i - 4) % 8
                    if live(a - d):
                        b = (a - d) // G
                        if t == 0:
                            wait_above(pe, u_copied, m - d, a - d)
                        for j in range(2):
                            kb = 2 * t + j
                            hi, lo = pT_hi[:, t % 4, j * 2 * P:(j + 1) * 2 * P], pT_lo[:, t % 4, j * 2 * P:(j + 1) * 2 * P]
                            ch, cl = ctx_hi[:, b * KB + kb, :], ctx_lo[:, b * KB + kb, :]
                            pe.matmul(bank(6, 2 * P), ch, hi, start=(kb == 0), stop=False)
                            pe.matmul(bank(6, 2 * P), ch, lo, start=False, stop=False)
                            mm = pe.matmul(bank(6, 2 * P), cl, hi, start=False, stop=(kb == KB - 1))
                        if t == 7:
                            mm.then_inc(u_ready, 1)
                    if i == 6 and live(a - 2):
                        b = (a - 2) // G
                        pe.wait_ge(u_copied, m - 1)
                        wait_above(pe, proj_added, m - 2, a - 2)
                        for h in range(2):
                            w = wprime_v[:, bass.ds((m - 2 - G * b) * (2 * D) + h * D, D)]
                            mm = pe.matmul(bank(7)[:, h * D:(h + 1) * D], u_s[:, h * P:(h + 1) * P], w, start=True, stop=True)
                        mm.then_inc(proj_ready, 1)

            wprime_v = wprime[:, :, :].rearrange("p h n -> p (h n)")
            pair_loop(pe, body)
            post_pe(pe)

        @block.scalar
        def _(act):
            act.dma_start(mask_u8[:, :, :].rearrange("p b n -> p (b n)"), mask.rearrange("b n -> (b n)").partition_broadcast(P)).then_inc(mask_in, 16)
            act.dma_start(gu_bias[:, :], gate_up_bias).then_inc(small_in, 16)
            act.dma_start(router_s[:, :], router_w).then_inc(small_in, 16)
            act.dma_start(router_bb[:, :], router_b.partition_broadcast(P)).then_inc(small_in, 16)
            act.dma_start(gain_b[:, :], q_gain.partition_broadcast(P)).then_inc(small_in, 16)
            act.dma_start(rope_s[:, :, :], rope).then_inc(small_in, 16)
            act.dma_start(down_b[:, :], down_bias).then_inc(small_in, 16)
            for k, task in enumerate(prep):
                kind, n = task
                if "act" not in engines_of(task):
                    continue
                act.wait_ge(prep_pe, k + 1)
                bk = bank(k % 8)
                if kind == "ctx":
                    o_ = ctxT_hi[:, n // 4, (n % 4) * 512:(n % 4 + 1) * 512]
                elif kind == "q":
                    if n >= 2:
                        act.wait_ge(prep_pe, prep.index(("qp", n - 2)) + 1)
                    o_ = qT[:, n % 2, :]
                elif kind == "wvT":
                    o_ = wvT[:, 4 * n:4 * n + 4, :].rearrange("p g c -> p (g c)")
                elif kind == "wp":
                    o_ = wprime[:, 2 * n:2 * n + 2, :].rearrange("p g c -> p (g c)")
                act.activation(o_, bk, ACT.Copy).then_inc(prep_act, 1)
            act.wait_ge(ctx_split, 16)

            def body(m, a):
                for i in range(8):
                    if i == 4 and live(a - 2):
                        act.wait_ge(u_ready, m - 1)
                        act.activation(u_s[:, :], bank(6, 2 * P), ACT.Copy).then_inc(u_copied, 1)
                    d = 1 if i >= 2 else 2
                    t = (i - 2) % 8
                    if live(a - d):
                        act.wait_ge(pT_ready, 8 * m + i - 9)
                        act.activation(pT_hi[:, t % 4, :], bank(4 + t % 2), ACT.Copy).then_inc(hi_ready, 1)
                    if i % 2 == 1:
                        d, h, half = (0, 0, (i - 5) // 2) if i >= 5 else (1, 1, (i - 1) // 2)
                        if live(a - d):
                            par, c = (a - d) % 2, 2 * h + half
                            act.wait_ge(nb_ready, 2 * (m - d) + h + 1)
                            act.activation(probs[:, par, h, half * 1024:(half + 1) * 1024],
                                           scores[:, h, half * 1024:(half + 1) * 1024], ACT.Exp,
                                           bias=neg_max[:, par, h:h + 1], scale=SCALE,
                                           accum_out=row_sum[:, par, c:c + 1]).then_inc(exps, 1)

            pair_loop(act, body)
            post_act(act)

        @block.vector
        def _(dve):
            dve.memset(att_acc[:, :, :, :], 0.0).then_inc(acc_clear, 1)
            dve.wait_ge(x_in, 16)
            layer_norm(dve, 0, xt, h0)
            for k, task in enumerate(prep):
                kind, n = task
                if "dve" not in engines_of(task):
                    continue
                bk = bank(k % 8)
                if kind == "ctx":
                    act_n = sum("act" in engines_of(t) for t in prep[:k + 1])
                    dve.wait_ge(prep_act, act_n)
                    keys = slice((n % 4) * 512, (n % 4 + 1) * 512)
                    dve.tensor_tensor(ctxT_lo[:, n // 4, keys], bk, ctxT_hi[:, n // 4, keys].bitcast(f32),
                                      ALU.subtract).then_inc(prep_dve, 1)
                    if n == 3:
                        dve.wait_ge(mask_in, 16)
                        dve.tensor_scalar(mask_bias[:, :, :], mask_u8[:, :, :], 1.0, MASKED, ALU.subtract, ALU.mult).then_inc(mask_ready, 1)
                        dve.tensor_reduce(attend[:, :], mask_u8[:, :, :], AX.X, ALU.max).then_inc(mask_ready, 1)
                    continue
                dve.wait_ge(prep_pe, k + 1)
                if kind == "small":
                    dve.tensor_copy(gu_biasT[:, :, :, :].rearrange("p a b c -> p (a b c)"), bk[:, 0:4 * E]).then_inc(acc_clear, 1)
                    dve.tensor_copy(router_wT[:, :, :].rearrange("p a b -> p (a b)"), bk[:, 4 * E:6 * E]).then_inc(prep_dve, 1)
                    continue
                if kind == "wkT":
                    o_ = wkT[:, 4 * n:4 * n + 4, :].rearrange("p g c -> p (g c)")
                elif kind == "hT":
                    o_ = hT0[:, :, :].rearrange("p c t -> p (c t)")
                elif kind == "qp":
                    for b in range(B):
                        last = dve.tensor_copy(qp[:, (b * G + n) * 2 * P:(b * G + n + 1) * 2 * P].rearrange("p (h t) -> p h t", h=2),
                                               bk.rearrange("p (h b t) -> p h b t", h=2, b=B)[:, :, b, :])
                    last.then_inc(prep_dve, 1)
                    continue
                elif kind == "wp":
                    o_ = wprime[:, 2 * n:2 * n + 2, :].rearrange("p g c -> p (g c)")
                dve.tensor_copy(o_, bk).then_inc(prep_dve, 1)
            dve.wait_ge(ctx_split, 16)
            dve.wait_ge(mask_ready, 2)
            dve.wait_ge(acc_clear, 2)

            def body(m, a):
                for i in range(8):
                    d = 1 if i >= 2 else 2
                    t = (i - 2) % 8
                    if i % 2 == 1 and live(a):
                        dve.wait_ge(scores_ready, 4 * m + i // 2 + 1)
                        wait_above(dve, exps, 4 * m + i // 2 - 3, 4 * a + i // 2 - 3)
                    if live(a - d):
                        dve.wait_ge(hi_ready, 8 * m + i - 9)
                        dve.tensor_tensor(pT_lo[:, t % 4, :], bank(4 + t % 2), pT_hi[:, t % 4, :].bitcast(f32),
                                          ALU.subtract).then_inc(lo_ready, 1)
                    if i % 2 == 1 and live(a):
                        b, h, half, par, c = a // G, i // 4, (i // 2) % 2, a % 2, i // 2
                        keys = slice(half * 1024, (half + 1) * 1024)
                        dve.tensor_tensor_reduce(scores[:, h, keys], ps[:, 1024 * half:1024 * (half + 1)], mask_bias[:, b, keys],
                                                 1.0, -MASKED, ALU.add, ALU.max, row_max[:, par, c:c + 1]).then_inc(scores_drained, 1)
                        if half == 1:
                            dve.wait_ge(scores_drained, 4 * m + c + 1)
                            dve.tensor_scalar(neg_max[:, par, h:h + 1], row_max[:, par, c - 1:c], row_max[:, par, c:c + 1], -SCALE,
                                              ALU.max, ALU.mult).then_inc(nb_ready, 1)
                    if i == 6 and live(a - 1):
                        par = (a - 1) % 2
                        dve.wait_ge(exps, 4 * m)
                        dve.tensor_reduce(head_sum[:, par, :], row_sum[:, par, :].rearrange("p (h two) -> p h two", two=2),
                                          AX.X, ALU.add).then_inc(sums_ready, 1)
                        dve.wait_ge(sums_ready, m)
                        dve.reciprocal(head_inv[:, par, :], head_sum[:, par, :]).then_inc(inv_ready, 1)
                    if i == 7 and live(a - 2):
                        b, par = (a - 2) // G, a % 2
                        dve.wait_ge(proj_ready, m - 1)
                        wait_above(dve, proj_added, m - 2, a - 2)
                        dve.wait_ge(inv_ready, m - 1)
                        for h in range(2):
                            last = dve.scalar_tensor_tensor(out=att_acc[:, b, h, :], in0=bank(7)[:, h * D:(h + 1) * D],
                                                            scalar=head_inv[:, par, h:h + 1], in1=att_acc[:, b, h, :],
                                                            op0=ALU.mult, op1=ALU.add)
                        last.then_inc(proj_added, 1)

            pair_loop(dve, body)
            post_dve(dve)


_INS = ['x', 'ctx_1024', 'mask_BxS2_bf1', 'L0_xattn_Wq', 'L0_xattn_Wk', 'L0_xattn_Wv', 'L0_xattn_Wo', 'L0_attn_w_qkv',
        'L0_attn_w_out', 'L0_attn_q_gain', 'L0_ffn_router_weight', 'L0_ffn_router_bias', 'L0_ffn_gate_up_proj',
        'L0_ffn_gate_up_proj_bias', 'L0_ffn_down_proj', 'L0_ffn_down_proj_bias']
_OUTS = [((2, 128, 256), 'float32')]


def _rope_table(tokens=128, width=16, base=10000.0):
    import numpy as _np
    half = width // 2
    freq = _np.float32(base) ** (-_np.arange(half, dtype=_np.float32) / _np.float32(half))
    theta = _np.arange(tokens, dtype=_np.float32)[:, None] * freq[None, :]
    c, s = _np.cos(theta), _np.sin(theta)
    return _np.stack([_np.concatenate([c, c], 1), _np.concatenate([-s, s], 1)], 1).astype(_np.float32)


def kernel(**inputs):
    import numpy as _np
    import concourse.bacc as _bacc
    from concourse import mybir as _mybir
    from concourse.bass_utils import run_bass_kernel_spmd as _run

    nc = _bacc.Bacc("TRN2", target_bir_lowering=False, num_devices=1)
    arrays, args = {}, []
    for name in _INS + ['rope']:
        a = _rope_table() if name == 'rope' else _np.ascontiguousarray(inputs[name])
        if a.dtype == _np.bool_:
            a = a.view(_np.uint8)
        arrays[f"in_{name}_dram"] = a
        args.append(nc.dram_tensor(f"in_{name}_dram", a.shape, _mybir.dt.from_np(a.dtype), kind="ExternalInput").ap())
    for i, (shape, dtype) in enumerate(_OUTS):
        dt = _mybir.dt.from_np(_np.dtype(dtype))
        args.append(nc.dram_tensor(f"out_{i}_dram", shape, dt, kind="ExternalOutput").ap())
    perceiver_block(nc, *args)
    r = _run(nc, [arrays], core_ids=[0])
    got = tuple(r.results[0][f"out_{i}_dram"] for i in range(len(_OUTS)))
    return got[0]
```

```python
import concourse.bass as bass
from concourse import mybir
from contextlib import ExitStack
import math



def perceiver_block(nc, x, ctx, mask, Wq, Wk, Wv, Wo, w_qkv, w_out, q_gain, router_w, router_b,
                    gate_up, gate_up_bias, down, down_bias, rope, out):
    f32, i32, f32r, bf16, u8 = mybir.dt.float32, mybir.dt.int32, mybir.dt.float32r, mybir.dt.bfloat16, mybir.dt.uint8
    ALU, ACT, AX = mybir.AluOpType, mybir.ActivationFunctionType, mybir.AxisListType
    P = 128

    B, T, D = x.shape
    KEYS, DV = ctx.shape[1], ctx.shape[2]
    DC = D // P
    H = Wq.shape[1] // P
    G = Wk.shape[1] // P
    KB = KEYS // P
    PAIRS = B * G
    SH = 16
    SD = D // SH
    E, TWO_I = gate_up.shape[0], gate_up.shape[2]
    IC = TWO_I // 2 // P
    SCALE = 1.0 / math.sqrt(P)
    MASKED = 3.0e38
    CAUSAL = -3.0e38
    LN_EPS, UNIT_EPS = 1e-5, 1e-6
    ROOT_BITS = float(0x5F3759DF)
    ALPHA, LIMIT = 1.702, 7.0

    es = ExitStack()
    with es:
        at = {"next": (nc.sbuf_base + 63) // 64 * 64}

        def size(dt):
            return {f32: 4, f32r: 4, bf16: 2, u8: 1}[dt]

        def sb(name, shape, dt, over=None):
            n = size(dt)
            for s in shape[1:]:
                n *= s
            n = (n + 31) // 32 * 32
            if over is None:
                offset = at["next"]
                at["next"] += n
            else:
                offset = over["next"]
                over["next"] += n
                assert over["next"] <= over["end"], name
            return nc.alloc_sbuf_tensor_at(name, shape, dt, offset=offset)

        def region(nbytes):
            start = at["next"]
            at["next"] += nbytes
            return lambda skip=0: {"next": start + skip, "end": start + nbytes}

        def sem(name):
            return es.enter_context(nc.semaphore(name))

        ident = sb("ident", [P, P], f32)
        xt = sb("xt", [P, B, D], f32)
        wprime = sb("wprime", [P, H, D], f32)
        mask_bias = sb("mask_bias", [P, B, KEYS], bf16)
        attend = sb("attend", [P, B], f32)
        att_acc = sb("att_acc", [P, B, 2, D], f32)
        w_qkv_s = sb("w_qkv_s", [P, DC, 3 * D], f32)
        w_out_s = sb("w_out_s", [P, DC, D], f32)
        gain_b = sb("gain_b", [P, SH], f32)
        rope_s = sb("rope_s", [P, 2, SD], f32)
        router_wT = sb("router_wT", [P, DC, E], f32)
        router_bb = sb("router_bb", [P, E], f32)
        gu_biasT = sb("gu_biasT", [P, IC, 2, E], f32)
        down_b = sb("down_b", [E, D], f32)
        causal = sb("causal", [P, P], f32)
        lower = sb("lower", [P, E, E], f32)
        minus_half = sb("minus_half", [P, 1], f32)
        ln_st = sb("ln_st", [P, 3, B, 6], f32)
        ln_mv = sb("ln_mv", [P, 3, B, 2], f32)
        ln_ve = sb("ln_ve", [P, 3, B], f32)
        ln_rs = sb("ln_rs", [P, 3, B], f32)
        row_max = sb("row_max", [P, 2, 8], f32)
        neg_max = sb("neg_max", [P, 2, 2], f32)
        row_sum = sb("row_sum", [P, 2, 4], f32)
        head_sum = sb("head_sum", [P, 2, 2], f32)
        head_inv = sb("head_inv", [P, 2, 2], f32)
        q_pair = sb("q_pair", [P, 2 * P], f32)
        u_s = sb("u_s", [P, 2 * P], f32)
        r_ctx = region(4 * B * KEYS * 4)
        r_p = region(2 * 2 * KEYS * 4)
        r_sm = region(2 * KEYS * 4)
        r_pt = region(2 * 4 * 4 * P * 4)
        r_qp = region(PAIRS * 2 * P * 4)
        r_qs = region(2 * 2 * 2 * P * 4)
        r_late = region(4 * DC * TWO_I * 4)

        o = r_ctx()
        ctx_hi = sb("ctx_hi", [P, B * KB, P], f32r, o)
        ctx_lo = sb("ctx_lo", [P, B * KB, P], f32r, o)
        ctxT_hi = sb("ctxT_hi", [P, B, KEYS], f32r, o)
        ctxT_lo = sb("ctxT_lo", [P, B, KEYS], f32r, o)
        o = r_p()
        probs = sb("probs", [P, 2, 2, KEYS], f32, o)
        o = r_sm()
        scores = sb("scores", [P, 2, KEYS], f32, o)
        o = r_pt()
        pT_hi = sb("pT_hi", [P, 4, 4 * P], f32r, o)
        pT_lo = sb("pT_lo", [P, 4, 4 * P], f32r, o)
        o = r_qp()
        qp = sb("qp", [P, PAIRS * 2 * P], f32, o)
        o = r_qs()
        qs_hi = sb("qs_hi", [P, 2, 2 * P], f32r, o)
        qs_lo = sb("qs_lo", [P, 2, 2 * P], f32r, o)

        o = r_p()
        wq_s = sb("wq_s", [P, DC, H * P], f32, o)
        wo_s = sb("wo_s", [P, H, D], f32, o)
        o = r_sm()
        wk_s = sb("wk_s", [P, G * P], f32, o)
        wv_s = sb("wv_s", [P, G * P], f32, o)
        wkT = sb("wkT", [P, G, P], f32, o)
        wvT = sb("wvT", [P, G, P], f32, o)
        o = r_pt()
        ctx_s = sb("ctx_s", [P, B * KB, P], f32, o)
        o = r_late()
        qT = sb("qT", [P, 2, 2 * B * T], f32, o)
        mask_u8 = sb("mask_u8", [P, B, KEYS], u8, o)
        h0 = sb("h0", [P, B, D], f32, o)
        hT0 = sb("hT0", [P, DC, B * T], f32, o)
        gu_bias = sb("gu_bias", [E, TWO_I], f32, o)
        router_s = sb("router_s", [E, D], f32, o)

        EA, DA = 3, 2
        o = r_late()
        gu_a = sb("gu_a", [P, EA, DC, TWO_I], f32, o)
        down_a = sb("down_a", [P, DA, IC, D], f32, o)
        o = r_p()
        gu_b = sb("gu_b", [P, E - EA, DC, TWO_I], f32, o)
        down_b_ = sb("down_b_", [P, E - DA, IC, D], f32, o)
        o = r_sm()
        gate_s = sb("gate_s", [P, 2, IC * T], f32, o)
        tanh_s = sb("tanh_s", [P, 2, IC * T], f32, o)
        up_c = sb("up_c", [P, 2, IC * T], f32, o)
        up_1 = sb("up_1", [P, 2, IC * T], f32, o)
        glu_s = sb("glu_s", [P, 2, IC * T], f32, o)
        act_s = sb("act_s", [P, 2, IC * T], f32, o)

        part = KB * P * 4

        def per_row(name, shape, dt, piece, skip):
            out_ = []
            for b in range(B):
                o = r_ctx((2 * piece + b) * part + skip)
                out_.append(sb(f"{name}{b}", [P] + shape, dt, o))
                assert o["next"] <= r_ctx()["next"] + (2 * piece + b + 1) * part, name
            return out_

        qkz = per_row("qkz", [3, D], f32, 0, 0)
        qkT = per_row("qkT", [6, P], f32, 0, 3072)
        v1 = per_row("v1", [D], f32, 0, 6144)
        h1 = per_row("h1", [D], f32, 0, 7168)
        sq = per_row("sq", [2 * D], f32, 1, 0)
        res = per_row("res", [D], f32, 1, 0)
        hT1 = per_row("hT1", [DC * P], f32, 1, 2048)
        even = per_row("even", [2, SH // 2, SD], f32, 1, 3072)
        rot_a = per_row("rot_a", [2, SH // 2, SD], f32, 1, 4096)
        rot_b = per_row("rot_b", [2, SH // 2, SD], f32, 1, 5120)
        y1 = per_row("y1", [D], f32, 1, 6144)
        yT = per_row("yT", [DC * P], f32, 1, 7168)
        sm1 = per_row("sm1", [SH, P], f32, 2, 0)
        p1T = per_row("p1T", [2, 4, P], f32, 3, 0)
        x1 = per_row("x1", [D], f32, 3, 4096)
        x2 = per_row("x2", [D], f32, 3, 5120)
        hT2 = per_row("hT2", [DC, T], f32, 3, 6144)
        cmp_a = per_row("cmp_a", [E, E], f32, 3, 7168)
        cmp_b = per_row("cmp_b", [E, E], f32, 3, 7424)
        gatesT = per_row("gatesT", [P], f32, 3, 7680)
        norm_s = per_row("norm_s", [4, 2 * SH], f32, 0, 7168)
        stat_s = sb("stat_s", [P, B, 4, SH], f32)
        lg = per_row("lg", [E], f32, 1, 1024)
        top = per_row("top", [8], f32, 1, 1056)
        gap = per_row("gap", [4], f32, 1, 1088)
        rank = per_row("rank", [E], f32, 1, 1120)
        pick = per_row("pick", [2, E], f32, 1, 1152)
        gates = per_row("gates", [2, E], f32, 1, 1216)
        assert at["next"] <= nc.sbuf_usable_end, at

        ps = es.enter_context(nc.psum_tensor("ps", [P, 8 * 512], f32))

        def bank(k, n=512):
            return ps[:, 512 * k:512 * k + n]

        x_in, wk_in, ctx_in, mask_in = sem("x_in"), sem("wk_in"), [sem(f"ctx_in{b}") for b in range(B)], sem("mask_in")
        wq_in = [sem(f"wq_in{i}") for i in range(4)]
        wv_in, wo_in, small_in = sem("wv_in"), sem("wo_in"), sem("small_in")
        attn_w_in, out_stored = sem("attn_w_in"), sem("out_stored")
        gu_in, down_in = [sem(f"gu_in{e}") for e in range(E)], [sem(f"down_in{e}") for e in range(E)]
        ident_ready, consts_ready, pool_set = sem("ident_ready"), sem("consts_ready"), sem("pool_set")
        ln_stat, ln_aggr, ln_var, ln_rstd, ln_out = sem("ln_stat"), sem("ln_aggr"), sem("ln_var"), sem("ln_rstd"), sem("ln_out")
        prep_pe, prep_act, prep_dve = sem("prep_pe"), sem("prep_act"), sem("prep_dve")
        ctx_rounded, ctx_split = sem("ctx_rounded"), sem("ctx_split")
        mask_ready, acc_clear = sem("mask_ready"), sem("acc_clear")
        q_hi_ready, q_split_ready = sem("q_hi_ready"), sem("q_split_ready")
        scores_ready, scores_drained, nb_ready, exps = sem("scores_ready"), sem("scores_drained"), sem("nb_ready"), sem("exps")
        pT_ready, hi_ready, lo_ready = sem("pT_ready"), sem("hi_ready"), sem("lo_ready")
        u_ready, u_copied, proj_ready, proj_added = sem("u_ready"), sem("u_copied"), sem("proj_ready"), sem("proj_added")
        sums_ready, inv_ready = sem("sums_ready"), sem("inv_ready")

        prep = [("wkT", 0), ("wkT", 1), ("hT", 0), ("ctx", 0), ("ctx", 1), ("ctx", 2), ("ctx", 3),
                ("q", 0), ("q", 1), ("qp", 0), ("q", 2), ("qp", 1), ("q", 3), ("qp", 2), ("q", 4), ("qp", 3),
                ("q", 5), ("qp", 4), ("q", 6), ("qp", 5), ("q", 7), ("qp", 6), ("ctx", 4), ("qp", 7),
                ("ctx", 5), ("ctx", 6), ("ctx", 7), ("wvT", 0), ("wvT", 1), ("small", 0)] + [("wp", g) for g in range(G)]
        on_act = {"q", "wvT"}

        def engines_of(task):
            kind, n = task
            if kind == "ctx":
                return ("act", "dve")
            if kind == "wp":
                return ("act",) if n % 2 else ("dve",)
            return ("act",) if kind in on_act else ("dve",)

        def evacuated(task):
            e = engines_of(task)[-1]
            upto = prep[:prep.index(task) + 1]
            return (prep_act if e == "act" else prep_dve), sum(e in engines_of(t) for t in upto)

        n_act = sum("act" in engines_of(t) for t in prep)
        n_dve = sum("dve" in engines_of(t) for t in prep)

        def pair_loop(eng, body):
            body(0, 0)
            body(1, 1)
            with eng.Fori(1, G // 2) as two:
                body(two * 2, 2)
                body(two * 2 + 1, 3)
            for m in range(G, PAIRS + 2):
                body(m, m)

        def wait_above(eng, s, value, at_value):
            if at_value > 0:
                eng.wait_ge(s, value)

        def live(p):
            return 0 <= p < PAIRS

        def norm_count(n, b):
            return b if n == 0 else B + 2 * b + n - 1

        def norm_stats(dve, n, b, src):
            k = norm_count(n, b)
            dve.bn_stats(ln_st[:, n, b, :], src).then_inc(ln_stat, 1)
            dve.wait_ge(ln_stat, k + 1)
            dve.bn_aggr(ln_mv[:, n, b, :], ln_st[:, n, b, :]).then_inc(ln_aggr, 1)
            dve.wait_ge(ln_aggr, k + 1)
            dve.tensor_scalar(ln_ve[:, n, b:b + 1], ln_mv[:, n, b, 1:2], LN_EPS, None, ALU.add).then_inc(ln_var, 1)

        def norm_root(pool, n, b):
            k = norm_count(n, b)
            pool.wait_ge(ln_var, k + 1)
            pool.tensor_tensor(ln_rs[:, n, b:b + 1], ln_ve[:, n, b:b + 1], minus_half[:, 0:1], ALU.pow).then_inc(ln_rstd, 1)

        def norm_apply(dve, n, b, src, dst):
            k = norm_count(n, b)
            dve.wait_ge(ln_rstd, k + 1)
            dve.tensor_scalar(dst, src, ln_mv[:, n, b, 0:1], ln_rs[:, n, b:b + 1], ALU.subtract, ALU.mult).then_inc(ln_out, 1)

        s_ = {name: sem(name) for name in (
            "qkz_clear", "up_min", "up_ready", "qk_pe", "squares", "self_nb", "self_exp", "self_pT",
            "self_y", "pT_act", "gap", "gap_exp", "gate_min", "tanh_ready", "res_added", "root_y", "root_u",
            "att_sum", "x1_ready", "norm_a", "norm_sums", "norm_gain", "normed", "rotated", "qk_final",
            "self_scores", "self_max", "pT_dve", "self_inv", "y_ready", "self_proj", "x2_ready",
            "router_ready", "lg", "top", "cmp", "before", "above", "ranked", "gap_one", "second", "gap_inv",
            "both", "gates_ready", "gatesT", "gatesT_copied", "bias_ready", "res_init", "gu_pe", "glu",
            "down_ready", "act_ready", "hT1_pe", "hT1_ready", "v_pe", "v_ready", "qkTa_ready", "qkTb_ready",
            "yT_pe", "yT_ready", "hT2_pe", "hT2_ready", "qkTa_pe", "qkTb_pe",)}.__getitem__

        A_BANK, B_BANK = 2, 3

        def run_steps(eng, step, steps):
            for name, n in steps:
                step(eng, name, n)

        SELF_0 = [
            ("x1", "dve", 0), ("h1", "dve", 1), ("hT1", "pe", 2), ("hT1", "act", 3), ("qk", "pe", 4), ("qk", "act", 5),
            ("v", "pe", 5), ("v", "act", 6), ("qk", "dve", 7), ("inv1", "dve", 8), ("inv2", "dve", 9), ("unit", "dve", 10),
            ("rope", "dve", 11), ("qkTa", "pe", 12), ("qkTa", "act", 13), ("qkTb", "pe", 13), ("qkTb", "act", 14),
            ("S0", "pe", 15), ("S0", "dve", 16), ("S0", "act", 17), ("S1", "pe", 17), ("S1", "dve", 18), ("S1", "act", 19),
            ("S2", "pe", 19), ("S2", "dve", 20), ("S2", "act", 21), ("S3", "pe", 21), ("S3", "dve", 22), ("S3", "act", 23),
            ("T0", "pe", 23), ("T0", "act", 24), ("T1", "pe", 25), ("Y0", "pe", 26), ("T1", "dve", 26), ("T2", "pe", 27),
            ("Y1", "pe", 28), ("T2", "act", 28), ("T3", "pe", 29), ("Y2", "pe", 30), ("T3", "dve", 30), ("Y3", "pe", 31),
            ("y", "dve", 32), ("yT", "pe", 33), ("yT", "act", 34), ("proj", "pe", 35), ("proj", "dve", 36), ("h2", "dve", 38),
            ("hT2", "pe", 39), ("hT2", "act", 40), ("router", "pe", 41), ("router", "dve", 42), ("rank", "act", 43),
            ("rank", "dve", 43), ("weigh", "dve", 44), ("gT", "pe", 45), ("gT", "dve", 46), ("bias", "pe", 47), ("bias", "dve", 48)]

        def beside(eng, m, i):
            return [(name, 0) for name, e, slot in SELF_0 if e == eng and m == G + 2 + slot // 8 and i == slot % 8] \
                if isinstance(m, int) else []

        TAIL = [(name, 1) if isinstance(name, str) else ("expert", name) for name in (
            "x1", "h1", 0, "hT1", "qk", 1, "v", "inv1", "inv2", "unit", "rope", 2, "qkTa", "qkTb", "S0", 3, "S1", "S2", "S3", 4,
            "T0", "T1", "Y0", "T2", 5, "Y1", "T3", "Y2", "Y3", 6, "y", "yT", 7, "proj", "h2", "hT2", "router", 8, "rank",
            "weigh", "gT", 9, "bias", 10, 11, 12, 13, 14, 15, 16, 17)]

        def pool_step(pool, name, b):
            if name == "x1":
                pool.wait_ge(proj_added, G * (b + 1))
                pool.memset(qkz[b][:, :, :], 0.0).then_inc(s_("qkz_clear"), 1)
                norm_root(pool, 1, b)
            elif name == "proj":
                norm_root(pool, 2, b)
            elif name == "expert" and b < B * E:
                pool.wait_ge(s_("up_min"), b + 1)
                pool.tensor_scalar(up_1[:, b % 2, :], up_c[:, b % 2, :], -LIMIT, 1.0, ALU.max, ALU.add).then_inc(s_("up_ready"), 1)

        def act_step(act, name, b):
            def copy_out(wait_for, dst, src, done):
                act.wait_ge(s_(wait_for), b + 1)
                act.activation(dst, src, ACT.Copy).then_inc(s_(done), 1)

            if name == "hT1":
                copy_out("hT1_pe", hT1[b][:, :], bank(A_BANK, DC * P), "hT1_ready")
            elif name == "qk":
                act.wait_ge(s_("qk_pe"), b + 1)
                act.activation(sq[b][:, :], bank(B_BANK), ACT.Square).then_inc(s_("squares"), 1)
            elif name == "v":
                copy_out("v_pe", v1[b][:, :], bank(A_BANK, D), "v_ready")
            elif name == "qkTa":
                copy_out("qkTa_pe", qkT[b][:, 0:4, :], bank(A_BANK), "qkTa_ready")
            elif name == "qkTb":
                copy_out("qkTb_pe", qkT[b][:, 4:6, :], bank(B_BANK, 2 * P), "qkTb_ready")
            elif name[0] == "S":
                g = int(name[1])
                act.wait_ge(s_("self_nb"), 4 * b + g + 1)
                for n in range(4 * g, 4 * g + 4):
                    last = act.activation(sm1[b][:, n, :], sm1[b][:, n, :], ACT.Exp, bias=stat_s[:, b, 1, n:n + 1],
                                          accum_out=stat_s[:, b, 2, n:n + 1])
                last.then_inc(s_("self_exp"), 1)
            elif name in ("T0", "T2"):
                g = int(name[1])
                act.wait_ge(s_("self_pT"), 4 * b + g + 1)
                if g == 2:
                    act.wait_ge(s_("self_y"), 4 * b + 1)
                act.activation(p1T[b][:, 0, :, :], bank(A_BANK), ACT.Copy).then_inc(s_("pT_act"), 1)
            elif name == "yT":
                copy_out("yT_pe", yT[b][:, :], bank(A_BANK, DC * P), "yT_ready")
            elif name == "hT2":
                copy_out("hT2_pe", hT2[b][:, :, :], bank(A_BANK, DC * P), "hT2_ready")
            elif name == "rank":
                act.wait_ge(s_("gap"), b + 1)
                act.activation(gap[b][:, 1:2], gap[b][:, 0:1], ACT.Exp).then_inc(s_("gap_exp"), 1)
            elif name == "expert" and b < B * E:
                act.wait_ge(s_("gate_min"), b + 1)
                act.activation(tanh_s[:, b % 2, :], gate_s[:, b % 2, :], ACT.Tanh, scale=ALPHA / 2).then_inc(s_("tanh_ready"), 1)
            elif name == "expert" and b == B * E:
                store(act, 0)

        def store(act, b=B - 1):
            act.wait_ge(s_("res_added"), E * (b + 1))
            act.dma_start(out[b], res[b][:, :]).then_inc(out_stored, 16)
            if b == B - 1:
                act.wait_ge(out_stored, 16 * B)

        def newton(dve, b, k):
            y, s, u = norm_s[b][:, 2, :], norm_s[b][:, 1, :], norm_s[b][:, 0, :]
            dve.wait_ge(s_("root_y"), 4 * b + k + 1)
            dve.scalar_tensor_tensor(out=u, in0=y, scalar=-0.5, in1=y, op0=ALU.mult, op1=ALU.mult).then_inc(s_("root_u"), 1)
            dve.wait_ge(s_("root_u"), 6 * b + 2 * k + 1)
            dve.tensor_tensor(u, u, s, ALU.mult).then_inc(s_("root_u"), 1)
            dve.wait_ge(s_("root_u"), 6 * b + 2 * k + 2)
            dve.scalar_tensor_tensor(out=y, in0=u, scalar=1.5, in1=y, op0=ALU.add, op1=ALU.mult).then_inc(s_("root_y"), 1)

        def dve_step(dve, name, b):
            if name == "x1":
                dve.wait_ge(proj_added, G * (b + 1))
                dve.tensor_tensor(y1[b][:, :], att_acc[:, b, 0, :], att_acc[:, b, 1, :], ALU.add).then_inc(s_("att_sum"), 1)
                dve.wait_ge(s_("att_sum"), b + 1)
                dve.scalar_tensor_tensor(out=x1[b][:, :], in0=y1[b][:, :], scalar=attend[:, b:b + 1], in1=xt[:, b, :],
                                         op0=ALU.mult, op1=ALU.add).then_inc(s_("x1_ready"), 1)
                dve.wait_ge(s_("x1_ready"), b + 1)
                norm_stats(dve, 1, b, x1[b][:, :])
            elif name == "h1":
                norm_apply(dve, 1, b, x1[b][:, :], h1[b][:, :])
            elif name == "qk":
                dve.wait_ge(s_("squares"), b + 1)
                dve.tensor_reduce(norm_s[b][:, 0, :], sq[b][:, :].rearrange("p (h d) -> p h d", d=SD), AX.X, ALU.add).then_inc(s_("norm_a"), 1)
                dve.wait_ge(s_("norm_a"), b + 1)
                dve.tensor_scalar(norm_s[b][:, 1, :], norm_s[b][:, 0, :], UNIT_EPS, None, ALU.add).then_inc(s_("norm_sums"), 1)
                dve.wait_ge(s_("norm_sums"), b + 1)
                dve.tensor_scalar(norm_s[b][:, 2, :].bitcast(i32), norm_s[b][:, 1, :].bitcast(i32), -0.5, ROOT_BITS,
                                  ALU.mult, ALU.add).then_inc(s_("root_y"), 1)
                newton(dve, b, 0)
            elif name in ("inv1", "inv2"):
                newton(dve, b, int(name[3]))
            elif name == "unit":
                dve.wait_ge(s_("root_y"), 4 * (b + 1))
                dve.wait_ge(small_in, 16 * 6)
                dve.tensor_tensor(norm_s[b][:, 3, 0:SH], norm_s[b][:, 2, 0:SH], gain_b[:, :], ALU.mult)
                dve.tensor_copy(norm_s[b][:, 3, SH:2 * SH], norm_s[b][:, 2, SH:2 * SH]).then_inc(s_("norm_gain"), 1)
                dve.wait_ge(s_("norm_gain"), b + 1)
                dve.wait_ge(s_("qkz_clear"), b + 1)
                qk_v = bank(B_BANK).rearrange("p (w n two d) -> p w n two d", w=2, two=2, d=SD)
                rg_v = norm_s[b][:, 3, :].rearrange("p (w n two) -> p w n two", w=2, two=2)
                for w in range(2):
                    dve.tensor_tensor(even[b][:, w], qk_v[:, w, :, 0, :], rg_v[:, w, :, 0:1].broadcast_to([P, SH // 2, SD]), ALU.mult)
                    dst = qkz[b][:, 1 + w, :].rearrange("p (n two d) -> p n two d", two=2, d=SD)
                    last = dve.tensor_tensor(dst[:, :, 1, :], qk_v[:, w, :, 1, :], rg_v[:, w, :, 1:2].broadcast_to([P, SH // 2, SD]), ALU.mult)
                last.then_inc(s_("normed"), 1)
            elif name == "rope":
                dve.wait_ge(s_("normed"), b + 1)
                ev = even[b][:, :, :, :].rearrange("p w n d -> p (w n) d")
                ra = rot_a[b][:, :, :, :].rearrange("p w n d -> p (w n) d")
                rb = rot_b[b][:, :, :, :].rearrange("p w n d -> p (w n) d")
                HD = SD // 2
                dve.tensor_tensor(ra, ev, rope_s[:, 0:1, :].broadcast_to([P, SH, SD]), ALU.mult)
                dve.tensor_tensor(rb[:, :, 0:HD], ev[:, :, HD:SD], rope_s[:, 1:2, 0:HD].broadcast_to([P, SH, HD]), ALU.mult)
                dve.tensor_tensor(rb[:, :, HD:SD], ev[:, :, 0:HD], rope_s[:, 1:2, HD:SD].broadcast_to([P, SH, HD]), ALU.mult)\
                    .then_inc(s_("rotated"), 1)
                dve.wait_ge(s_("rotated"), b + 1)
                for w in range(2):
                    dst = qkz[b][:, 2 * w, :].rearrange("p (n two d) -> p n two d", two=2, d=SD)
                    last = dve.tensor_tensor(dst[:, :, 0, :], rot_a[b][:, w], rot_b[b][:, w], ALU.add)
                last.then_inc(s_("qk_final"), 1)
            elif name[0] == "S":
                g = int(name[1])
                dve.wait_ge(consts_ready, 2)
                dve.wait_ge(s_("self_scores"), 4 * b + g + 1)
                for r in range(4):
                    n = 4 * g + r
                    last = dve.tensor_tensor_reduce(sm1[b][:, n, :], bank(A_BANK + g % 2)[:, r * P:(r + 1) * P], causal[:, :],
                                                    1.0, CAUSAL, ALU.add, ALU.max, stat_s[:, b, 0, n:n + 1])
                last.then_inc(s_("self_max"), 1)
                dve.wait_ge(s_("self_max"), 4 * b + g + 1)
                dve.tensor_scalar(stat_s[:, b, 1, 4 * g:4 * g + 4], stat_s[:, b, 0, 4 * g:4 * g + 4], -1.0, None, ALU.mult)\
                    .then_inc(s_("self_nb"), 1)
            elif name in ("T1", "T3"):
                g = int(name[1])
                dve.wait_ge(s_("self_pT"), 4 * b + g + 1)
                if g == 3:
                    dve.wait_ge(s_("self_y"), 4 * b + 2)
                dve.tensor_copy(p1T[b][:, 1, :, :], bank(A_BANK).rearrange("p (h t) -> p h t", t=P)).then_inc(s_("pT_dve"), 1)
            elif name == "y":
                dve.wait_ge(s_("self_exp"), 4 * b + 4)
                dve.reciprocal(stat_s[:, b, 3, :], stat_s[:, b, 2, :]).then_inc(s_("self_inv"), 1)
                dve.wait_ge(s_("self_inv"), b + 1)
                dve.wait_ge(s_("self_y"), 4 * b + 4)
                y_v = bank(B_BANK, D).rearrange("p (c g r d) -> p c g r d", c=2, g=4, r=2)
                l_v = stat_s[:, b, 3, :].rearrange("p (g c r) -> p c g r", c=2, r=2)
                o_v = y1[b][:, :].rearrange("p (c g r d) -> p c g r d", c=2, g=4, r=2)
                for c in range(2):
                    for r in range(2):
                        last = dve.tensor_tensor(o_v[:, c, :, r, :], y_v[:, c, :, r, :],
                                                 l_v[:, c, :, r:r + 1].broadcast_to([P, 4, SD]), ALU.mult)
                last.then_inc(s_("y_ready"), 1)
            elif name == "proj":
                dve.wait_ge(s_("self_proj"), b + 1)
                dve.tensor_tensor(x2[b][:, :], x1[b][:, :], bank(B_BANK, D), ALU.add).then_inc(s_("x2_ready"), 1)
                dve.wait_ge(s_("x2_ready"), b + 1)
                norm_stats(dve, 2, b, x2[b][:, :])
            elif name == "h2":
                norm_apply(dve, 2, b, x2[b][:, :], h1[b][:, :])
            elif name == "router":
                dve.wait_ge(s_("router_ready"), b + 1)
                dve.tensor_tensor(lg[b][:, :], bank(B_BANK, E), router_bb[:, :], ALU.add).then_inc(s_("lg"), 1)
                dve.wait_ge(s_("lg"), b + 1)
                dve.max(top[b][:, :], lg[b][:, :]).then_inc(s_("top"), 1)
                l_e = lg[b][:, :].unsqueeze(2).broadcast_to([P, E, E])
                l_j = lg[b][:, :].unsqueeze(1).broadcast_to([P, E, E])
                dve.tensor_tensor(cmp_a[b][:, :, :], l_j, l_e, ALU.is_gt)
                dve.tensor_tensor(cmp_b[b][:, :, :], l_j, l_e, ALU.is_equal).then_inc(s_("cmp"), 1)
                dve.wait_ge(s_("top"), b + 1)
                dve.tensor_tensor(gap[b][:, 0:1], top[b][:, 1:2], top[b][:, 0:1], ALU.subtract).then_inc(s_("gap"), 1)
            elif name == "rank":
                dve.wait_ge(s_("cmp"), b + 1)
                dve.tensor_tensor(cmp_b[b][:, :, :], cmp_b[b][:, :, :], lower[:, :, :], ALU.mult).then_inc(s_("before"), 1)
                dve.wait_ge(s_("before"), b + 1)
                dve.tensor_tensor(cmp_a[b][:, :, :], cmp_a[b][:, :, :], cmp_b[b][:, :, :], ALU.add).then_inc(s_("above"), 1)
                dve.wait_ge(s_("above"), b + 1)
                dve.tensor_reduce(rank[b][:, :], cmp_a[b][:, :, :], AX.X, ALU.add).then_inc(s_("ranked"), 1)
            elif name == "weigh":
                dve.wait_ge(s_("gap_exp"), b + 1)
                dve.tensor_scalar(gap[b][:, 2:3], gap[b][:, 1:2], 1.0, None, ALU.add).then_inc(s_("gap_one"), 1)
                dve.wait_ge(s_("ranked"), b + 1)
                dve.tensor_scalar(pick[b][:, 0, :], rank[b][:, :], 1.0, gap[b][:, 1:2], ALU.is_equal, ALU.mult).then_inc(s_("second"), 1)
                dve.wait_ge(s_("gap_one"), b + 1)
                dve.reciprocal(gap[b][:, 3:4], gap[b][:, 2:3]).then_inc(s_("gap_inv"), 1)
                dve.wait_ge(s_("second"), b + 1)
                dve.scalar_tensor_tensor(out=pick[b][:, 1, :], in0=rank[b][:, :], scalar=0.0, in1=pick[b][:, 0, :],
                                         op0=ALU.is_equal, op1=ALU.add).then_inc(s_("both"), 1)
                dve.wait_ge(s_("gap_inv"), b + 1)
                dve.wait_ge(s_("both"), b + 1)
                dve.tensor_scalar(gates[b][:, 0, :], pick[b][:, 1, :], gap[b][:, 3:4], None, ALU.mult)
                dve.tensor_scalar(gates[b][:, 1, :], pick[b][:, 1, :], gap[b][:, 3:4], 0.5, ALU.mult, ALU.mult).then_inc(s_("gates_ready"), 1)
            elif name == "gT":
                dve.wait_ge(s_("gatesT"), b + 1)
                dve.tensor_copy(gatesT[b][0:E, :], ps[0:E, 512 * A_BANK:512 * A_BANK + P]).then_inc(s_("gatesT_copied"), 1)
            elif name == "bias":
                dve.wait_ge(s_("bias_ready"), b + 1)
                dve.tensor_tensor(res[b][:, :], bank(B_BANK, D), x2[b][:, :], ALU.add).then_inc(s_("res_init"), 1)
            elif name == "expert":
                n = b
                if n < B * E:
                    k, e = n % 2, n % E
                    dve.wait_ge(s_("gu_pe"), n + 1)
                    for ic in range(IC):
                        last = dve.tensor_scalar(gate_s[:, k, ic * T:(ic + 1) * T], bank(4 + k)[:, ic * T:(ic + 1) * T],
                                                 gu_biasT[:, ic, 0, e:e + 1], LIMIT, ALU.add, ALU.min)
                    last.then_inc(s_("gate_min"), 1)
                    for ic in range(IC):
                        last = dve.tensor_scalar(up_c[:, k, ic * T:(ic + 1) * T], bank(4 + k)[:, (IC + ic) * T:(IC + ic + 1) * T],
                                                 gu_biasT[:, ic, 1, e:e + 1], LIMIT, ALU.add, ALU.min)
                    last.then_inc(s_("up_min"), 1)
                if 1 <= n <= B * E:
                    k = (n - 1) % 2
                    dve.wait_ge(s_("tanh_ready"), n)
                    dve.scalar_tensor_tensor(out=glu_s[:, k, :], in0=tanh_s[:, k, :], scalar=1.0, in1=gate_s[:, k, :],
                                             op0=ALU.add, op1=ALU.mult).then_inc(s_("glu"), 1)
                    dve.wait_ge(s_("glu"), n)
                    dve.wait_ge(s_("up_ready"), n)
                    if n >= 3:
                        dve.wait_ge(s_("down_ready"), n - 2)
                    dve.tensor_tensor(act_s[:, k, :], glu_s[:, k, :], up_1[:, k, :], ALU.mult).then_inc(s_("act_ready"), 1)
                if 2 <= n:
                    row, e = (n - 2) // E, (n - 2) % E
                    dve.wait_ge(s_("down_ready"), n - 1)
                    if e == 0:
                        dve.wait_ge(s_("res_init"), row + 1)
                    else:
                        dve.wait_ge(s_("res_added"), n - 2)
                    dve.scalar_tensor_tensor(out=res[row][:, :], in0=bank(6 + n % 2, D), scalar=gates[row][:, 1, e:e + 1],
                                             in1=res[row][:, :], op0=ALU.mult, op1=ALU.add).then_inc(s_("res_added"), 1)

        def pe_step(pe, name, b):
            if name == "hT1":
                pe.wait_ge(ln_out, norm_count(1, b) + 1)
                if b > 0:
                    pe.wait_ge(s_("gatesT_copied"), b)
                for c in range(DC):
                    mm = pe.transpose(bank(A_BANK)[:, c * P:(c + 1) * P], h1[b][:, c * P:(c + 1) * P], ident[:, :])
                mm.then_inc(s_("hT1_pe"), 1)
            elif name == "qk":
                if b == 0:
                    pe.wait_ge(attn_w_in, 32)
                else:
                    pe.wait_ge(s_("res_init"), b)
                pe.wait_ge(s_("hT1_ready"), b + 1)
                for c in range(DC):
                    mm = pe.matmul(bank(B_BANK), hT1[b][:, c * P:(c + 1) * P], w_qkv_s[:, c, 0:2 * D], start=(c == 0), stop=(c == DC - 1))
                mm.then_inc(s_("qk_pe"), 1)
            elif name == "v":
                for c in range(DC):
                    mm = pe.matmul(bank(A_BANK, D), hT1[b][:, c * P:(c + 1) * P], w_qkv_s[:, c, 2 * D:3 * D], start=(c == 0), stop=(c == DC - 1))
                mm.then_inc(s_("v_pe"), 1)
            elif name in ("qkTa", "qkTb"):
                pe.wait_ge(s_("qk_final"), b + 1)
                if name == "qkTa":
                    pe.wait_ge(s_("v_ready"), b + 1)
                for n in range(4) if name == "qkTa" else range(4, 6):
                    dst = bank(A_BANK if n < 4 else B_BANK)[:, n % 4 * P:(n % 4 + 1) * P]
                    mm = pe.transpose(dst, qkz[b][:, n // DC, n % DC * P:(n % DC + 1) * P], ident[:, :])
                mm.then_inc(s_(name + "_pe"), 1)
            elif name[0] == "S":
                g = int(name[1])
                rows = slice(32 * g, 32 * g + 32)
                if g == 0:
                    pe.wait_ge(s_("qkTa_ready"), b + 1)
                    pe.wait_ge(s_("qkTb_ready"), b + 1)
                elif g >= 2:
                    pe.wait_ge(s_("self_max"), 4 * b + g - 1)
                for r in range(4):
                    c, odd = r // 2, r % 2
                    mm = pe.matmul(bank(A_BANK + g % 2)[:, r * P:(r + 1) * P], qkT[b][rows, odd * DC + c, :], qkT[b][rows, 2 * DC + c, :],
                                   start=True, stop=True)
                mm.then_inc(s_("self_scores"), 1)
            elif name[0] == "T":
                g = int(name[1])
                pe.wait_ge(s_("self_exp"), 4 * b + g + 1)
                if g == 0:
                    pe.wait_ge(s_("self_max"), 4 * b + 3)
                else:
                    pe.wait_ge(s_("pT_act") if g % 2 else s_("pT_dve"), 2 * b + (g - 1) // 2 + 1)
                for r in range(4):
                    mm = pe.transpose(bank(A_BANK)[:, r * P:(r + 1) * P], sm1[b][:, 4 * g + r, :], ident[:, :])
                mm.then_inc(s_("self_pT"), 1)
            elif name[0] == "Y":
                g = int(name[1])
                pe.wait_ge(s_("pT_dve") if g % 2 else s_("pT_act"), 2 * b + g // 2 + 1)
                if g == 0:
                    pe.wait_ge(s_("self_max"), 4 * b + 4)
                for r in range(4):
                    h = (r // 2) * 8 + 2 * g + r % 2
                    mm = pe.matmul(bank(B_BANK)[:, h * SD:(h + 1) * SD], p1T[b][:, g % 2, r, :], v1[b][:, h * SD:(h + 1) * SD],
                                   start=True, stop=True)
                mm.then_inc(s_("self_y"), 1)
            elif name == "yT":
                pe.wait_ge(s_("y_ready"), b + 1)
                for c in range(DC):
                    mm = pe.transpose(bank(A_BANK)[:, c * P:(c + 1) * P], y1[b][:, c * P:(c + 1) * P], ident[:, :])
                mm.then_inc(s_("yT_pe"), 1)
            elif name == "proj":
                pe.wait_ge(s_("yT_ready"), b + 1)
                for c in range(DC):
                    mm = pe.matmul(bank(B_BANK, D), yT[b][:, c * P:(c + 1) * P], w_out_s[:, c, :], start=(c == 0), stop=(c == DC - 1))
                mm.then_inc(s_("self_proj"), 1)
            elif name == "hT2":
                pe.wait_ge(ln_out, norm_count(2, b) + 1)
                for c in range(DC):
                    mm = pe.transpose(bank(A_BANK)[:, c * P:(c + 1) * P], h1[b][:, c * P:(c + 1) * P], ident[:, :])
                mm.then_inc(s_("hT2_pe"), 1)
            elif name == "router":
                pe.wait_ge(s_("hT2_ready"), b + 1)
                for c in range(DC):
                    mm = pe.matmul(bank(B_BANK, E), hT2[b][:, c, :], router_wT[:, c, :], start=(c == 0), stop=(c == DC - 1))
                mm.then_inc(s_("router_ready"), 1)
            elif name == "gT":
                pe.wait_ge(s_("gates_ready"), b + 1)
                pe.transpose(ps[0:E, 512 * A_BANK:512 * A_BANK + P], gates[b][:, 0, :], ident[:, :]).then_inc(s_("gatesT"), 1)
            elif name == "bias":
                pe.wait_ge(s_("gatesT_copied"), b + 1)
                pe.matmul(bank(B_BANK, D), gatesT[b][0:E, :], down_b[:, :], start=True, stop=True).then_inc(s_("bias_ready"), 1)
            elif name == "expert":
                n = b
                if n < B * E:
                    row, e = n // E, n % E
                    if row == 0:
                        pe.wait_ge(gu_in[e], 16)
                    if e == 0:
                        pe.wait_ge(s_("hT2_ready"), row + 1)
                    if n == 0:
                        pe.wait_ge(proj_added, PAIRS)
                    if n >= 2:
                        pe.wait_ge(s_("up_min"), n - 1)
                    w = gu_a[:, e] if e < EA else gu_b[:, e - EA]
                    for j in range(2):
                        for ic in range(IC):
                            for c in range(DC):
                                lhs = w[:, c, ic * 2 * P:(ic + 1) * 2 * P].rearrange("p (i two) -> p two i", two=2)[:, j, :]
                                mm = pe.matmul(bank(4 + n % 2)[:, (j * IC + ic) * T:(j * IC + ic + 1) * T], lhs, hT2[row][:, c, :],
                                               start=(c == 0), stop=(c == DC - 1))
                    mm.then_inc(s_("gu_pe"), 1)
                if n >= 2:
                    o = n - 2
                    row, e = o // E, o % E
                    if row == 0:
                        pe.wait_ge(down_in[e], 16)
                    pe.wait_ge(s_("act_ready"), o + 1)
                    if o >= 2:
                        pe.wait_ge(s_("res_added"), o - 1)
                    w = down_a[:, e] if e < DA else down_b_[:, e - DA]
                    for ic in range(IC):
                        mm = pe.matmul(bank(6 + o % 2, D), act_s[:, o % 2, ic * T:(ic + 1) * T], w[:, ic, :],
                                       start=(ic == 0), stop=(ic == IC - 1))
                    mm.then_inc(s_("down_ready"), 1)

        block = es.enter_context(nc.Block())

        @block.sync
        def _(sp):
            sp.dma_start(xt[:, :, :], x.rearrange("b t d -> t b d")).then_inc(x_in, 16)
            sp.dma_start(wk_s[:, :], Wk).then_inc(wk_in, 16)
            ctx_v = ctx.rearrange("b (k p) d -> p b k d", p=P)
            for b in range(B):
                if b == 0:
                    sp.dma_start(ctx_s[:, 0:KB, :], ctx_v[:, 0]).then_inc(ctx_in[0], 16)
                    for i in range(4):
                        w = H * P // 4
                        sp.dma_start(wq_s[:, :, i * w:(i + 1) * w],
                                     Wq.rearrange("(c p) n -> p c n", p=P)[:, :, i * w:(i + 1) * w]).then_inc(wq_in[i], 16)
                else:
                    sp.dma_start(ctx_s[:, KB:2 * KB, :], ctx_v[:, 1]).then_inc(ctx_in[1], 16)
            sp.dma_start(wv_s[:, :], Wv).then_inc(wv_in, 16)
            sp.dma_start(wo_s[:, :, :], Wo.rearrange("(h p) n -> p h n", p=P)).then_inc(wo_in, 16)
            sp.dma_start(w_qkv_s[:, :, :], w_qkv.rearrange("(c p) n -> p c n", p=P)).then_inc(attn_w_in, 16)
            sp.dma_start(w_out_s[:, :, :], w_out.rearrange("(c p) n -> p c n", p=P)).then_inc(attn_w_in, 16)
            sp.wait_ge(prep_act, n_act)
            sp.wait_ge(prep_dve, n_dve)
            sp.wait_ge(mask_ready, 1)
            gu_v = gate_up.rearrange("e (c p) n -> p e c n", p=P)
            down_v = down.rearrange("e (c p) n -> p e c n", p=P)
            for e in range(EA):
                sp.dma_start(gu_a[:, e], gu_v[:, e]).then_inc(gu_in[e], 16)
            for e in range(DA):
                sp.dma_start(down_a[:, e], down_v[:, e]).then_inc(down_in[e], 16)
            sp.wait_ge(pT_ready, G * PAIRS)
            for e in range(min(EA, DA), E):
                if e >= DA:
                    sp.dma_start(down_b_[:, e - DA], down_v[:, e]).then_inc(down_in[e], 16)
                if e >= EA:
                    sp.dma_start(gu_b[:, e - EA], gu_v[:, e]).then_inc(gu_in[e], 16)

        @block.gpsimd
        def _(pool):
            pool.memset(ident[:, :], 0.0).then_inc(pool_set, 1)
            pool.memset(minus_half[:, :], -0.5).then_inc(pool_set, 1)
            pool.memset(causal[:, :], 0.0).then_inc(pool_set, 1)
            pool.memset(lower[:, :, :], 1.0).then_inc(pool_set, 1)
            pool.wait_ge(pool_set, 4)
            pool.affine_select(out=ident[:, :], in_=ident[:, :], compare_op=ALU.not_equal, fill=1.0, base=0,
                               pattern=[[-1, P]], channel_multiplier=1).then_inc(ident_ready, 1)
            for b in range(B):
                norm_root(pool, 0, b)
            pool.affine_select(out=causal[:, :], in_=causal[:, :], compare_op=ALU.is_ge, fill=CAUSAL, base=0,
                               pattern=[[-1, P]], channel_multiplier=1).then_inc(consts_ready, 1)
            pool.affine_select(out=lower[:, :, :], in_=lower[:, :, :], compare_op=ALU.is_gt, fill=0.0, base=0,
                               pattern=[[1, E], [-1, E]], channel_multiplier=0).then_inc(consts_ready, 1)

            def split_ctx(j):
                part = slice(4 * j, 4 * j + 4)
                pool.wait_ge(ctx_rounded, j + 1)
                pool.tensor_tensor(ctx_lo[:, part, :], ctx_s[:, part, :], ctx_hi[:, part, :].bitcast(f32), ALU.subtract)\
                    .then_inc(ctx_split, 1)

            def split_q(m, par, m_at):
                if m_at >= 2:
                    pool.wait_ge(scores_ready, 8 * (m - 1))
                wait_above(pool, q_split_ready, m, m_at)
                src = qp[:, bass.ds(m * (2 * P), 2 * P)]
                pool.tensor_copy(q_pair[:, :], src)
                pool.tensor_copy(qs_hi[:, par, :], src).then_inc(q_hi_ready, 1)
                pool.wait_ge(q_hi_ready, m + 1)
                pool.tensor_tensor(qs_lo[:, par, :], q_pair[:, :], qs_hi[:, par, :].bitcast(f32), ALU.subtract)\
                    .then_inc(q_split_ready, 1)

            for j in range(8):
                split_ctx(j)
            s, v = evacuated(("qp", G - 1))
            pool.wait_ge(s, v)
            split_q(0, 0, 0)
            split_q(1, 1, 1)
            with pool.Fori(1, G // 2) as two:
                split_q(two * 2, 0, 2)
                split_q(two * 2 + 1, 1, 3)
            for m in range(G, PAIRS):
                split_q(m, m % 2, m)
                if m == G + 3:
                    run_steps(pool, pool_step, [("x1", 0)])
                if m == G + 6:
                    run_steps(pool, pool_step, [("proj", 0)])
            run_steps(pool, pool_step, TAIL)

        @block.tensor
        def _(pe):
            pe.wait_ge(ident_ready, 1)
            for k, task in enumerate(prep):
                kind, n = task
                if k >= 8:
                    s, v = evacuated(prep[k - 8])
                    pe.wait_ge(s, v)
                bk = bank(k % 8)
                if kind in ("wkT", "wvT"):
                    pe.wait_ge(wk_in if kind == "wkT" else wv_in, 16)
                    src = wk_s if kind == "wkT" else wv_s
                    for i in range(4):
                        g = 4 * n + i
                        mm = pe.transpose(bk[:, i * P:(i + 1) * P], src[:, g * P:(g + 1) * P], ident[:, :])
                elif kind == "ctx":
                    if n % 4 == 0:
                        pe.wait_ge(ctx_in[n // 4], 16)
                    for i in range(4):
                        mm = pe.transpose(bk[:, i * P:(i + 1) * P], ctx_s[:, 4 * n + i, :], ident[:, :])
                elif kind == "hT":
                    pe.wait_ge(ln_out, B)
                    for c in range(DC):
                        for b in range(B):
                            mm = pe.transpose(bk[:, (c * B + b) * P:(c * B + b + 1) * P], h0[:, b, c * P:(c + 1) * P], ident[:, :])
                elif kind == "q":
                    if n == 0:
                        s, v = evacuated(("hT", 0))
                        pe.wait_ge(s, v)
                    if n % 2 == 0:
                        pe.wait_ge(wq_in[n // 2], 16)
                    for i in range(2):
                        for c in range(DC):
                            h = 2 * n + i
                            mm = pe.matmul(bk[:, i * B * T:(i + 1) * B * T], wq_s[:, c, h * P:(h + 1) * P], hT0[:, c, :],
                                           start=(c == 0), stop=(c == DC - 1))
                elif kind == "qp":
                    s, v = evacuated(("q", n))
                    pe.wait_ge(s, v)
                    if n == 0:
                        s, v = evacuated(("wkT", 1))
                        pe.wait_ge(s, v)
                    mm = pe.matmul(bk, wkT[:, n, :], qT[:, n % 2, :], start=True, stop=True)
                elif kind == "wp":
                    if n == 0:
                        pe.wait_ge(wo_in, 16)
                        s, v = evacuated(("wvT", 1))
                        pe.wait_ge(s, v)
                    for i in range(2):
                        mm = pe.matmul(bk[:, i * D:(i + 1) * D], wvT[:, n, :], wo_s[:, 2 * n + i, :], start=True, stop=True)
                elif kind == "small":
                    pe.wait_ge(small_in, 16 * 6)
                    for ic in range(IC):
                        for j in range(2):
                            src = gu_bias[:, ic * 2 * P:(ic + 1) * 2 * P].rearrange("e (i two) -> e two i", two=2)[:, j, :]
                            pe.transpose(bk[:, (2 * ic + j) * E:(2 * ic + j + 1) * E], src, ident[0:E, 0:E])
                    for c in range(DC):
                        mm = pe.transpose(bk[:, (4 + c) * E:(5 + c) * E], router_s[:, c * P:(c + 1) * P], ident[0:E, 0:E])
                mm.then_inc(prep_pe, 1)

            pe.wait_ge(prep_act, n_act)
            pe.wait_ge(prep_dve, n_dve)
            pe.wait_ge(ctx_split, 8)

            def body(m, a):
                par = a % 2
                for i in range(8):
                    if live(a):
                        b, h = a // G, i // 4
                        if i == 0:
                            pe.wait_ge(q_split_ready, m + 1)
                        wait_above(pe, scores_drained, 8 * m + i - 1, 8 * a + i - 1)
                        dst = bank(i % 2)
                        keys = slice((i % 4) * 512, (i % 4 + 1) * 512)
                        qh, ql = qs_hi[:, par, h * P:(h + 1) * P], qs_lo[:, par, h * P:(h + 1) * P]
                        pe.matmul(dst, qh, ctxT_hi[:, b, keys], start=True, stop=False)
                        pe.matmul(dst, qh, ctxT_lo[:, b, keys], start=False, stop=False)
                        mm = pe.matmul(dst, ql, ctxT_hi[:, b, keys], start=False, stop=True)
                        mm.then_inc(scores_ready, 1)
                    d = 1 if i >= 2 else 2
                    t = (i - 2) % 8
                    if live(a - d) or live(a - (1 if i >= 4 else 2)):
                        wait_above(pe, lo_ready, 8 * m + i - 11, 8 * a + i - 11)
                    if live(a - d):
                        if t % 4 == 0:
                            pe.wait_ge(exps, 4 * (m - d) + 3 + t // 4)
                        for j in range(4):
                            kb, h = 2 * t + j // 2, j % 2
                            mm = pe.transpose(bank(4 + t % 2)[:, j * P:(j + 1) * P],
                                              probs[:, (a - d) % 2, h, kb * P:(kb + 1) * P], ident[:, :])
                        mm.then_inc(pT_ready, 1)
                    d = 1 if i >= 4 else 2
                    t = (i - 4) % 8
                    if live(a - d):
                        b = (a - d) // G
                        u_bank = bank(6 + (a - d) % 2, 2 * P)
                        for j in range(2):
                            kb = 2 * t + j
                            hi, lo = pT_hi[:, t % 4, j * 2 * P:(j + 1) * 2 * P], pT_lo[:, t % 4, j * 2 * P:(j + 1) * 2 * P]
                            ch, cl = ctx_hi[:, b * KB + kb, :], ctx_lo[:, b * KB + kb, :]
                            pe.matmul(u_bank, ch, hi, start=(kb == 0), stop=False)
                            pe.matmul(u_bank, ch, lo, start=False, stop=False)
                            mm = pe.matmul(u_bank, cl, hi, start=False, stop=(kb == KB - 1))
                        if t == 7:
                            mm.then_inc(u_ready, 1)
                    if i == 6 and live(a - 2):
                        b = (a - 2) // G
                        pe.wait_ge(u_copied, m - 1)
                        for h in range(2):
                            w = wprime_v[:, bass.ds((m - 2 - G * b) * (2 * D) + h * D, D)]
                            mm = pe.matmul(bank(6 + a % 2)[:, h * D:(h + 1) * D], u_s[:, h * P:(h + 1) * P], w, start=True, stop=True)
                        mm.then_inc(proj_ready, 1)
                    run_steps(pe, pe_step, beside('pe', m, i))

            wprime_v = wprime[:, :, :].rearrange("p h n -> p (h n)")
            pair_loop(pe, body)
            run_steps(pe, pe_step, TAIL)

        @block.scalar
        def _(act):
            act.dma_start(mask_u8[:, :, :].rearrange("p b n -> p (b n)"), mask.rearrange("b n -> (b n)").partition_broadcast(P)).then_inc(mask_in, 16)
            act.dma_start(gu_bias[:, :], gate_up_bias).then_inc(small_in, 16)
            act.dma_start(router_s[:, :], router_w).then_inc(small_in, 16)
            act.dma_start(router_bb[:, :], router_b.partition_broadcast(P)).then_inc(small_in, 16)
            act.dma_start(gain_b[:, :], q_gain.partition_broadcast(P)).then_inc(small_in, 16)
            act.dma_start(rope_s[:, :, :], rope).then_inc(small_in, 16)
            act.dma_start(down_b[:, :], down_bias).then_inc(small_in, 16)
            for k, task in enumerate(prep):
                kind, n = task
                if "act" not in engines_of(task):
                    continue
                if kind == "ctx":
                    if n % 4 == 0:
                        act.wait_ge(ctx_in[n // 4], 16)
                    act.activation(ctx_hi[:, 4 * n:4 * n + 4, :], ctx_s[:, 4 * n:4 * n + 4, :], ACT.Copy).then_inc(ctx_rounded, 1)
                act.wait_ge(prep_pe, k + 1)
                bk = bank(k % 8)
                if kind == "ctx":
                    o_ = ctxT_hi[:, n // 4, (n % 4) * 512:(n % 4 + 1) * 512]
                elif kind == "q":
                    if n >= 2:
                        act.wait_ge(prep_pe, prep.index(("qp", n - 2)) + 1)
                    o_ = qT[:, n % 2, :]
                elif kind == "wvT":
                    o_ = wvT[:, 4 * n:4 * n + 4, :].rearrange("p g c -> p (g c)")
                elif kind == "wp":
                    o_ = wprime[:, 2 * n:2 * n + 2, :].rearrange("p g c -> p (g c)")
                act.activation(o_, bk, ACT.Copy).then_inc(prep_act, 1)
            act.wait_ge(ctx_split, 8)

            def body(m, a):
                for i in range(8):
                    d = 1 if i >= 2 else 2
                    t = (i - 2) % 8
                    if live(a - d):
                        act.wait_ge(pT_ready, 8 * m + i - 9)
                        act.activation(pT_hi[:, t % 4, :], bank(4 + t % 2), ACT.Copy).then_inc(hi_ready, 1)
                    if i == 4 and live(a - 2):
                        act.wait_ge(u_ready, m - 1)
                        act.activation(u_s[:, :], bank(6 + a % 2, 2 * P), ACT.Copy).then_inc(u_copied, 1)
                    if i % 2 == 1:
                        d, h, half = (0, 0, (i - 5) // 2) if i >= 5 else (1, 1, (i - 1) // 2)
                        if live(a - d):
                            par, c = (a - d) % 2, 2 * h + half
                            act.wait_ge(nb_ready, 2 * (m - d) + h + 1)
                            act.activation(probs[:, par, h, half * 1024:(half + 1) * 1024],
                                           scores[:, h, half * 1024:(half + 1) * 1024], ACT.Exp,
                                           bias=neg_max[:, par, h:h + 1], scale=SCALE,
                                           accum_out=row_sum[:, par, c:c + 1]).then_inc(exps, 1)
                    run_steps(act, act_step, beside('act', m, i))

            pair_loop(act, body)
            run_steps(act, act_step, TAIL)
            store(act)

        @block.vector
        def _(dve):
            dve.memset(att_acc[:, :, :, :], 0.0).then_inc(acc_clear, 1)
            dve.wait_ge(x_in, 16)
            for b in range(B):
                norm_stats(dve, 0, b, xt[:, b, :])
            for b in range(B):
                norm_apply(dve, 0, b, xt[:, b, :], h0[:, b, :])
            for k, task in enumerate(prep):
                kind, n = task
                if "dve" not in engines_of(task):
                    continue
                bk = bank(k % 8)
                if kind == "ctx":
                    act_n = sum("act" in engines_of(t) for t in prep[:k + 1])
                    dve.wait_ge(prep_act, act_n)
                    keys = slice((n % 4) * 512, (n % 4 + 1) * 512)
                    dve.tensor_tensor(ctxT_lo[:, n // 4, keys], bk, ctxT_hi[:, n // 4, keys].bitcast(f32),
                                      ALU.subtract).then_inc(prep_dve, 1)
                    if n == 3:
                        dve.wait_ge(mask_in, 16)
                        dve.tensor_scalar(mask_bias[:, :, :], mask_u8[:, :, :], 1.0, MASKED, ALU.subtract, ALU.mult).then_inc(mask_ready, 1)
                        dve.tensor_reduce(attend[:, :], mask_u8[:, :, :], AX.X, ALU.max).then_inc(mask_ready, 1)
                    continue
                dve.wait_ge(prep_pe, k + 1)
                if kind == "small":
                    dve.tensor_copy(gu_biasT[:, :, :, :].rearrange("p a b c -> p (a b c)"), bk[:, 0:4 * E]).then_inc(acc_clear, 1)
                    dve.tensor_copy(router_wT[:, :, :].rearrange("p a b -> p (a b)"), bk[:, 4 * E:6 * E]).then_inc(prep_dve, 1)
                    continue
                if kind == "wkT":
                    o_ = wkT[:, 4 * n:4 * n + 4, :].rearrange("p g c -> p (g c)")
                elif kind == "hT":
                    o_ = hT0[:, :, :].rearrange("p c t -> p (c t)")
                elif kind == "qp":
                    for b in range(B):
                        last = dve.tensor_copy(qp[:, (b * G + n) * 2 * P:(b * G + n + 1) * 2 * P].rearrange("p (h t) -> p h t", h=2),
                                               bk.rearrange("p (h b t) -> p h b t", h=2, b=B)[:, :, b, :])
                    last.then_inc(prep_dve, 1)
                    continue
                elif kind == "wp":
                    o_ = wprime[:, 2 * n:2 * n + 2, :].rearrange("p g c -> p (g c)")
                dve.tensor_copy(o_, bk).then_inc(prep_dve, 1)
            dve.wait_ge(ctx_split, 8)
            dve.wait_ge(mask_ready, 2)
            dve.wait_ge(acc_clear, 2)

            def add_head(m, a, h):
                b, par = (a - 2) // G, a % 2
                if h == 0:
                    dve.wait_ge(proj_ready, m - 1)
                    wait_above(dve, proj_added, m - 2, a - 2)
                    dve.wait_ge(inv_ready, m - 1)
                last = dve.scalar_tensor_tensor(out=att_acc[:, b, h, :], in0=bank(6 + a % 2)[:, h * D:(h + 1) * D],
                                                scalar=head_inv[:, par, h:h + 1], in1=att_acc[:, b, h, :],
                                                op0=ALU.mult, op1=ALU.add)
                if h == 1:
                    last.then_inc(proj_added, 1)

            def body(m, a):
                for i in range(8):
                    d = 1 if i >= 2 else 2
                    t = (i - 2) % 8
                    if i == 7 and live(a - 2):
                        add_head(m, a, 0)
                    if live(a):
                        dve.wait_ge(scores_ready, 8 * m + i + 1)
                        wait_above(dve, exps, 4 * m + i // 2 - 3, 4 * a + i // 2 - 3)
                        wait_above(dve, scores_drained, 8 * m + i, 8 * a + i)
                    if live(a - d):
                        dve.wait_ge(hi_ready, 8 * m + i - 9)
                        dve.tensor_tensor(pT_lo[:, t % 4, :], bank(4 + t % 2), pT_hi[:, t % 4, :].bitcast(f32),
                                          ALU.subtract).then_inc(lo_ready, 1)
                    if live(a):
                        b, h, par = a // G, i // 4, a % 2
                        keys = slice((i % 4) * 512, (i % 4 + 1) * 512)
                        dve.tensor_tensor_reduce(scores[:, h, keys], bank(i % 2), mask_bias[:, b, keys], 1.0,
                                                 row_max[:, par, i - 1:i] if i % 4 else -MASKED,
                                                 ALU.add, ALU.max, row_max[:, par, i:i + 1]).then_inc(scores_drained, 1)
                        if i % 4 == 3:
                            dve.wait_ge(scores_drained, 8 * m + i + 1)
                            dve.tensor_scalar(neg_max[:, par, h:h + 1], row_max[:, par, i:i + 1], -SCALE, None,
                                              ALU.mult).then_inc(nb_ready, 1)
                    if i == 6 and live(a - 1):
                        par = (a - 1) % 2
                        dve.wait_ge(exps, 4 * m)
                        dve.tensor_reduce(head_sum[:, par, :], row_sum[:, par, :].rearrange("p (h two) -> p h two", two=2),
                                          AX.X, ALU.add).then_inc(sums_ready, 1)
                        dve.wait_ge(sums_ready, m)
                        dve.reciprocal(head_inv[:, par, :], head_sum[:, par, :]).then_inc(inv_ready, 1)
                    if i == 7 and live(a - 2):
                        add_head(m, a, 1)
                    run_steps(dve, dve_step, beside('dve', m, i))

            pair_loop(dve, body)
            run_steps(dve, dve_step, TAIL)


_INS = ['x', 'ctx_1024', 'mask_BxS2_bf1', 'L0_xattn_Wq', 'L0_xattn_Wk', 'L0_xattn_Wv', 'L0_xattn_Wo', 'L0_attn_w_qkv',
        'L0_attn_w_out', 'L0_attn_q_gain', 'L0_ffn_router_weight', 'L0_ffn_router_bias', 'L0_ffn_gate_up_proj',
        'L0_ffn_gate_up_proj_bias', 'L0_ffn_down_proj', 'L0_ffn_down_proj_bias']
_OUTS = [((2, 128, 256), 'float32')]


def _rope_table(tokens=128, width=16, base=10000.0):
    import numpy as _np
    half = width // 2
    freq = _np.float32(base) ** (-_np.arange(half, dtype=_np.float32) / _np.float32(half))
    theta = _np.arange(tokens, dtype=_np.float32)[:, None] * freq[None, :]
    c, s = _np.cos(theta), _np.sin(theta)
    return _np.stack([_np.concatenate([c, c], 1), _np.concatenate([-s, s], 1)], 1).astype(_np.float32)


def kernel(**inputs):
    import numpy as _np
    import concourse.bacc as _bacc
    from concourse import mybir as _mybir
    from concourse.bass_utils import run_bass_kernel_spmd as _run

    nc = _bacc.Bacc("TRN2", target_bir_lowering=False, num_devices=1)
    arrays, args = {}, []
    for name in _INS + ['rope']:
        a = _rope_table() if name == 'rope' else _np.ascontiguousarray(inputs[name])
        if a.dtype == _np.bool_:
            a = a.view(_np.uint8)
        arrays[f"in_{name}_dram"] = a
        args.append(nc.dram_tensor(f"in_{name}_dram", a.shape, _mybir.dt.from_np(a.dtype), kind="ExternalInput").ap())
    for i, (shape, dtype) in enumerate(_OUTS):
        dt = _mybir.dt.from_np(_np.dtype(dtype))
        args.append(nc.dram_tensor(f"out_{i}_dram", shape, dt, kind="ExternalOutput").ap())
    perceiver_block(nc, *args)
    r = _run(nc, [arrays], core_ids=[0])
    got = tuple(r.results[0][f"out_{i}_dram"] for i in range(len(_OUTS)))
    return got[0]
```

```python
import concourse.bass as bass
from concourse import mybir
from contextlib import ExitStack
import math



def perceiver_block(nc, x, ctx, mask, Wq, Wk, Wv, Wo, w_qkv, w_out, q_gain, router_w, router_b,
                    gate_up, gate_up_bias, down, down_bias, rope, out):
    f32, i32, f32r, bf16, u8 = mybir.dt.float32, mybir.dt.int32, mybir.dt.float32r, mybir.dt.bfloat16, mybir.dt.uint8
    ALU, ACT, AX = mybir.AluOpType, mybir.ActivationFunctionType, mybir.AxisListType
    P = 128

    B, T, D = x.shape
    KEYS, DV = ctx.shape[1], ctx.shape[2]
    DC = D // P
    H = Wq.shape[1] // P
    G = Wk.shape[1] // P
    KB = KEYS // P
    PAIRS = B * G
    SH = 16
    SD = D // SH
    E, TWO_I = gate_up.shape[0], gate_up.shape[2]
    IC = TWO_I // 2 // P
    SCALE = 1.0 / math.sqrt(P)
    MASKED = 3.0e38
    CAUSAL = -3.0e38
    LN_EPS, UNIT_EPS = 1e-5, 1e-6
    ROOT_BITS = float(0x5F3759DF)
    ALPHA, LIMIT = 1.702, 7.0

    es = ExitStack()
    with es:
        at = {"next": (nc.sbuf_base + 63) // 64 * 64}

        def size(dt):
            return {f32: 4, f32r: 4, bf16: 2, u8: 1}[dt]

        def sb(name, shape, dt, over=None):
            n = size(dt)
            for s in shape[1:]:
                n *= s
            n = (n + 31) // 32 * 32
            if over is None:
                offset = at["next"]
                at["next"] += n
            else:
                offset = over["next"]
                over["next"] += n
                assert over["next"] <= over["end"], name
            return nc.alloc_sbuf_tensor_at(name, shape, dt, offset=offset)

        def region(nbytes):
            start = at["next"]
            at["next"] += nbytes
            return lambda skip=0: {"next": start + skip, "end": start + nbytes}

        def sem(name):
            return es.enter_context(nc.semaphore(name))

        ident = sb("ident", [P, P], f32)
        xt = sb("xt", [P, B, D], f32)
        wprime = sb("wprime", [P, H, D], f32)
        mask_bias = sb("mask_bias", [P, B, KEYS], bf16)
        attend = sb("attend", [P, B], f32)
        att_acc = sb("att_acc", [P, B, 2, D], f32)
        r_qkv = region(DC * 3 * D * 4)
        w_out_s = sb("w_out_s", [P, DC, D], f32)
        gain_b = sb("gain_b", [P, SH], f32)
        rope_s = sb("rope_s", [P, 2, SD], f32)
        router_wT = sb("router_wT", [P, DC, E], f32)
        router_bb = sb("router_bb", [P, E], f32)
        gu_biasT = sb("gu_biasT", [P, IC, 2, E], f32)
        down_b = sb("down_b", [E, D], f32)
        causal = sb("causal", [P, P], f32)
        lower = sb("lower", [P, E, E], f32)
        minus_half = sb("minus_half", [P, 1], f32)
        ln_st = sb("ln_st", [P, 3, B, 6], f32)
        ln_mv = sb("ln_mv", [P, 3, B, 2], f32)
        ln_ve = sb("ln_ve", [P, 3, B], f32)
        ln_rs = sb("ln_rs", [P, 3, B], f32)
        row_max = sb("row_max", [P, 2, 8], f32)
        neg_max = sb("neg_max", [P, 2, 2], f32)
        row_sum = sb("row_sum", [P, 2, 4], f32)
        head_sum = sb("head_sum", [P, 2, 2], f32)
        head_inv = sb("head_inv", [P, 2, 2], f32)
        att_inv = sb("att_inv", [P, 2], f32)
        q_pair = sb("q_pair", [P, 2 * P], f32)
        u_s = sb("u_s", [P, 2 * P], f32)
        r_ctx = region(4 * B * KEYS * 4)
        r_p = region(2 * 2 * KEYS * 4)
        r_sm = region(2 * KEYS * 4)
        r_pt = region(2 * 4 * 4 * P * 4)
        r_qp = region(PAIRS * 2 * P * 4)
        r_qs = region(2 * 2 * 2 * P * 4)
        r_late = region(4 * DC * TWO_I * 4)

        o = r_ctx()
        ctx_hi = sb("ctx_hi", [P, B * KB, P], f32r, o)
        ctx_lo = sb("ctx_lo", [P, B * KB, P], f32r, o)
        ctxT_hi = sb("ctxT_hi", [P, B, KEYS], f32r, o)
        ctxT_lo = sb("ctxT_lo", [P, B, KEYS], f32r, o)
        o = r_p()
        probs = sb("probs", [P, 2, 2, KEYS], f32, o)
        o = r_sm()
        scores = sb("scores", [P, 2, KEYS], f32, o)
        o = r_pt()
        pT_hi = sb("pT_hi", [P, 4, 4 * P], f32r, o)
        pT_lo = sb("pT_lo", [P, 4, 4 * P], f32r, o)
        o = r_qp()
        qp = sb("qp", [P, PAIRS * 2 * P], f32, o)
        o = r_qs()
        qs_hi = sb("qs_hi", [P, 2, 2 * P], f32r, o)
        qs_lo = sb("qs_lo", [P, 2, 2 * P], f32r, o)

        w_qkv_s = sb("w_qkv_s", [P, DC, 3 * D], f32, r_qkv())

        wvT = sb("wvT", [P, G, P], f32, r_qkv())
        o = r_p()
        wq_s = sb("wq_s", [P, DC, H * P], f32, o)
        wo_s = sb("wo_s", [P, H, D], f32, o)
        o = r_sm()
        wk_s = sb("wk_s", [P, G * P], f32, o)
        wv_s = sb("wv_s", [P, G * P], f32, o)
        wkT = sb("wkT", [P, G, P], f32, o)
        o = r_pt()
        ctx_s = sb("ctx_s", [P, B * KB, P], f32, o)
        o = r_late()
        qT = sb("qT", [P, 2, 2 * B * T], f32, o)
        mask_u8 = sb("mask_u8", [P, B, KEYS], u8, o)
        h0 = sb("h0", [P, B, D], f32, o)
        hT0 = sb("hT0", [P, DC, B * T], f32, o)
        gu_bias = sb("gu_bias", [E, TWO_I], f32, o)
        router_s = sb("router_s", [E, D], f32, o)

        EA, DA = 3, 2
        o = r_late()
        gu_a = sb("gu_a", [P, EA, DC, TWO_I], f32, o)
        down_a = sb("down_a", [P, DA, IC, D], f32, o)
        o = r_p()
        gu_b = sb("gu_b", [P, E - EA, DC, TWO_I], f32, o)
        down_b_ = sb("down_b_", [P, E - DA, IC, D], f32, o)
        o = r_sm()
        gate_r = sb("gate_r", [P, 2, IC * T], f32, o)
        up_r = sb("up_r", [P, 2, IC * T], f32, o)
        gate_s = sb("gate_s", [P, 2, IC * T], f32, o)
        up_c = sb("up_c", [P, 2, IC * T], f32, o)
        tanh_s = sb("tanh_s", [P, 2, IC * T], f32, o)
        glu_s = sb("glu_s", [P, 2, IC * T], f32, o)
        act_s = sb("act_s", [P, 2, IC * T], f32, o)

        part = KB * P * 4

        def per_row(name, shape, dt, piece, skip):
            out_ = []
            for b in range(B):
                o = r_ctx((2 * piece + b) * part + skip)
                out_.append(sb(f"{name}{b}", [P] + shape, dt, o))
                assert o["next"] <= r_ctx()["next"] + (2 * piece + b + 1) * part, name
            return out_

        qkz = per_row("qkz", [3, D], f32, 0, 0)
        qkT = per_row("qkT", [6, P], f32, 0, 3072)
        vz = per_row("vz", [2, D], f32, 0, 6144)
        sq = per_row("sq", [2 * D], f32, 1, 0)
        res = per_row("res", [D], f32, 1, 0)
        hT1 = per_row("hT1", [DC * P], f32, 1, 2048)
        even = per_row("even", [SH, SD], f32, 1, 3072)
        rot_a = per_row("rot_a", [SH, SD], f32, 1, 4096)
        rot_b = per_row("rot_b", [SH, SD], f32, 1, 5120)
        y1 = per_row("y1", [D], f32, 1, 6144)
        h1 = per_row("h1", [D], f32, 1, 6144)
        yT = per_row("yT", [DC * P], f32, 1, 7168)
        sm1 = per_row("sm1", [SH, P], f32, 2, 0)
        qk_c = per_row("qk_c", [2 * D], f32, 2, 0)
        p1T = per_row("p1T", [2, 4, P], f32, 3, 0)
        x1 = per_row("x1", [D], f32, 3, 4096)
        x2 = per_row("x2", [D], f32, 3, 5120)
        hT2 = per_row("hT2", [DC, T], f32, 3, 6144)
        cmp_a = per_row("cmp_a", [E, E], f32, 3, 7168)
        cmp_b = per_row("cmp_b", [E, E], f32, 3, 7424)
        gatesT = per_row("gatesT", [P], f32, 3, 7680)
        norm_s = per_row("norm_s", [4, 2 * SH], f32, 1, 6144)
        stat_s = sb("stat_s", [P, B, 4, SH], f32)
        lg = per_row("lg", [E], f32, 1, 1024)
        top = per_row("top", [8], f32, 1, 1056)
        gap = per_row("gap", [4], f32, 1, 1088)
        rank = per_row("rank", [E], f32, 1, 1120)
        pick = per_row("pick", [2, E], f32, 1, 1152)
        gates = per_row("gates", [2, E], f32, 1, 1216)
        assert at["next"] <= nc.sbuf_usable_end, at

        ps = es.enter_context(nc.psum_tensor("ps", [P, 8 * 512], f32))

        def bank(k, n=512):
            return ps[:, 512 * k:512 * k + n]

        x_in, wk_in, mask_in = sem("x_in"), [sem(f"wk_in{n}") for n in range(2)], sem("mask_in")
        ctx_in = [sem(f"ctx_in{n}") for n in range(3)]
        wq_in = [sem(f"wq_in{i}") for i in range(4)]
        wv_in, wo_in, small_in = sem("wv_in"), sem("wo_in"), sem("small_in")
        attn_w_in, out_stored = sem("attn_w_in"), sem("out_stored")
        gu_in, down_in = [sem(f"gu_in{e}") for e in range(E)], [sem(f"down_in{e}") for e in range(E)]
        ident_ready, consts_ready, pool_set = sem("ident_ready"), sem("consts_ready"), sem("pool_set")
        ln_stat, ln_aggr, ln_var, ln_rstd, ln_out = sem("ln_stat"), sem("ln_aggr"), sem("ln_var"), sem("ln_rstd"), sem("ln_out")
        prep_pe, prep_act, prep_dve = sem("prep_pe"), sem("prep_act"), sem("prep_dve")
        ctx_rounded, ctx_split = sem("ctx_rounded"), sem("ctx_split")
        mask_ready, acc_clear = sem("mask_ready"), sem("acc_clear")
        q_hi_ready, q_split_ready = sem("q_hi_ready"), sem("q_split_ready")
        scores_ready, scores_drained, nb_ready, exps = sem("scores_ready"), sem("scores_drained"), sem("nb_ready"), sem("exps")
        pT_ready, hi_ready, lo_ready = sem("pT_ready"), sem("hi_ready"), sem("lo_ready")
        u_ready, u_copied, proj_ready, proj_added = sem("u_ready"), sem("u_copied"), sem("proj_ready"), sem("proj_added")
        wprime_pe, wprime_ready = sem("wprime_pe"), sem("wprime_ready")
        sums_ready, inv_ready = sem("sums_ready"), sem("inv_ready")

        prep = [("wkT", 0), ("wkT", 1), ("hT", 0), ("ctx", 0), ("ctx", 1), ("ctx", 2), ("ctx", 3),
                ("q", 0), ("q", 1), ("qp", 0), ("q", 2), ("qp", 1), ("q", 3), ("qp", 2), ("q", 4), ("qp", 3),
                ("q", 5), ("ctx", 4), ("qp", 4), ("q", 6), ("ctx", 5), ("qp", 5), ("q", 7), ("ctx", 6), ("qp", 6),
                ("ctx", 7), ("qp", 7), ("wvT", 0), ("wvT", 1), ("small", 0)]
        on_act = {"q", "wvT"}

        def engines_of(task):
            kind, n = task
            if kind == "ctx":
                return ("act", "dve")
            return ("act",) if kind in on_act else ("dve",)

        def evacuated(task):
            e = engines_of(task)[-1]
            upto = prep[:prep.index(task) + 1]
            return (prep_act if e == "act" else prep_dve), sum(e in engines_of(t) for t in upto)

        n_act = sum("act" in engines_of(t) for t in prep)
        n_dve = sum("dve" in engines_of(t) for t in prep)

        def pair_loop(eng, body):
            body(0, 0)
            body(1, 1)
            with eng.Fori(1, G // 2) as two:
                body(two * 2, 2)
                body(two * 2 + 1, 3)
            for m in range(G, PAIRS + 2):
                body(m, m)

        def wait_above(eng, s, value, at_value):
            if at_value > 0:
                eng.wait_ge(s, value)

        def live(p):
            return 0 <= p < PAIRS

        def norm_count(n, b):
            return b if n == 0 else B + 2 * b + n - 1

        def norm_stats(dve, n, b, src):
            k = norm_count(n, b)
            dve.bn_stats(ln_st[:, n, b, :], src).then_inc(ln_stat, 1)
            dve.wait_ge(ln_stat, k + 1)
            dve.bn_aggr(ln_mv[:, n, b, :], ln_st[:, n, b, :]).then_inc(ln_aggr, 1)
            dve.wait_ge(ln_aggr, k + 1)
            dve.tensor_scalar(ln_ve[:, n, b:b + 1], ln_mv[:, n, b, 1:2], LN_EPS, None, ALU.add).then_inc(ln_var, 1)

        def norm_root(pool, n, b):
            k = norm_count(n, b)
            pool.wait_ge(ln_var, k + 1)
            pool.tensor_tensor(ln_rs[:, n, b:b + 1], ln_ve[:, n, b:b + 1], minus_half[:, 0:1], ALU.pow).then_inc(ln_rstd, 1)

        def norm_apply(dve, n, b, src, dst):
            k = norm_count(n, b)
            dve.wait_ge(ln_rstd, k + 1)
            dve.tensor_scalar(dst, src, ln_mv[:, n, b, 0:1], ln_rs[:, n, b:b + 1], ALU.subtract, ALU.mult).then_inc(ln_out, 1)

        s_ = {name: sem(name) for name in (
            "qk_copied", "rotated", "even_ready", "root_y", "norm_gain", "qkz_clear", "qk_final", "qk_pe",
            "squares", "v_pe", "v_ready", "self_nb", "self_exp", "self_pT", "self_y", "pT_copied",
            "yT_ready", "gap", "gap_exp", "gu_pe", "up_clip", "gate_min", "glu", "tanh_ready", "res_added",
            "root_u", "att_sum", "x1_ready", "norm_a", "norm_sums", "self_scores", "self_max", "att_inv",
            "x1_half", "self_inv",
            "norm_pool", "norm_dve", "self_proj", "x2_ready", "router_ready", "lg", "top", "cmp", "before", "above",
            "ranked", "gap_one", "second", "gap_inv", "both", "gates_ready", "gatesT", "gatesT_copied",
            "bias_ready", "res_init", "gate_raw", "act_ready", "up_raw", "down_ready", "hT1_pe",
            "hT1_ready", "qkTa_ready", "qkTb_ready", "hT2_pe", "hT2_ready", "qkTa_pe", "qkTb_pe",)}.__getitem__

        A_BANK, B_BANK = 2, 3

        S_BANK = [(2, 3, 2, 3), (2, 4, 5, 2)]
        T_BANK = [(2, 2, 2, 2), (4, 5, 2, 4)]

        def before_in(bank_, *lists):
            return [max([g + 1 for g, k in enumerate(banks) if k == bank_], default=0) for banks in lists]

        def run_steps(eng, step, steps):
            for name, n in steps:
                step(eng, name, n)

        SELF_0 = [
            ("x1", "dve", 0), ("x1b", "dve", 1), ("stats1", "dve", 2), ("h1", "dve", 4), ("hT1", "pe", 5), ("hT1", "act", 6),
            ("qk", "pe", 7), ("qk", "act", 9), ("v", "pe", 8), ("v", "act", 10), ("qk", "dve", 10), ("inv0", "dve", 11),
            ("inv1", "dve", 12), ("inv2", "dve", 13), ("qkTa", "pe", 16), ("qkTa", "act", 17), ("qkTb", "pe", 17),
            ("qkTb", "act", 18), ("S0", "pe", 19), ("S0", "dve", 20), ("S1", "pe", 20), ("S1", "dve", 21), ("S2", "pe", 21),
            ("S0", "act", 22), ("N0", "dve", 23), ("S3", "pe", 23), ("S2", "dve", 24), ("S3", "dve", 25), ("S1", "act", 25),
            ("N1", "dve", 26), ("T0", "pe", 26), ("T0", "act", 26), ("Y0", "pe", 27), ("S2", "act", 28), ("T1", "pe", 29),
            ("T1", "act", 29), ("N2", "dve", 29), ("Y1", "pe", 30), ("S3", "act", 30), ("N3", "dve", 31), ("T2", "pe", 32),
            ("T2", "act", 33), ("Y2", "pe", 34), ("T3", "pe", 34), ("T3", "act", 34), ("Y3", "pe", 35), ("yT", "act", 36),
            ("proj", "pe", 37), ("proj", "dve", 40), ("stats2", "dve", 41), ("h2", "dve", 43), ("hT2", "pe", 44),
            ("hT2", "act", 46), ("router", "pe", 47), ("router", "dve", 49), ("rank", "act", 50), ("rank", "dve", 51),
            ("weigh", "dve", 53), ("gT", "pe", 54), ("gT", "dve", 56)]
        EXPERTS_0 = [
            (("gu", 0), "pe", 53), (("raw", 0), "act", 54), (("clip", 0), "dve", 55), (("tanh", 0), "act", 56),
            (("gu", 1), "pe", 56), (("glu", 0), "dve", 57), (("raw", 1), "act", 57), (("clip", 1), "dve", 58),
            (("bias", 0), "pe", 61), (("att_inv", 1), "dve", 60), (("x1", 1), "dve", 61), (("x1b", 1), "dve", 61)]

        def beside(eng, m, i):
            return [(name, 0) if isinstance(name, str) else name
                    for name, e, slot in SELF_0 + EXPERTS_0 if e == eng and m == G + 2 + slot // 8 and i == slot % 8] \
                if isinstance(m, int) else []

        def run_tail(eng, step, names):
            run_steps(eng, step, [(name, 1) if isinstance(name, str) else name for name in names])

        def experts(first, last, *parts):
            return [(name, n - late) for n in range(first, last) for name, late in parts if n - late < B * E]

        def rotate(eng, name, b):
            if name == "rope":
                eng.wait_ge(s_("qk_copied"), b + 1)
                eng.wait_ge(small_in, 16 * 6)
                ev = qk_c[b][:, :].rearrange("p (n two d) -> p n two d", two=2, d=SD)[:, :, 0, :]
                HD = SD // 2
                eng.tensor_tensor(rot_a[b][:, :, :], ev, rope_s[:, 0:1, :].broadcast_to([P, SH, SD]), ALU.mult)
                eng.tensor_tensor(rot_b[b][:, :, 0:HD], ev[:, :, HD:SD], rope_s[:, 1:2, 0:HD].broadcast_to([P, SH, HD]), ALU.mult)
                eng.tensor_tensor(rot_b[b][:, :, HD:SD], ev[:, :, 0:HD], rope_s[:, 1:2, HD:SD].broadcast_to([P, SH, HD]), ALU.mult)\
                    .then_inc(s_("rotated"), 1)
                eng.wait_ge(s_("rotated"), b + 1)
                eng.tensor_tensor(even[b][:, :, :], rot_a[b][:, :, :], rot_b[b][:, :, :], ALU.add).then_inc(s_("even_ready"), 1)
            elif name == "unit":
                eng.wait_ge(s_("root_y"), 4 * (b + 1))
                eng.tensor_tensor(norm_s[b][:, 3, 0:SH], norm_s[b][:, 2, 0:SH], gain_b[:, :], ALU.mult)
                eng.tensor_copy(norm_s[b][:, 3, SH:2 * SH], norm_s[b][:, 2, SH:2 * SH]).then_inc(s_("norm_gain"), 1)
                eng.wait_ge(s_("norm_gain"), b + 1)
                eng.wait_ge(s_("qkz_clear"), b + 1)
                eng.wait_ge(s_("even_ready"), b + 1)
                rg_v = norm_s[b][:, 3, :].rearrange("p (w n two) -> p w n two", w=2, two=2)
                odd = qk_c[b][:, :].rearrange("p (w n two d) -> p w n two d", w=2, two=2, d=SD)
                for w in range(2):
                    for parity, src in ((0, even[b][:, w * (SH // 2):(w + 1) * (SH // 2), :]), (1, odd[:, w, :, 1, :])):
                        dst = qkz[b][:, 2 * w if parity == 0 else 1 + w, :].rearrange("p (n two d) -> p n two d", two=2, d=SD)
                        last = eng.tensor_tensor(dst[:, :, parity, :], src,
                                                 rg_v[:, w, :, parity:parity + 1].broadcast_to([P, SH // 2, SD]), ALU.mult)
                last.then_inc(s_("qk_final"), 1)

        def over_sum(eng, g, b):
            eng.wait_ge(s_("self_inv"), 4 * b + g + 1)
            for n in range(4 * g, 4 * g + 4):
                last = eng.tensor_scalar(sm1[b][:, n, :], sm1[b][:, n, :], stat_s[:, b, 3, n:n + 1], None, ALU.mult)
            last.then_inc(s_("norm_dve") if b else s_("norm_pool"), 1)

        def pool_step(pool, name, b):
            if name == "x1":
                pool.wait_ge(proj_added, G * (b + 1))
                pool.memset(vz[b][:, :, :], 0.0)
                pool.memset(qkz[b][:, :, :], 0.0).then_inc(s_("qkz_clear"), 1)
                norm_root(pool, 1, b)
            elif name == "proj":
                norm_root(pool, 2, b)
            elif name in ("unit", "rope"):
                rotate(pool, name, b)
            elif name[0] == "N":
                over_sum(pool, int(name[1]), b)

        def act_step(act, name, b):
            def copy_out(wait_for, dst, src, done):
                act.wait_ge(s_(wait_for), b + 1)
                act.activation(dst, src, ACT.Copy).then_inc(s_(done), 1)

            if name == "hT1":
                copy_out("hT1_pe", hT1[b][:, :], bank(A_BANK, DC * P), "hT1_ready")
            elif name == "qk":
                act.wait_ge(s_("qk_pe"), b + 1)
                act.activation(qk_c[b][:, :], bank(B_BANK), ACT.Copy).then_inc(s_("qk_copied"), 1)
                act.activation(sq[b][:, :], bank(B_BANK), ACT.Square).then_inc(s_("squares"), 1)
            elif name == "v":
                act.wait_ge(s_("v_pe"), b + 1)
                act.wait_ge(s_("qkz_clear"), b + 1)
                v_v = bank(A_BANK, D).rearrange("p (n two d) -> p n two d", two=2, d=SD)
                for odd in range(2):
                    dst = vz[b][:, odd, :].rearrange("p (n two d) -> p n two d", two=2, d=SD)
                    last = act.activation(dst[:, :, odd, :], v_v[:, :, odd, :], ACT.Copy)
                last.then_inc(s_("v_ready"), 1)
            elif name == "qkTa":
                copy_out("qkTa_pe", qkT[b][:, 0:4, :], bank(A_BANK), "qkTa_ready")
            elif name == "qkTb":
                copy_out("qkTb_pe", qkT[b][:, 4:6, :], bank(B_BANK, 2 * P), "qkTb_ready")
            elif name[0] == "S":
                g = int(name[1])
                act.wait_ge(s_("self_nb"), 4 * b + g + 1)
                for n in range(4 * g, 4 * g + 4):
                    last = act.activation(sm1[b][:, n, :], sm1[b][:, n, :], ACT.Exp, bias=stat_s[:, b, 1, n:n + 1],
                                          accum_out=stat_s[:, b, 2, n:n + 1])
                last.then_inc(s_("self_exp"), 1)
            elif name[0] == "T":
                g = int(name[1])
                act.wait_ge(s_("self_pT"), 4 * b + g + 1)
                if g >= 2:
                    act.wait_ge(s_("self_y"), 4 * b + g - 1)
                act.activation(p1T[b][:, g % 2, :, :], bank(T_BANK[b][g]), ACT.Copy).then_inc(s_("pT_copied"), 1)
            elif name == "yT":
                act.wait_ge(s_("self_y"), 4 * b + 4)
                act.activation(yT[b][:, :], bank(B_BANK, DC * P), ACT.Copy).then_inc(s_("yT_ready"), 1)
            elif name == "hT2":
                copy_out("hT2_pe", hT2[b][:, :, :], bank(A_BANK, DC * P), "hT2_ready")
            elif name == "rank":
                act.wait_ge(s_("gap"), b + 1)
                act.activation(gap[b][:, 1:2], gap[b][:, 0:1], ACT.Exp).then_inc(s_("gap_exp"), 1)
            elif name == "raw":
                n = b
                k, e = n % 2, n % E
                act.wait_ge(s_("gu_pe"), n + 1)
                if n >= 2:
                    act.wait_ge(s_("up_clip"), n - 1)
                for j, dst, done in ((0, gate_r, "gate_raw"), (1, up_r, "up_raw")):
                    for ic in range(IC):
                        last = act.activation(dst[:, k, ic * T:(ic + 1) * T], bank(k)[:, (j * IC + ic) * T:(j * IC + ic + 1) * T],
                                              ACT.Identity, bias=gu_biasT[:, ic, j, e:e + 1])
                    last.then_inc(s_(done), 1)
            elif name == "tanh":
                n = b
                act.wait_ge(s_("gate_min"), n + 1)
                if n >= 2:
                    act.wait_ge(s_("glu"), n - 1)
                act.activation(tanh_s[:, n % 2, :], gate_s[:, n % 2, :], ACT.Tanh, scale=ALPHA / 2).then_inc(s_("tanh_ready"), 1)
            elif name == "store":
                store(act, 0)

        def store(act, b=B - 1):
            act.wait_ge(s_("res_added"), E * (b + 1))
            act.dma_start(out[b], res[b][:, :]).then_inc(out_stored, 16)
            if b == B - 1:
                act.wait_ge(out_stored, 16 * B)

        def newton(dve, b, k):
            y, s, u = norm_s[b][:, 2, :], norm_s[b][:, 1, :], norm_s[b][:, 0, :]
            dve.wait_ge(s_("root_y"), 4 * b + k + 1)
            dve.scalar_tensor_tensor(out=u, in0=y, scalar=-0.5, in1=y, op0=ALU.mult, op1=ALU.mult).then_inc(s_("root_u"), 1)
            dve.wait_ge(s_("root_u"), 6 * b + 2 * k + 1)
            dve.tensor_tensor(u, u, s, ALU.mult).then_inc(s_("root_u"), 1)
            dve.wait_ge(s_("root_u"), 6 * b + 2 * k + 2)
            dve.scalar_tensor_tensor(out=y, in0=u, scalar=1.5, in1=y, op0=ALU.add, op1=ALU.mult).then_inc(s_("root_y"), 1)

        def dve_step(dve, name, b):
            if name == "att_inv":
                dve.wait_ge(inv_ready, PAIRS)
                dve.tensor_scalar(att_inv[:, :], head_inv[:, (PAIRS - 1) % 2, :], attend[:, b:b + 1], None, ALU.mult)\
                    .then_inc(s_("att_inv"), 1)
            elif name == "x1":
                dve.wait_ge(proj_added, G if b == 0 else PAIRS - 1)
                dve.wait_ge(u_ready, G * (b + 1))
                dve.tensor_tensor(y1[b][:, :], att_acc[:, b, 0, :], att_acc[:, b, 1, :], ALU.add).then_inc(s_("att_sum"), 1)
            elif name == "x1b":
                dve.wait_ge(s_("att_sum"), b + 1)
                dve.scalar_tensor_tensor(out=x1[b][:, :], in0=y1[b][:, :], scalar=attend[:, b:b + 1], in1=xt[:, b, :],
                                         op0=ALU.mult, op1=ALU.add).then_inc(s_("x1_ready"), 1)
            elif name == "stats1":
                dve.wait_ge(s_("x1_ready"), b + 1)
                if b == B - 1:
                    dve.wait_ge(proj_added, PAIRS)
                norm_stats(dve, 1, b, x1[b][:, :])
            elif name == "h1":
                norm_apply(dve, 1, b, x1[b][:, :], h1[b][:, :])
            elif name == "qk":
                dve.wait_ge(s_("squares"), b + 1)
                dve.tensor_reduce(norm_s[b][:, 0, :], sq[b][:, :].rearrange("p (h d) -> p h d", d=SD), AX.X, ALU.add).then_inc(s_("norm_a"), 1)
                dve.wait_ge(s_("norm_a"), b + 1)
                dve.tensor_scalar(norm_s[b][:, 1, :], norm_s[b][:, 0, :], UNIT_EPS, None, ALU.add).then_inc(s_("norm_sums"), 1)
                dve.wait_ge(s_("norm_sums"), b + 1)
                dve.tensor_scalar(norm_s[b][:, 2, :].bitcast(i32), norm_s[b][:, 1, :].bitcast(i32), -0.5, ROOT_BITS,
                                  ALU.mult, ALU.add).then_inc(s_("root_y"), 1)
            elif name in ("inv0", "inv1", "inv2"):
                newton(dve, b, int(name[3]))
            elif name in ("unit", "rope"):
                rotate(dve, name, b)
            elif name[0] == "S":
                g = int(name[1])
                dve.wait_ge(consts_ready, 2)
                dve.wait_ge(s_("self_scores"), 4 * b + g + 1)
                for r in range(4):
                    n = 4 * g + r
                    last = dve.tensor_tensor_reduce(sm1[b][:, n, :], bank(S_BANK[b][g])[:, r * P:(r + 1) * P], causal[:, :],
                                                    1.0, CAUSAL, ALU.add, ALU.max, stat_s[:, b, 0, n:n + 1])
                last.then_inc(s_("self_max"), 1)
                dve.wait_ge(s_("self_max"), 4 * b + g + 1)
                dve.tensor_scalar(stat_s[:, b, 1, 4 * g:4 * g + 4], stat_s[:, b, 0, 4 * g:4 * g + 4], -1.0, None, ALU.mult)\
                    .then_inc(s_("self_nb"), 1)
            elif name[0] == "N":
                g = int(name[1])
                dve.wait_ge(s_("self_exp"), 4 * b + g + 1)
                dve.reciprocal(stat_s[:, b, 3, 4 * g:4 * g + 4], stat_s[:, b, 2, 4 * g:4 * g + 4]).then_inc(s_("self_inv"), 1)
                if b > 0:
                    over_sum(dve, g, b)
            elif name == "proj":
                dve.wait_ge(s_("self_proj"), b + 1)
                dve.tensor_tensor(x2[b][:, :], x1[b][:, :], bank(B_BANK, D), ALU.add).then_inc(s_("x2_ready"), 1)
            elif name == "stats2":
                dve.wait_ge(s_("x2_ready"), b + 1)
                norm_stats(dve, 2, b, x2[b][:, :])
            elif name == "h2":
                norm_apply(dve, 2, b, x2[b][:, :], h1[b][:, :])
            elif name == "router":
                dve.wait_ge(s_("router_ready"), b + 1)
                dve.tensor_tensor(lg[b][:, :], bank(B_BANK, E), router_bb[:, :], ALU.add).then_inc(s_("lg"), 1)
                dve.wait_ge(s_("lg"), b + 1)
                dve.max(top[b][:, :], lg[b][:, :]).then_inc(s_("top"), 1)
                l_e = lg[b][:, :].unsqueeze(2).broadcast_to([P, E, E])
                l_j = lg[b][:, :].unsqueeze(1).broadcast_to([P, E, E])
                dve.tensor_tensor(cmp_a[b][:, :, :], l_j, l_e, ALU.is_gt)
                dve.tensor_tensor(cmp_b[b][:, :, :], l_j, l_e, ALU.is_equal).then_inc(s_("cmp"), 1)
                dve.wait_ge(s_("top"), b + 1)
                dve.tensor_tensor(gap[b][:, 0:1], top[b][:, 1:2], top[b][:, 0:1], ALU.subtract).then_inc(s_("gap"), 1)
            elif name == "rank":
                dve.wait_ge(s_("cmp"), b + 1)
                dve.tensor_tensor(cmp_b[b][:, :, :], cmp_b[b][:, :, :], lower[:, :, :], ALU.mult).then_inc(s_("before"), 1)
                dve.wait_ge(s_("before"), b + 1)
                dve.tensor_tensor(cmp_a[b][:, :, :], cmp_a[b][:, :, :], cmp_b[b][:, :, :], ALU.add).then_inc(s_("above"), 1)
                dve.wait_ge(s_("above"), b + 1)
                dve.tensor_reduce(rank[b][:, :], cmp_a[b][:, :, :], AX.X, ALU.add).then_inc(s_("ranked"), 1)
            elif name == "weigh":
                dve.wait_ge(s_("gap_exp"), b + 1)
                dve.tensor_scalar(gap[b][:, 2:3], gap[b][:, 1:2], 1.0, None, ALU.add).then_inc(s_("gap_one"), 1)
                dve.wait_ge(s_("ranked"), b + 1)
                dve.tensor_scalar(pick[b][:, 0, :], rank[b][:, :], 1.0, gap[b][:, 1:2], ALU.is_equal, ALU.mult).then_inc(s_("second"), 1)
                dve.wait_ge(s_("gap_one"), b + 1)
                dve.reciprocal(gap[b][:, 3:4], gap[b][:, 2:3]).then_inc(s_("gap_inv"), 1)
                dve.wait_ge(s_("second"), b + 1)
                dve.scalar_tensor_tensor(out=pick[b][:, 1, :], in0=rank[b][:, :], scalar=0.0, in1=pick[b][:, 0, :],
                                         op0=ALU.is_equal, op1=ALU.add).then_inc(s_("both"), 1)
                dve.wait_ge(s_("gap_inv"), b + 1)
                dve.wait_ge(s_("both"), b + 1)
                dve.tensor_scalar(gates[b][:, 0, :], pick[b][:, 1, :], gap[b][:, 3:4], None, ALU.mult)
                dve.tensor_scalar(gates[b][:, 1, :], pick[b][:, 1, :], gap[b][:, 3:4], 0.5, ALU.mult, ALU.mult).then_inc(s_("gates_ready"), 1)
            elif name == "gT":
                dve.wait_ge(s_("gatesT"), b + 1)
                dve.tensor_copy(gatesT[b][0:E, :], ps[0:E, 512 * A_BANK:512 * A_BANK + P]).then_inc(s_("gatesT_copied"), 1)
            elif name == "bias":
                dve.wait_ge(s_("bias_ready"), b + 1)
                dve.tensor_tensor(res[b][:, :], bank(B_BANK, D), x2[b][:, :], ALU.add).then_inc(s_("res_init"), 1)
            elif name == "clip":
                n = b
                k = n % 2
                dve.wait_ge(s_("gate_raw"), n + 1)
                if n >= 2:
                    dve.wait_ge(s_("act_ready"), n - 1)
                dve.tensor_scalar(gate_s[:, k, :], gate_r[:, k, :], LIMIT, None, ALU.min).then_inc(s_("gate_min"), 1)
                dve.wait_ge(s_("up_raw"), n + 1)
                dve.tensor_scalar(up_c[:, k, :], up_r[:, k, :], LIMIT, -LIMIT, ALU.min, ALU.max).then_inc(s_("up_clip"), 1)
            elif name == "glu":
                n = b
                k = n % 2
                dve.wait_ge(s_("tanh_ready"), n + 1)
                dve.scalar_tensor_tensor(out=glu_s[:, k, :], in0=tanh_s[:, k, :], scalar=1.0, in1=gate_s[:, k, :],
                                         op0=ALU.add, op1=ALU.mult).then_inc(s_("glu"), 1)
                dve.wait_ge(s_("glu"), n + 1)
                dve.wait_ge(s_("up_clip"), n + 1)
                if n >= 2:
                    dve.wait_ge(s_("down_ready"), n - 1)
                dve.scalar_tensor_tensor(out=act_s[:, k, :], in0=up_c[:, k, :], scalar=1.0, in1=glu_s[:, k, :],
                                         op0=ALU.add, op1=ALU.mult).then_inc(s_("act_ready"), 1)
            elif name == "add":
                n = b
                row, e = n // E, n % E
                dve.wait_ge(s_("down_ready"), n + 1)
                if e == 0:
                    dve.wait_ge(s_("res_init"), row + 1)
                else:
                    dve.wait_ge(s_("res_added"), n)
                dve.scalar_tensor_tensor(out=res[row][:, :], in0=bank(6 + n % 2, D), scalar=gates[row][:, 1, e:e + 1],
                                         in1=res[row][:, :], op0=ALU.mult, op1=ALU.add).then_inc(s_("res_added"), 1)

        def pe_step(pe, name, b):
            if name == "hT1":
                pe.wait_ge(ln_out, norm_count(1, b) + 1)
                if b > 0:
                    pe.wait_ge(s_("gatesT_copied"), b)
                for c in range(DC):
                    mm = pe.transpose(bank(A_BANK)[:, c * P:(c + 1) * P], h1[b][:, c * P:(c + 1) * P], ident[:, :])
                mm.then_inc(s_("hT1_pe"), 1)
            elif name == "qk":
                if b == 0:
                    pe.wait_ge(attn_w_in, 32)
                else:
                    pe.wait_ge(s_("res_init"), b)
                pe.wait_ge(s_("hT1_ready"), b + 1)
                for c in range(DC):
                    mm = pe.matmul(bank(B_BANK), hT1[b][:, c * P:(c + 1) * P], w_qkv_s[:, c, 0:2 * D], start=(c == 0), stop=(c == DC - 1))
                mm.then_inc(s_("qk_pe"), 1)
            elif name == "v":
                for c in range(DC):
                    mm = pe.matmul(bank(A_BANK, D), hT1[b][:, c * P:(c + 1) * P], w_qkv_s[:, c, 2 * D:3 * D], start=(c == 0), stop=(c == DC - 1))
                mm.then_inc(s_("v_pe"), 1)
            elif name in ("qkTa", "qkTb"):
                pe.wait_ge(s_("qk_final"), b + 1)
                if name == "qkTa":
                    pe.wait_ge(s_("v_ready"), b + 1)
                for n in range(4) if name == "qkTa" else range(4, 6):
                    dst = bank(A_BANK if n < 4 else B_BANK)[:, n % 4 * P:(n % 4 + 1) * P]
                    mm = pe.transpose(dst, qkz[b][:, n // DC, n % DC * P:(n % DC + 1) * P], ident[:, :])
                mm.then_inc(s_(name + "_pe"), 1)
            elif name[0] == "S":
                g = int(name[1])
                rows = slice(32 * g, 32 * g + 32)
                if g == 0:
                    pe.wait_ge(s_("qkTa_ready"), b + 1)
                    pe.wait_ge(s_("qkTb_ready"), b + 1)
                before, = before_in(S_BANK[b][g], S_BANK[b][:g])
                if before:
                    pe.wait_ge(s_("self_max"), 4 * b + before)
                for r in range(4):
                    c, odd = r // 2, r % 2
                    mm = pe.matmul(bank(S_BANK[b][g])[:, r * P:(r + 1) * P], qkT[b][rows, odd * DC + c, :], qkT[b][rows, 2 * DC + c, :],
                                   start=True, stop=True)
                mm.then_inc(s_("self_scores"), 1)
            elif name[0] == "T":
                g = int(name[1])
                pe.wait_ge(s_("norm_dve") if b else s_("norm_pool"), g + 1)
                scores_before, before = before_in(T_BANK[b][g], S_BANK[b], T_BANK[b][:g])
                if before:
                    pe.wait_ge(s_("pT_copied"), 4 * b + before)
                else:
                    pe.wait_ge(s_("self_max"), 4 * b + scores_before)
                for r in range(4):
                    mm = pe.transpose(bank(T_BANK[b][g])[:, r * P:(r + 1) * P], sm1[b][:, 4 * g + r, :], ident[:, :])
                mm.then_inc(s_("self_pT"), 1)
            elif name[0] == "Y":
                g = int(name[1])
                rows = slice(32 * g, 32 * g + 32)
                pe.wait_ge(s_("pT_copied"), 4 * b + g + 1)
                if g == 0 and b == 0:
                    pe.wait_ge(s_("self_max"), 4)
                for r in range(4):
                    c, odd = r // 2, r % 2
                    mm = pe.matmul(ps[rows, 512 * B_BANK + c * P:512 * B_BANK + (c + 1) * P],
                                   vz[b][:, odd, c * P + 32 * g:c * P + 32 * g + 32], p1T[b][:, g % 2, r, :],
                                   start=(odd == 0), stop=(odd == 1))
                mm.then_inc(s_("self_y"), 1)
            elif name == "proj":
                pe.wait_ge(s_("yT_ready"), b + 1)
                for c in range(DC):
                    mm = pe.matmul(bank(B_BANK, D), yT[b][:, c * P:(c + 1) * P], w_out_s[:, c, :], start=(c == 0), stop=(c == DC - 1))
                mm.then_inc(s_("self_proj"), 1)
            elif name == "hT2":
                pe.wait_ge(ln_out, norm_count(2, b) + 1)
                for c in range(DC):
                    mm = pe.transpose(bank(A_BANK)[:, c * P:(c + 1) * P], h1[b][:, c * P:(c + 1) * P], ident[:, :])
                mm.then_inc(s_("hT2_pe"), 1)
            elif name == "router":
                pe.wait_ge(s_("hT2_ready"), b + 1)
                for c in range(DC):
                    mm = pe.matmul(bank(B_BANK, E), hT2[b][:, c, :], router_wT[:, c, :], start=(c == 0), stop=(c == DC - 1))
                mm.then_inc(s_("router_ready"), 1)
            elif name == "gT":
                pe.wait_ge(s_("gates_ready"), b + 1)
                pe.transpose(ps[0:E, 512 * A_BANK:512 * A_BANK + P], gates[b][:, 0, :], ident[:, :]).then_inc(s_("gatesT"), 1)
            elif name == "bias":
                pe.wait_ge(s_("gatesT_copied"), b + 1)
                pe.matmul(bank(B_BANK, D), gatesT[b][0:E, :], down_b[:, :], start=True, stop=True).then_inc(s_("bias_ready"), 1)
            elif name == "gu":
                n = b
                row, e = n // E, n % E
                if row == 0:
                    pe.wait_ge(gu_in[e], 16)
                if e == 0:
                    pe.wait_ge(s_("hT2_ready"), row + 1)
                if n == 0:
                    pe.wait_ge(scores_drained, 8 * PAIRS)
                if n >= 2:
                    pe.wait_ge(s_("up_raw"), n - 1)
                w = gu_a[:, e] if e < EA else gu_b[:, e - EA]
                for j in range(2):
                    for ic in range(IC):
                        for c in range(DC):
                            lhs = w[:, c, ic * 2 * P:(ic + 1) * 2 * P].rearrange("p (i two) -> p two i", two=2)[:, j, :]
                            mm = pe.matmul(bank(n % 2)[:, (j * IC + ic) * T:(j * IC + ic + 1) * T], lhs, hT2[row][:, c, :],
                                           start=(c == 0), stop=(c == DC - 1))
                mm.then_inc(s_("gu_pe"), 1)
            elif name == "down":
                n = b
                row, e = n // E, n % E
                if row == 0:
                    pe.wait_ge(down_in[e], 16)
                pe.wait_ge(s_("act_ready"), n + 1)
                if n < 2:
                    pe.wait_ge(proj_added, PAIRS - 1 + n)
                if n >= 2:
                    pe.wait_ge(s_("res_added"), n - 1)
                w = down_a[:, e] if e < DA else down_b_[:, e - DA]
                for ic in range(IC):
                    mm = pe.matmul(bank(6 + n % 2, D), act_s[:, n % 2, ic * T:(ic + 1) * T], w[:, ic, :],
                                   start=(ic == 0), stop=(ic == IC - 1))
                mm.then_inc(s_("down_ready"), 1)

        block = es.enter_context(nc.Block())

        @block.sync
        def _(sp):
            sp.dma_start(xt[:, :, :], x.rearrange("b t d -> t b d")).then_inc(x_in, 16)
            half = G * P // 2
            sp.dma_start(wk_s[:, 0:half], Wk[:, 0:half]).then_inc(wk_in[0], 16)
            sp.dma_start(wk_s[:, half:2 * half], Wk[:, half:2 * half]).then_inc(wk_in[1], 16)
            ctx_v = ctx.rearrange("b (k p) d -> p b k d", p=P)
            for b in range(B):
                if b == 0:
                    sp.dma_start(ctx_s[:, 0:KB // 2, :], ctx_v[:, 0, 0:KB // 2]).then_inc(ctx_in[0], 16)
                    sp.dma_start(ctx_s[:, KB // 2:KB, :], ctx_v[:, 0, KB // 2:KB]).then_inc(ctx_in[1], 16)
                    for i in range(4):
                        w = H * P // 4
                        sp.dma_start(wq_s[:, :, i * w:(i + 1) * w],
                                     Wq.rearrange("(c p) n -> p c n", p=P)[:, :, i * w:(i + 1) * w]).then_inc(wq_in[i], 16)
                else:
                    sp.dma_start(ctx_s[:, KB:2 * KB, :], ctx_v[:, 1]).then_inc(ctx_in[2], 16)
            sp.dma_start(wv_s[:, :], Wv).then_inc(wv_in, 16)
            sp.dma_start(wo_s[:, :, :], Wo.rearrange("(h p) n -> p h n", p=P)).then_inc(wo_in, 16)
            sp.dma_start(w_out_s[:, :, :], w_out.rearrange("(c p) n -> p c n", p=P)).then_inc(attn_w_in, 16)
            sp.wait_ge(prep_act, n_act)
            sp.wait_ge(prep_dve, n_dve)
            sp.wait_ge(mask_ready, 1)
            gu_v = gate_up.rearrange("e (c p) n -> p e c n", p=P)
            down_v = down.rearrange("e (c p) n -> p e c n", p=P)
            for e in range(EA):
                sp.dma_start(gu_a[:, e], gu_v[:, e]).then_inc(gu_in[e], 16)
            for e in range(DA):
                sp.dma_start(down_a[:, e], down_v[:, e]).then_inc(down_in[e], 16)
            sp.wait_ge(wprime_pe, G)
            sp.dma_start(w_qkv_s[:, :, :], w_qkv.rearrange("(c p) n -> p c n", p=P)).then_inc(attn_w_in, 16)
            sp.wait_ge(pT_ready, G * PAIRS)
            for e in range(min(EA, DA), E):
                if e >= DA:
                    sp.dma_start(down_b_[:, e - DA], down_v[:, e]).then_inc(down_in[e], 16)
                if e >= EA:
                    sp.dma_start(gu_b[:, e - EA], gu_v[:, e]).then_inc(gu_in[e], 16)

        @block.gpsimd
        def _(pool):
            pool.memset(ident[:, :], 0.0).then_inc(pool_set, 1)
            pool.memset(minus_half[:, :], -0.5).then_inc(pool_set, 1)
            pool.memset(causal[:, :], 0.0).then_inc(pool_set, 1)
            pool.memset(lower[:, :, :], 1.0).then_inc(pool_set, 1)
            pool.wait_ge(pool_set, 4)
            pool.affine_select(out=ident[:, :], in_=ident[:, :], compare_op=ALU.not_equal, fill=1.0, base=0,
                               pattern=[[-1, P]], channel_multiplier=1).then_inc(ident_ready, 1)
            for b in range(B):
                norm_root(pool, 0, b)
            pool.affine_select(out=causal[:, :], in_=causal[:, :], compare_op=ALU.is_ge, fill=CAUSAL, base=0,
                               pattern=[[-1, P]], channel_multiplier=1).then_inc(consts_ready, 1)
            pool.affine_select(out=lower[:, :, :], in_=lower[:, :, :], compare_op=ALU.is_gt, fill=0.0, base=0,
                               pattern=[[1, E], [-1, E]], channel_multiplier=0).then_inc(consts_ready, 1)

            def split_ctx(j):
                part = slice(4 * j, 4 * j + 4)
                pool.wait_ge(ctx_rounded, j + 1)
                pool.tensor_tensor(ctx_lo[:, part, :], ctx_s[:, part, :], ctx_hi[:, part, :].bitcast(f32), ALU.subtract)\
                    .then_inc(ctx_split, 1)

            def split_q(m, par, m_at):
                if m_at >= 2:
                    pool.wait_ge(scores_ready, 8 * (m - 1))
                wait_above(pool, q_split_ready, m, m_at)
                src = qp[:, bass.ds(m * (2 * P), 2 * P)]
                pool.tensor_copy(q_pair[:, :], src)
                pool.tensor_copy(qs_hi[:, par, :], src).then_inc(q_hi_ready, 1)
                pool.wait_ge(q_hi_ready, m + 1)
                pool.tensor_tensor(qs_lo[:, par, :], q_pair[:, :], qs_hi[:, par, :].bitcast(f32), ALU.subtract)\
                    .then_inc(q_split_ready, 1)

            for j in range(4):
                split_ctx(j)
            for g in range(2):
                s, v = evacuated(("qp", g))
                pool.wait_ge(s, v)
                split_q(g, g, g)
            for j in range(4, 8):
                split_ctx(j)
            s, v = evacuated(("qp", G - 1))
            pool.wait_ge(s, v)
            with pool.Fori(1, G // 2) as two:
                split_q(two * 2, 0, 2)
                split_q(two * 2 + 1, 1, 3)
            for m in range(G, PAIRS):
                split_q(m, m % 2, m)
                if m == G + 3:
                    run_steps(pool, pool_step, [("x1", 0)])
                if m == G + 4:
                    run_steps(pool, pool_step, [("rope", 0), ("unit", 0)])
                if m == G + 5:
                    run_steps(pool, pool_step, [("N0", 0)])
                if m == G + 6:
                    run_steps(pool, pool_step, [("N1", 0), ("N2", 0), ("N3", 0)])
                if m == G + 7:
                    run_steps(pool, pool_step, [("proj", 0)])
            run_tail(pool, pool_step, ("x1", "rope", "proj"))

        @block.tensor
        def _(pe):
            pe.wait_ge(ident_ready, 1)
            for k, task in enumerate(prep):
                kind, n = task
                if k >= 8:
                    s, v = evacuated(prep[k - 8])
                    pe.wait_ge(s, v)
                bk = bank(k % 8)
                if kind in ("wkT", "wvT"):
                    pe.wait_ge(wk_in[n] if kind == "wkT" else wv_in, 16)
                    src = wk_s if kind == "wkT" else wv_s
                    for i in range(4):
                        g = 4 * n + i
                        mm = pe.transpose(bk[:, i * P:(i + 1) * P], src[:, g * P:(g + 1) * P], ident[:, :])
                elif kind == "ctx":
                    if n in (0, 2, 4):
                        pe.wait_ge(ctx_in[n // 2], 16)
                    for i in range(4):
                        mm = pe.transpose(bk[:, i * P:(i + 1) * P], ctx_s[:, 4 * n + i, :], ident[:, :])
                elif kind == "hT":
                    pe.wait_ge(ln_out, B)
                    for c in range(DC):
                        for b in range(B):
                            mm = pe.transpose(bk[:, (c * B + b) * P:(c * B + b + 1) * P], h0[:, b, c * P:(c + 1) * P], ident[:, :])
                elif kind == "q":
                    if n == 0:
                        s, v = evacuated(("hT", 0))
                        pe.wait_ge(s, v)
                    if n % 2 == 0:
                        pe.wait_ge(wq_in[n // 2], 16)
                    for i in range(2):
                        for c in range(DC):
                            h = 2 * n + i
                            mm = pe.matmul(bk[:, i * B * T:(i + 1) * B * T], wq_s[:, c, h * P:(h + 1) * P], hT0[:, c, :],
                                           start=(c == 0), stop=(c == DC - 1))
                elif kind == "qp":
                    s, v = evacuated(("q", n))
                    pe.wait_ge(s, v)
                    if n == 0:
                        s, v = evacuated(("wkT", 1))
                        pe.wait_ge(s, v)
                    mm = pe.matmul(bk, wkT[:, n, :], qT[:, n % 2, :], start=True, stop=True)
                elif kind == "small":
                    pe.wait_ge(small_in, 16 * 6)
                    for ic in range(IC):
                        for j in range(2):
                            src = gu_bias[:, ic * 2 * P:(ic + 1) * 2 * P].rearrange("e (i two) -> e two i", two=2)[:, j, :]
                            pe.transpose(bk[:, (2 * ic + j) * E:(2 * ic + j + 1) * E], src, ident[0:E, 0:E])
                    for c in range(DC):
                        mm = pe.transpose(bk[:, (4 + c) * E:(5 + c) * E], router_s[:, c * P:(c + 1) * P], ident[0:E, 0:E])
                mm.then_inc(prep_pe, 1)

            def banks_free(*banks):
                for k in range(len(prep) - 8, len(prep)):
                    if k % 8 in banks:
                        s, v = evacuated(prep[k])
                        pe.wait_ge(s, v)

            def wprime_step(g):
                if g == 0:
                    pe.wait_ge(wo_in, 16)
                    s, v = evacuated(("wvT", 1))
                    pe.wait_ge(s, v)
                if g < 2:
                    banks_free(2 + g)
                else:
                    pe.wait_ge(wprime_ready, g - 1)
                for i in range(2):
                    mm = pe.matmul(bank(2 + g % 2)[:, i * D:(i + 1) * D], wvT[:, g, :], wo_s[:, 2 * g + i, :], start=True, stop=True)
                mm.then_inc(wprime_pe, 1)

            banks_free(0, 1)

            def body(m, a):
                par = a % 2
                if a == 1:
                    pe.wait_ge(prep_act, n_act)
                    pe.wait_ge(prep_dve, n_dve)
                    pe.wait_ge(ctx_split, 8)
                for i in range(8):
                    if live(a):
                        b, h = a // G, i // 4
                        if i == 0:
                            pe.wait_ge(q_split_ready, m + 1)
                        wait_above(pe, scores_drained, 8 * m + i - 1, 8 * a + i - 1)
                        dst = bank(i % 2)
                        keys = slice((i % 4) * 512, (i % 4 + 1) * 512)
                        qh, ql = qs_hi[:, par, h * P:(h + 1) * P], qs_lo[:, par, h * P:(h + 1) * P]
                        pe.matmul(dst, qh, ctxT_hi[:, b, keys], start=True, stop=False)
                        pe.matmul(dst, qh, ctxT_lo[:, b, keys], start=False, stop=False)
                        mm = pe.matmul(dst, ql, ctxT_hi[:, b, keys], start=False, stop=True)
                        mm.then_inc(scores_ready, 1)
                    if a == 0:
                        wprime_step(i)
                    if a == 1 and i == 7:
                        pe.wait_ge(wprime_ready, G)
                    d = 1 if i >= 2 else 2
                    t = (i - 2) % 8
                    if live(a - d) or live(a - (1 if i >= 4 else 2)):
                        wait_above(pe, lo_ready, 8 * m + i - 11, 8 * a + i - 11)
                    if live(a - d):
                        if t % 4 == 0:
                            pe.wait_ge(exps, 4 * (m - d) + 3 + t // 4)
                        for j in range(4):
                            kb, h = 2 * t + j // 2, j % 2
                            mm = pe.transpose(bank(4 + t % 2)[:, j * P:(j + 1) * P],
                                              probs[:, (a - d) % 2, h, kb * P:(kb + 1) * P], ident[:, :])
                        mm.then_inc(pT_ready, 1)
                    d = 1 if i >= 4 else 2
                    t = (i - 4) % 8
                    if live(a - d):
                        b = (a - d) // G
                        u_bank = bank(6 + (a - d) % 2, 2 * P)
                        for j in range(2):
                            kb = 2 * t + j
                            hi, lo = pT_hi[:, t % 4, j * 2 * P:(j + 1) * 2 * P], pT_lo[:, t % 4, j * 2 * P:(j + 1) * 2 * P]
                            ch, cl = ctx_hi[:, b * KB + kb, :], ctx_lo[:, b * KB + kb, :]
                            pe.matmul(u_bank, ch, hi, start=(kb == 0), stop=False)
                            pe.matmul(u_bank, ch, lo, start=False, stop=False)
                            mm = pe.matmul(u_bank, cl, hi, start=False, stop=(kb == KB - 1))
                        if t == 7:
                            mm.then_inc(u_ready, 1)
                    if i == 6 and live(a - 2):
                        b = (a - 2) // G
                        pe.wait_ge(u_copied, m - 1)
                        for h in range(2):
                            w = wprime_v[:, bass.ds((m - 2 - G * b) * (2 * D) + h * D, D)]
                            mm = pe.matmul(bank(6 + a % 2)[:, h * D:(h + 1) * D], u_s[:, h * P:(h + 1) * P], w, start=True, stop=True)
                        mm.then_inc(proj_ready, 1)
                    run_steps(pe, pe_step, beside('pe', m, i))

            wprime_v = wprime[:, :, :].rearrange("p h n -> p (h n)")
            pair_loop(pe, body)
            run_tail(pe, pe_step, [
                ("gu", 2), ("down", 0), "hT1", ("gu", 3), "qk", "v", ("down", 1), ("gu", 4), ("gu", 5), "qkTa",
                "qkTb", ("down", 2), "S0", "S1", "S2", "S3", ("down", 3), "T0", ("gu", 6), "T1", "Y0", "T2", "Y1", "T3", "Y2", "Y3",
                "proj", ("down", 4), ("gu", 7), "hT2", "router", ("down", 5), ("gu", 8), ("down", 6), ("gu", 9),
                ("down", 7), "gT", ("gu", 10), "bias", ("down", 8)]
                + experts(11, 14, ("gu", 0), ("down", 2)) + [("gu", 14), ("gu", 15), ("down", 12)] + experts(15, 18, ("down", 2)))

        @block.scalar
        def _(act):
            act.dma_start(mask_u8[:, :, :].rearrange("p b n -> p (b n)"), mask.rearrange("b n -> (b n)").partition_broadcast(P)).then_inc(mask_in, 16)
            act.dma_start(gu_bias[:, :], gate_up_bias).then_inc(small_in, 16)
            act.dma_start(router_s[:, :], router_w).then_inc(small_in, 16)
            act.dma_start(router_bb[:, :], router_b.partition_broadcast(P)).then_inc(small_in, 16)
            act.dma_start(gain_b[:, :], q_gain.partition_broadcast(P)).then_inc(small_in, 16)
            act.dma_start(rope_s[:, :, :], rope).then_inc(small_in, 16)
            act.dma_start(down_b[:, :], down_bias).then_inc(small_in, 16)
            for k, task in enumerate(prep):
                kind, n = task
                if "act" not in engines_of(task):
                    continue
                if kind == "ctx":
                    if n in (0, 2, 4):
                        act.wait_ge(ctx_in[n // 2], 16)
                    act.activation(ctx_hi[:, 4 * n:4 * n + 4, :], ctx_s[:, 4 * n:4 * n + 4, :], ACT.Copy).then_inc(ctx_rounded, 1)
                act.wait_ge(prep_pe, k + 1)
                bk = bank(k % 8)
                if kind == "ctx":
                    o_ = ctxT_hi[:, n // 4, (n % 4) * 512:(n % 4 + 1) * 512]
                elif kind == "q":
                    if n >= 2:
                        act.wait_ge(prep_pe, prep.index(("qp", n - 2)) + 1)
                    o_ = qT[:, n % 2, :]
                elif kind == "wvT":
                    o_ = wvT[:, 4 * n:4 * n + 4, :].rearrange("p g c -> p (g c)")
                act.activation(o_, bk, ACT.Copy).then_inc(prep_act, 1)

            def body(m, a):
                if a == 1:
                    act.wait_ge(ctx_split, 8)
                for i in range(8):
                    if a == 0:
                        act.wait_ge(wprime_pe, i + 1)
                        act.activation(wprime[:, 2 * i:2 * i + 2, :].rearrange("p g c -> p (g c)"), bank(2 + i % 2), ACT.Copy)\
                            .then_inc(wprime_ready, 1)
                    d = 1 if i >= 2 else 2
                    t = (i - 2) % 8
                    if live(a - d):
                        act.wait_ge(pT_ready, 8 * m + i - 9)
                        act.activation(pT_hi[:, t % 4, :], bank(4 + t % 2), ACT.Copy).then_inc(hi_ready, 1)
                    if i == 4 and live(a - 2):
                        act.wait_ge(u_ready, m - 1)
                        act.activation(u_s[:, :], bank(6 + a % 2, 2 * P), ACT.Copy).then_inc(u_copied, 1)
                    if i in (0, 3, 5, 7):
                        d, h, half = (0, 0, (i - 5) // 2) if i >= 5 else (1, 1, i // 3)
                        if live(a - d):
                            par, c = (a - d) % 2, 2 * h + half
                            act.wait_ge(nb_ready, 2 * (m - d) + h + 1)
                            act.activation(probs[:, par, h, half * 1024:(half + 1) * 1024],
                                           scores[:, h, half * 1024:(half + 1) * 1024], ACT.Exp,
                                           bias=neg_max[:, par, h:h + 1], scale=SCALE,
                                           accum_out=row_sum[:, par, c:c + 1]).then_inc(exps, 1)
                    run_steps(act, act_step, beside('act', m, i))

            pair_loop(act, body)
            run_tail(act, act_step, [
                ("tanh", 1), ("raw", 2), ("tanh", 2), "hT1", ("raw", 3), "qk", "v", ("raw", 4), "qkTa", "qkTb", ("tanh", 3), ("raw", 5),
                ("tanh", 4), "S0", "S1", "S2", "S3", "T0", "T1", "T2", "T3", "yT", ("tanh", 5), ("raw", 6), "hT2",
                ("tanh", 6), ("raw", 7), "rank", ("tanh", 7), ("raw", 8)]
                + experts(9, 12, ("tanh", 1), ("raw", 0)) + [("store", 0)] + experts(12, 15, ("tanh", 1), ("raw", 0))
                + [("tanh", 14), ("raw", 15), ("tanh", 15)])
            store(act)

        @block.vector
        def _(dve):
            dve.memset(att_acc[:, :, :, :], 0.0).then_inc(acc_clear, 1)
            dve.wait_ge(x_in, 16)
            for b in range(B):
                norm_stats(dve, 0, b, xt[:, b, :])
            for b in range(B):
                norm_apply(dve, 0, b, xt[:, b, :], h0[:, b, :])
            for k, task in enumerate(prep):
                kind, n = task
                if "dve" not in engines_of(task):
                    continue
                bk = bank(k % 8)
                if kind == "ctx":
                    act_n = sum("act" in engines_of(t) for t in prep[:k + 1])
                    dve.wait_ge(prep_act, act_n)
                    keys = slice((n % 4) * 512, (n % 4 + 1) * 512)
                    dve.tensor_tensor(ctxT_lo[:, n // 4, keys], bk, ctxT_hi[:, n // 4, keys].bitcast(f32),
                                      ALU.subtract).then_inc(prep_dve, 1)
                    if n == 3:
                        dve.wait_ge(mask_in, 16)
                        dve.tensor_scalar(mask_bias[:, :, :], mask_u8[:, :, :], 1.0, MASKED, ALU.subtract, ALU.mult).then_inc(mask_ready, 1)
                        dve.tensor_reduce(attend[:, :], mask_u8[:, :, :], AX.X, ALU.max).then_inc(mask_ready, 1)
                    continue
                dve.wait_ge(prep_pe, k + 1)
                if kind == "small":
                    dve.tensor_copy(gu_biasT[:, :, :, :].rearrange("p a b c -> p (a b c)"), bk[:, 0:4 * E]).then_inc(acc_clear, 1)
                    dve.tensor_copy(router_wT[:, :, :].rearrange("p a b -> p (a b)"), bk[:, 4 * E:6 * E]).then_inc(prep_dve, 1)
                    continue
                if kind == "wkT":
                    o_ = wkT[:, 4 * n:4 * n + 4, :].rearrange("p g c -> p (g c)")
                elif kind == "hT":
                    o_ = hT0[:, :, :].rearrange("p c t -> p (c t)")
                elif kind == "qp":
                    for b in range(B):
                        last = dve.tensor_copy(qp[:, (b * G + n) * 2 * P:(b * G + n + 1) * 2 * P].rearrange("p (h t) -> p h t", h=2),
                                               bk.rearrange("p (h b t) -> p h b t", h=2, b=B)[:, :, b, :])
                    last.then_inc(prep_dve, 1)
                    continue
                dve.tensor_copy(o_, bk).then_inc(prep_dve, 1)
            dve.wait_ge(mask_ready, 2)
            dve.wait_ge(acc_clear, 2)

            def add_head(m, a, h):
                b, par = (a - 2) // G, a % 2
                if h == 0:
                    dve.wait_ge(proj_ready, m - 1)
                    wait_above(dve, proj_added, m - 2, a - 2)
                    dve.wait_ge(inv_ready, m - 1)
                if a - 2 == PAIRS - 1:
                    if h == 0:
                        dve.wait_ge(s_("att_inv"), 1)
                        dve.wait_ge(s_("x1_ready"), B)
                    else:
                        dve.wait_ge(s_("x1_half"), 1)
                    dve.scalar_tensor_tensor(out=x1[b][:, :], in0=bank(6 + a % 2)[:, h * D:(h + 1) * D],
                                             scalar=att_inv[:, h:h + 1], in1=x1[b][:, :],
                                             op0=ALU.mult, op1=ALU.add).then_inc(proj_added if h else s_("x1_half"), 1)
                    return
                last = dve.scalar_tensor_tensor(out=att_acc[:, b, h, :], in0=bank(6 + a % 2)[:, h * D:(h + 1) * D],
                                                scalar=head_inv[:, par, h:h + 1], in1=att_acc[:, b, h, :],
                                                op0=ALU.mult, op1=ALU.add)
                if h == 1:
                    last.then_inc(proj_added, 1)

            def body(m, a):
                if a == 1:
                    dve.wait_ge(ctx_split, 8)
                for i in range(8):
                    d = 1 if i >= 2 else 2
                    t = (i - 2) % 8
                    if i == 7 and live(a - 2):
                        add_head(m, a, 0)
                    if live(a):
                        dve.wait_ge(scores_ready, 8 * m + i + 1)
                        wait_above(dve, exps, 4 * m + i // 2 - 3, 4 * a + i // 2 - 3)
                        wait_above(dve, scores_drained, 8 * m + i, 8 * a + i)
                    if live(a - d):
                        dve.wait_ge(hi_ready, 8 * m + i - 9)
                        dve.tensor_tensor(pT_lo[:, t % 4, :], bank(4 + t % 2), pT_hi[:, t % 4, :].bitcast(f32),
                                          ALU.subtract).then_inc(lo_ready, 1)
                    if live(a):
                        b, h, par = a // G, i // 4, a % 2
                        keys = slice((i % 4) * 512, (i % 4 + 1) * 512)
                        dve.tensor_tensor_reduce(scores[:, h, keys], bank(i % 2), mask_bias[:, b, keys], 1.0,
                                                 row_max[:, par, i - 1:i] if i % 4 else -MASKED,
                                                 ALU.add, ALU.max, row_max[:, par, i:i + 1]).then_inc(scores_drained, 1)
                        if i % 4 == 3:
                            dve.wait_ge(scores_drained, 8 * m + i + 1)
                            dve.tensor_scalar(neg_max[:, par, h:h + 1], row_max[:, par, i:i + 1], -SCALE, None,
                                              ALU.mult).then_inc(nb_ready, 1)
                    if i == 6 and live(a - 1):
                        par = (a - 1) % 2
                        dve.wait_ge(exps, 4 * m)
                        dve.tensor_reduce(head_sum[:, par, :], row_sum[:, par, :].rearrange("p (h two) -> p h two", two=2),
                                          AX.X, ALU.add).then_inc(sums_ready, 1)
                        dve.wait_ge(sums_ready, m)
                        dve.reciprocal(head_inv[:, par, :], head_sum[:, par, :]).then_inc(inv_ready, 1)
                    if i == 7 and live(a - 2):
                        add_head(m, a, 1)
                    run_steps(dve, dve_step, beside('dve', m, i))

            pair_loop(dve, body)
            run_tail(dve, dve_step, [
                "stats1", ("glu", 1), "h1", ("clip", 2), ("bias", 0), ("glu", 2), ("clip", 3), ("add", 0),
                "qk", "inv0", "inv1", "inv2", "unit", ("add", 1), ("clip", 4), ("glu", 3), "S0", "S1", "S2", "N0", "S3", "N1", "N2",
                "N3", ("glu", 4), ("clip", 5), ("add", 2), ("add", 3), "proj", "stats2", ("glu", 5), "h2", ("clip", 6),
                ("add", 4), "router", ("glu", 6), ("clip", 7), ("add", 5), "rank", "weigh", ("glu", 7), ("clip", 8),
                ("add", 6), ("glu", 8), ("clip", 9), ("add", 7), "gT", ("glu", 9), ("clip", 10), "bias", ("add", 8)]
                + experts(11, 14, ("glu", 1), ("clip", 0), ("add", 2))
                + [("glu", 13), ("clip", 14), ("clip", 15), ("glu", 14), ("add", 12), ("glu", 15)]
                + experts(15, 18, ("add", 2)))


_INS = ['x', 'ctx_1024', 'mask_BxS2_bf1', 'L0_xattn_Wq', 'L0_xattn_Wk', 'L0_xattn_Wv', 'L0_xattn_Wo', 'L0_attn_w_qkv',
        'L0_attn_w_out', 'L0_attn_q_gain', 'L0_ffn_router_weight', 'L0_ffn_router_bias', 'L0_ffn_gate_up_proj',
        'L0_ffn_gate_up_proj_bias', 'L0_ffn_down_proj', 'L0_ffn_down_proj_bias']
_OUTS = [((2, 128, 256), 'float32')]


def _rope_table(tokens=128, width=16, base=10000.0):
    import numpy as _np
    half = width // 2
    freq = _np.float32(base) ** (-_np.arange(half, dtype=_np.float32) / _np.float32(half))
    theta = _np.arange(tokens, dtype=_np.float32)[:, None] * freq[None, :]
    c, s = _np.cos(theta), _np.sin(theta)
    return _np.stack([_np.concatenate([c, c], 1), _np.concatenate([-s, s], 1)], 1).astype(_np.float32)


def kernel(**inputs):
    import numpy as _np
    import concourse.bacc as _bacc
    from concourse import mybir as _mybir
    from concourse.bass_utils import run_bass_kernel_spmd as _run

    nc = _bacc.Bacc("TRN2", target_bir_lowering=False, num_devices=1)
    arrays, args = {}, []
    for name in _INS + ['rope']:
        a = _rope_table() if name == 'rope' else _np.ascontiguousarray(inputs[name])
        if a.dtype == _np.bool_:
            a = a.view(_np.uint8)
        arrays[f"in_{name}_dram"] = a
        args.append(nc.dram_tensor(f"in_{name}_dram", a.shape, _mybir.dt.from_np(a.dtype), kind="ExternalInput").ap())
    for i, (shape, dtype) in enumerate(_OUTS):
        dt = _mybir.dt.from_np(_np.dtype(dtype))
        args.append(nc.dram_tensor(f"out_{i}_dram", shape, dt, kind="ExternalOutput").ap())
    perceiver_block(nc, *args)
    r = _run(nc, [arrays], core_ids=[0])
    got = tuple(r.results[0][f"out_{i}_dram"] for i in range(len(_OUTS)))
    return got[0]
```
